# Optimizing a Trainium2 kernel written in Bass

```python
import numpy as np
import jax
import jax.numpy as jnp

def _softmax(x, axis=-1):
    return jax.nn.softmax(x, axis=axis)

def _gelu(x):
    return jax.nn.gelu(x, approximate=True)

def _silu(x):
    return jax.nn.silu(x)

def _sigmoid(x):
    return jax.nn.sigmoid(x)

def _layernorm(x, axis=-1, eps=1e-05):
    m = jnp.mean(x, axis=axis, keepdims=True)
    v = jnp.var(x, axis=axis, keepdims=True)
    return (x - m) / jnp.sqrt(v + eps)

def _scatter_add(tgt, idx, src, axis=0):
    return tgt.at[idx].add(src)

def _segment_sum(src, seg, n):
    return jax.ops.segment_sum(src, seg, n)
kernel_name = 'mk_adaln_ffn_d2_seqx_r4_59dd1c'

def setup_inputs(seed: int=0):
    np.random.seed(seed)
    _w = jnp.asarray

    def _rec_inputs():
        import jax
        import jax.numpy as jnp
        _rk = jax.random.key(seed)
        x = -0.003407 + 1.001 * jax.random.normal(jax.random.fold_in(_rk, 1), (8, 256, 512), jnp.float32)
        _lenS = 256 - jax.random.randint(jax.random.fold_in(_rk, 7), (8,), 0, max(1, 256 // 4) + 1, jnp.int32)
        _lenS2 = 256 - jax.random.randint(jax.random.fold_in(_rk, 8), (8,), 0, max(1, 256 // 4) + 1, jnp.int32)
        itok_Bx257_0_4111 = jax.random.randint(jax.random.fold_in(_rk, 11), (8, 257), 0, 1028, jnp.int32)
        itok_B_37_3939 = jax.random.randint(jax.random.fold_in(_rk, 12), (8,), 37, 985, jnp.int32)
        itok_B_0_6 = jax.random.randint(jax.random.fold_in(_rk, 13), (8,), 0, 7, jnp.int32)
        return (x, itok_Bx257_0_4111, itok_B_37_3939, itok_B_0_6)
    x, itok_Bx257_0_4111, itok_B_37_3939, itok_B_0_6 = _rec_inputs()

    def _L0_cond_setup():
        import jax, jax.numpy as jnp
        import numpy as np
        H, G, HD = (8, 4, 64)
        GSZ = H // G
        BLOCK = 16
        WINDOW = 256
        SCALE = 256.0 ** (-0.5)
        EPS = 1e-06
        THETA = 10000.0
        B, T, D = (16, 4, 512)
        NBLK = 257

        def _rms(x, scale):
            var = jnp.mean(x * x, axis=-1, keepdims=True)
            return x * jax.lax.rsqrt(var + EPS) * (1.0 + scale)

        def _rope(x, pos):
            half = HD // 2
            inv = 1.0 / THETA ** (jnp.arange(half, dtype=jnp.float32) / half)
            ang = pos[:, :, None].astype(jnp.float32) * inv
            cos = jnp.cos(ang)[:, None, :, :]
            sin = jnp.sin(ang)[:, None, :, :]
            x1, x2 = (x[..., :half], x[..., half:])
            return jnp.concatenate([x1 * cos - x2 * sin, x2 * cos + x1 * sin], axis=-1)
        key = jax.random.key(seed)
        ks = jax.random.split(key, 10)
        inv_d = 1.0 / np.sqrt(D)
        return {'x': jax.random.normal(ks[0], (B, T, D), jnp.float32), 'Wq': jax.random.normal(ks[1], (H * HD, D), jnp.float32) * inv_d, 'Wk': jax.random.normal(ks[2], (G * HD, D), jnp.float32) * inv_d, 'Wv': jax.random.normal(ks[3], (G * HD, D), jnp.float32) * inv_d, 'Wo': jax.random.normal(ks[4], (D, H * HD), jnp.float32) * inv_d, 'q_norm_scale': jax.random.normal(ks[5], (HD,), jnp.float32) * 0.02, 'k_norm_scale': jax.random.normal(ks[6], (HD,), jnp.float32) * 0.02, 'k_blocks': jax.random.normal(ks[7], (B * NBLK, G, BLOCK, HD), jnp.float32), 'v_blocks': jax.random.normal(ks[8], (B * NBLK, G, BLOCK, HD), jnp.float32), 'block_tables': jnp.arange(B * NBLK, dtype=jnp.int32).reshape(B, NBLK), 'kv_lens': jax.random.randint(ks[9], (B,), 0, 1024, dtype=jnp.int32)}
    _L0_cond_all = _L0_cond_setup()
    _L0_cond_in = {k: v for k, v in _L0_cond_all.items() if k in ('Wq', 'Wk', 'Wv', 'Wo', 'q_norm_scale', 'k_norm_scale', 'k_blocks', 'v_blocks')}
    del _L0_cond_all

    def _L0_ffn_setup():
        import jax, jax.numpy as jnp
        import numpy as np
        TOP_K = 2
        key = jax.random.key(seed)
        ks = jax.random.split(key, 7)
        B, S, H = (2, 512, 512)
        E, A, NS = (8, 64, 4096)
        x = jax.random.normal(ks[0], (B, S, H), jnp.float32)
        gate_w = jax.random.normal(ks[1], (E, H), jnp.float32) * 0.01
        W = jax.random.normal(ks[2], (H, H), jnp.float32) * 0.02
        atoms = jax.random.normal(ks[3], (A, NS), jnp.float32) * 0.02
        expert_atom_weights = jax.random.normal(ks[4], (E, A), jnp.float32) * 0.1
        importance = jax.random.normal(ks[5], (E, NS), jnp.float32) * 0.1
        mask_idx = jax.random.randint(ks[6], (NS,), 0, H * H, jnp.int32)
        return dict(x=x, gate_w=gate_w, W=W, atoms=atoms, expert_atom_weights=expert_atom_weights, importance=importance, mask_idx=mask_idx)
    _L0_ffn_all = _L0_ffn_setup()
    _L0_ffn_in = {k: v for k, v in _L0_ffn_all.items() if k in ('gate_w', 'W', 'atoms', 'expert_atom_weights', 'importance', 'mask_idx')}
    del _L0_ffn_all

    def _L1_cond_setup():
        import jax, jax.numpy as jnp
        import numpy as np
        B, T, D_IN, D_OUT = (16, 512, 512, 512)
        N_ADAPTERS, RANK = (8, 16)
        key = jax.random.key(seed)
        k_x, k_w, k_a, k_b, k_s, k_idx = jax.random.split(key, 6)
        x = jax.random.normal(k_x, (B, T, D_IN), dtype=jnp.float32)
        W = jax.random.normal(k_w, (D_OUT, D_IN), dtype=jnp.float32) * (1.0 / np.sqrt(D_IN))
        A = jax.random.normal(k_a, (N_ADAPTERS, RANK, D_IN), dtype=jnp.float32) * 0.02
        Bm = jax.random.normal(k_b, (N_ADAPTERS, D_OUT, RANK), dtype=jnp.float32) * 0.02
        scalings = jnp.ones((N_ADAPTERS,), dtype=jnp.float32)
        adapter_idx = jax.random.randint(k_idx, (B,), 0, N_ADAPTERS, dtype=jnp.int32)
        return {'x': x, 'W': W, 'A': A, 'Bm': Bm, 'scalings': scalings, 'adapter_idx': adapter_idx}
    _L1_cond_all = _L1_cond_setup()
    _L1_cond_in = {k: v for k, v in _L1_cond_all.items() if k in ('W', 'A', 'Bm', 'scalings')}
    del _L1_cond_all

    def _L1_ffn_setup():
        import jax, jax.numpy as jnp
        import numpy as np
        NUM_EXPERTS = 8
        HIDDEN = 512
        INTER = 512
        TOP_K = 2
        key = jax.random.key(seed)
        ks = jax.random.split(key, 7)
        hidden_states = jax.random.normal(ks[0], (4, 512, HIDDEN), dtype=jnp.float32)
        gate_w = jax.random.normal(ks[1], (HIDDEN, NUM_EXPERTS), dtype=jnp.float32) * 0.02
        fc1_w = jax.random.normal(ks[2], (NUM_EXPERTS, HIDDEN, INTER), dtype=jnp.float32) * 0.02
        fc1_b = jnp.zeros((NUM_EXPERTS, INTER), dtype=jnp.float32)
        fc2_w = jax.random.normal(ks[3], (NUM_EXPERTS, INTER, HIDDEN), dtype=jnp.float32) * 0.02
        fc2_b = jnp.zeros((NUM_EXPERTS, HIDDEN), dtype=jnp.float32)
        alpha = jax.random.normal(ks[4], (NUM_EXPERTS,), dtype=jnp.float32)
        return {'hidden_states': hidden_states, 'gate_w': gate_w, 'fc1_w': fc1_w, 'fc1_b': fc1_b, 'fc2_w': fc2_w, 'fc2_b': fc2_b, 'alpha': alpha}
    _L1_ffn_all = _L1_ffn_setup()
    _L1_ffn_in = {k: v for k, v in _L1_ffn_all.items() if k in ('gate_w', 'fc1_w', 'fc1_b', 'fc2_w', 'fc2_b', 'alpha')}
    del _L1_ffn_all
    return {'x': x, 'itok_Bx257_0_4111': itok_Bx257_0_4111, 'itok_B_37_3939': itok_B_37_3939, 'itok_B_0_6': itok_B_0_6, 'L0_cond_Wq': _L0_cond_in['Wq'], 'L0_cond_Wk': _L0_cond_in['Wk'], 'L0_cond_Wv': _L0_cond_in['Wv'], 'L0_cond_Wo': _L0_cond_in['Wo'], 'L0_cond_q_norm_scale': _L0_cond_in['q_norm_scale'], 'L0_cond_k_norm_scale': _L0_cond_in['k_norm_scale'], 'L0_cond_k_blocks': _L0_cond_in['k_blocks'], 'L0_cond_v_blocks': _L0_cond_in['v_blocks'], 'L0_ffn_gate_w': _L0_ffn_in['gate_w'], 'L0_ffn_W': _L0_ffn_in['W'], 'L0_ffn_atoms': _L0_ffn_in['atoms'], 'L0_ffn_expert_atom_weights': _L0_ffn_in['expert_atom_weights'], 'L0_ffn_importance': _L0_ffn_in['importance'], 'L0_ffn_mask_idx': _L0_ffn_in['mask_idx'], 'L1_cond_W': _L1_cond_in['W'], 'L1_cond_A': _L1_cond_in['A'], 'L1_cond_Bm': _L1_cond_in['Bm'], 'L1_cond_scalings': _L1_cond_in['scalings'], 'L1_ffn_gate_w': _L1_ffn_in['gate_w'], 'L1_ffn_fc1_w': _L1_ffn_in['fc1_w'], 'L1_ffn_fc1_b': _L1_ffn_in['fc1_b'], 'L1_ffn_fc2_w': _L1_ffn_in['fc2_w'], 'L1_ffn_fc2_b': _L1_ffn_in['fc2_b'], 'L1_ffn_alpha': _L1_ffn_in['alpha']}

def reference(x, itok_Bx257_0_4111, itok_B_37_3939, itok_B_0_6, L0_cond_Wq, L0_cond_Wk, L0_cond_Wv, L0_cond_Wo, L0_cond_q_norm_scale, L0_cond_k_norm_scale, L0_cond_k_blocks, L0_cond_v_blocks, L0_ffn_gate_w, L0_ffn_W, L0_ffn_atoms, L0_ffn_expert_atom_weights, L0_ffn_importance, L0_ffn_mask_idx, L1_cond_W, L1_cond_A, L1_cond_Bm, L1_cond_scalings, L1_ffn_gate_w, L1_ffn_fc1_w, L1_ffn_fc1_b, L1_ffn_fc2_w, L1_ffn_fc2_b, L1_ffn_alpha):
    import jax
    import jax.numpy as jnp

    def _L0_cond_ref(x, Wq, Wk, Wv, Wo, q_norm_scale, k_norm_scale, k_blocks, v_blocks, block_tables, kv_lens):
        import jax, jax.numpy as jnp
        import numpy as np
        H, G, HD = (8, 4, 64)
        GSZ = H // G
        BLOCK = 16
        WINDOW = 256
        SCALE = 256.0 ** (-0.5)
        EPS = 1e-06
        THETA = 10000.0
        B, T, D = (16, 4, 512)
        NBLK = 257

        def _rms(x, scale):
            var = jnp.mean(x * x, axis=-1, keepdims=True)
            return x * jax.lax.rsqrt(var + EPS) * (1.0 + scale)

        def _rope(x, pos):
            half = HD // 2
            inv = 1.0 / THETA ** (jnp.arange(half, dtype=jnp.float32) / half)
            ang = pos[:, :, None].astype(jnp.float32) * inv
            cos = jnp.cos(ang)[:, None, :, :]
            sin = jnp.sin(ang)[:, None, :, :]
            x1, x2 = (x[..., :half], x[..., half:])
            return jnp.concatenate([x1 * cos - x2 * sin, x2 * cos + x1 * sin], axis=-1)
        Bx, Tx, _ = x.shape
        q = jnp.einsum('btd,od->bto', x, Wq).reshape(Bx, Tx, H, HD).transpose(0, 2, 1, 3)
        k = jnp.einsum('btd,od->bto', x, Wk).reshape(Bx, Tx, G, HD).transpose(0, 2, 1, 3)
        v = jnp.einsum('btd,od->bto', x, Wv).reshape(Bx, Tx, G, HD).transpose(0, 2, 1, 3)
        q = _rms(q, q_norm_scale)
        k = _rms(k, k_norm_scale)
        pos = kv_lens[:, None] + jnp.arange(Tx, dtype=jnp.int32)
        q = _rope(q, pos)
        k = _rope(k, pos)
        slot = pos // BLOCK
        off = pos % BLOCK
        blk = jnp.take_along_axis(block_tables, slot, axis=1)
        k_blocks = k_blocks.at[blk, :, off, :].set(k.transpose(0, 2, 1, 3))
        v_blocks = v_blocks.at[blk, :, off, :].set(v.transpose(0, 2, 1, 3))
        k_all = k_blocks[block_tables].transpose(0, 2, 1, 3, 4).reshape(Bx, G, -1, HD)
        v_all = v_blocks[block_tables].transpose(0, 2, 1, 3, 4).reshape(Bx, G, -1, HD)
        S = k_all.shape[2]
        qg = q.reshape(Bx, G, GSZ, Tx, HD)
        scores = jnp.einsum('bghtd,bgsd->bghts', qg, k_all) * SCALE
        kpos = jnp.arange(S, dtype=jnp.int32)
        allowed = (kpos[None, None, :] <= pos[:, :, None]) & (kpos[None, None, :] > pos[:, :, None] - WINDOW)
        scores = jnp.where(allowed[:, None, None, :, :], scores, -jnp.inf)
        p = jax.nn.softmax(scores, axis=-1)
        o = jnp.einsum('bghts,bgsd->bghtd', p, v_all).reshape(Bx, H, Tx, HD)
        o = o.transpose(0, 2, 1, 3).reshape(Bx, Tx, H * HD)
        return jnp.einsum('bto,do->btd', o, Wo)

    def _L0_ffn_ref(x, gate_w, W, atoms, expert_atom_weights, importance, mask_idx):
        import jax, jax.numpy as jnp
        import numpy as np
        TOP_K = 2
        B, S, H = x.shape
        xt = x.reshape(-1, H)
        logits = jnp.clip(xt @ gate_w.T, -50.0, 50.0)
        top_w, top_idx = jax.lax.top_k(logits, TOP_K)
        rw = jax.nn.softmax(top_w, axis=-1)
        deltas = jax.nn.softmax(expert_atom_weights, axis=-1) @ atoms
        weighted = deltas * jax.nn.sigmoid(importance)
        rows = mask_idx // H
        cols = mask_idx % H
        vals = jnp.einsum('tk,tks->ts', rw, weighted[top_idx])
        xg = xt[:, cols]
        contrib = jax.ops.segment_sum((xg * vals).T, rows, num_segments=H)
        out = xt @ W.T + contrib.T
        return out.reshape(B, S, H)

    def _L1_cond_ref(x, W, A, Bm, scalings, adapter_idx):
        import jax, jax.numpy as jnp
        import numpy as np
        B, T, D_IN, D_OUT = (16, 512, 512, 512)
        N_ADAPTERS, RANK = (8, 16)
        H = jnp.einsum('btd,od->bto', x, W)
        A_b = A[adapter_idx]
        B_b = Bm[adapter_idx]
        s_b = scalings[adapter_idx]
        xa = jnp.einsum('btd,brd->btr', x, A_b)
        delta = jnp.einsum('btr,bor->bto', xa, B_b)
        delta = jax.lax.stop_gradient(delta * s_b[:, None, None])
        return H + delta

    def _L1_ffn_ref(hidden_states, gate_w, fc1_w, fc1_b, fc2_w, fc2_b, alpha):
        import jax, jax.numpy as jnp
        import numpy as np
        NUM_EXPERTS = 8
        HIDDEN = 512
        INTER = 512
        TOP_K = 2
        B, S, H = hidden_states.shape
        x = hidden_states.reshape(-1, H)
        probs = jax.nn.softmax(x @ gate_w, axis=-1)
        gate_score, gate_idx = jax.lax.top_k(probs, TOP_K)
        gate_score = gate_score / jnp.sum(gate_score, axis=-1, keepdims=True)
        onehot = jax.nn.one_hot(gate_idx, NUM_EXPERTS, dtype=x.dtype)
        combine = jnp.einsum('tk,tke->te', gate_score, onehot) * alpha[None, :]
        h = jnp.einsum('th,ehi->eti', x, fc1_w) + fc1_b[:, None, :]
        h = jax.nn.gelu(h, approximate=False)
        y = jnp.einsum('eti,eih->eth', h, fc2_w) + fc2_b[:, None, :]
        out = jnp.einsum('eth,te->th', y, combine)
        return out.reshape(B, S, H)
    x = x + _L0_ffn_ref(_L0_cond_ref(x, L0_cond_Wq, L0_cond_Wk, L0_cond_Wv, L0_cond_Wo, L0_cond_q_norm_scale, L0_cond_k_norm_scale, L0_cond_k_blocks, L0_cond_v_blocks, itok_Bx257_0_4111, itok_B_37_3939), L0_ffn_gate_w, L0_ffn_W, L0_ffn_atoms, L0_ffn_expert_atom_weights, L0_ffn_importance, L0_ffn_mask_idx)
    x = x + _L1_ffn_ref(_L1_cond_ref(x, L1_cond_W, L1_cond_A, L1_cond_Bm, L1_cond_scalings, itok_B_0_6), L1_ffn_gate_w, L1_ffn_fc1_w, L1_ffn_fc1_b, L1_ffn_fc2_w, L1_ffn_fc2_b, L1_ffn_alpha)
    return x

_drawn_inputs = setup_inputs


def setup_inputs(seed=0):
    import zlib

    import numpy as np

    out = dict(_drawn_inputs(seed))
    spreads = {'L1_cond_scalings': (1.0, 0.6), 'L1_ffn_fc1_b': (0.0, 0.408), 'L1_ffn_fc2_b': (0.0, 0.1)}
    factors = {'L0_cond_Wq': 3.057,
     'L0_cond_Wk': 19.862,
     'L0_cond_q_norm_scale': 8.0,
     'L0_cond_k_norm_scale': 64.0,
     'L0_cond_k_blocks': 4.105,
     'L0_ffn_gate_w': 37.903,
     'L0_ffn_atoms': 25.087,
     'L0_ffn_expert_atom_weights': 37.31,
     'L0_ffn_importance': 56.304,
     'L1_cond_A': 3.047,
     'L1_cond_Bm': 3.445,
     'L0_cond_Wv': 3.22}
    for name, (base, spread) in spreads.items():
        noise = np.random.default_rng([zlib.crc32(name.encode()), seed]).standard_normal(out[name].shape)
        drawn = base * np.exp(spread * noise) if base else spread * noise
        out[name] = jnp.asarray(drawn.astype(out[name].dtype))
    for name, factor in factors.items():
        out[name] = (out[name] * factor).astype(out[name].dtype)
    return out
```

```python
import numpy as np

import concourse.bass as bass
from concourse import mybir
from contextlib import ExitStack

F32 = mybir.dt.float32
BF16 = mybir.dt.bfloat16
I32 = mybir.dt.int32
ALU = mybir.AluOpType
ACT = mybir.ActivationFunctionType
AX = mybir.AxisListType.X

P = 128
NB, T, D = 8, 256, 512
N = NB * T
NT = N // P
KC = D // P
NH, NG, HD = 8, 4, 64
BLK, NBLK = 16, 257
NPHYS = 16 * NBLK
SEQ = BLK * NBLK
WIN = 256
NJ = 2 * WIN
NC = NJ // P
KW = WIN + P
SB = NJ // BLK + 1
SW = T // BLK + 1
SCALE = 256.0 ** -0.5
RMS_EPS = 1e-6
THETA = 10000.0
NE = 8
NS = 4096
ST = NS // P
NTILE = 2 * N // P + NE
CELLS = D * D
RANK = 16
BIG = 1e30
NQK = NH + NG
QK = NQK * HD


def words(region, off, dims, dt=F32, parts=P):
    n = int(np.prod(dims))
    a = region[0:parts, off:off + n]
    if dt != F32:
        a = a.bitcast(dt)
    if len(dims) == 1:
        return a
    names = "abcd"[:len(dims)]
    return a.rearrange(f"p ({' '.join(names)}) -> p {' '.join(names)}",
                       **{c: int(d) for c, d in zip(names[1:], dims[1:])})


def program(nc, d):
    ctx = ExitStack()
    with ctx:
        def sb(name, shape, dt=F32):
            return ctx.enter_context(nc.sbuf_tensor(name, shape, dt))

        def sem(name):
            return ctx.enter_context(nc.semaphore(name))

        def sem2(name):
            return [sem(name + "_0"), sem(name + "_1")]

        R1 = sb("R1", [P, 16384])
        R2 = sb("R2", [P, 16384])
        R3 = sb("R3", [P, 8192])
        R4 = sb("R4", [P, 8192])
        zero = words(R1, 0, [2048])
        mask_bc = words(R1, 2048, [NS], I32)
        eq_all = words(R1, 6144, [ST, P])
        eq_low = words(R1, 10240, [ST, P])
        table_bc = words(R3, 0, [BLK + NB * NBLK + 24], I32)
        hits = words(R3, 2112, [NC * NB, NB * SW])
        win = words(R3, 7012, [NB, SB])
        eqk = words(R3, 7276, [NB, 9])
        tmp9 = words(R3, 7348, [NB, 9])
        wr_blk = words(R3, 7420, [NB, SW])
        wr_tok = words(R3, 7556, [NB, SW])
        imp = words(R4, 4096, [ST, NE])
        wgt = words(R4, 4352, [ST, NE])
        wqkv = words(R2, 0, [KC, 2 * D])
        tab_a = words(R2, 4096, [NT, 2, HD])
        tab_b = words(R2, 6144, [NT, 2, HD])
        xt = [words(R2, 8192 + 512 * s, [KC, P]) for s in range(2)]
        sq = [words(R2, 9216, [QK]), words(R2, 14336, [QK])]
        nrm = words(R2, 9984, [QK])
        rot_a = words(R2, 10752, [QK])
        rot_b = words(R2, 11520, [QK])
        qkv_out = [words(R2, 12288 + 1024 * s, [2 * D]) for s in range(2)]
        ang = words(R2, 14336, [NT, HD // 2])
        ang2 = words(R2, 14848, [NT, HD // 2])
        sin_t = words(R2, 15360, [NT, HD // 2])
        cos_t = words(R2, 15872, [NT, HD // 2])
        k_t = words(R2, 0, [2, NJ])
        q_in = [words(R2, 2048 + 1024 * s, [2, D]) for s in range(2)]
        q_t = words(R2, 4096, [4, T])
        msk_s = [words(R2, 6144 + KW * s, [KW]) for s in range(2)]
        prob = [words(R2, 6912 + KW * s, [KW]) for s in range(3)]
        prob_t = [words(R2, 8064 + KW * s, [KW]) for s in range(3)]
        mask = words(R2, 9216, [2, KW])
        key_bias = words(R2, 9984, [NJ])
        o_sb = words(R2, 10496, [D])
        o_t = words(R2, 11520, [KC, P])
        a_row = words(R2, 12544, [D])
        a_t = words(R2, 13568, [KC, P])
        stage = words(R2, 14080, [2048])
        w_o = words(R4, 0, [KC, D])
        w0_t = words(R4, 2048, [KC, D])
        kv = [words(R4, 4096 + 2048 * s, [NC, D]) for s in range(2)]
        m_w = words(R1, 0, [KC, NE, D])
        a_rows = words(R3, 0, [NT, D])
        xs_in = [words(R3, 512 * s, [D]) for s in range(2)]
        xs_t = [words(R3, 1024 + 512 * s, [KC, P]) for s in range(2)]
        h_sb = [words(R3, 2048 + 512 * s, [D]) for s in range(2)]
        h_t = [words(R3, 3072 + 512 * s, [KC, P]) for s in range(2)]
        y_sb = [words(R3, 4096 + 512 * s, [D]) for s in range(2)]
        fc1 = words(R2, 0, [KC, NE, D])
        fc2 = words(R1, 0, [KC, NE, D])
        b1_bc = words(R4, 0, [NE, D])
        b2_bc = words(R4, 4096, [NE, D])
        x_row = [words(R3, 512 * s, [D]) for s in range(2)]
        y1 = [words(R3, 1024 + 512 * s, [D]) for s in range(2)]
        y2 = [words(R3, 2048 + 512 * s, [D]) for s in range(2)]
        x1 = [words(R3, 3072 + 512 * s, [D]) for s in range(2)]
        x1_t = [words(R3, 4096 + 512 * s, [KC, P]) for s in range(2)]
        xa_t = [words(R3, 5120 + 128 * s, [P]) for s in range(2)]
        x2_t = [words(R3, 5376 + 512 * s, [KC, P]) for s in range(2)]
        x2 = [words(R3, 6400 + 512 * s, [D]) for s in range(2)]
        w1_t = words(R2, 0, [KC, D])
        lora_a = words(R2, 2048, [KC, P])
        lora_b = words(R2, 2560, [D])
        x2_rows = words(R4, 0, [NT, D])

        ident = sb("ident", [P, P])
        tri = sb("tri", [P, P], BF16)
        ones = sb("ones", [P, P], BF16)
        low = sb("low", [P, P])
        band = sb("band", [P, KW], BF16)
        jrow = sb("jrow", [P, NJ], BF16)
        gate0 = sb("gate0", [P, KC, NE])
        gate1 = sb("gate1", [P, KC, NE])
        lens_i = sb("lens_i", [P, NB], I32)
        ints = sb("ints", [P, 64], I32)
        lens = sb("lens", [P, NB])
        lo = sb("lo", [P, NB])
        first = sb("first", [P, NB])
        adapt_i = sb("adapt_i", [P, NB], I32)
        scal_bc = sb("scal_bc", [P, NE])
        alpha_bc = sb("alpha_bc", [P, NE])
        part = sb("part", [P, 4])
        iot = sb("iot", [P, 64], I32)
        iof = sb("iof", [P, 64])
        rev = sb("rev", [P, NE])
        sel_b = sb("sel_b", [P, NB])
        gains = sb("gains", [P, 2, HD])
        inv_f = sb("inv_f", [P, HD // 2])
        pos = sb("pos", [P, NT])
        carry = sb("carry", [P, NB])
        off = sb("off", [P, NB])
        blk = sb("blk", [P, NC, NB])
        edge = sb("edge", [P, 2, NB, NB])
        best = sb("best", [P, NC, NB])
        fidx = sb("fidx", [P, NC, NB])
        found = sb("found", [P, NC, NB])
        old_idx = sb("old_idx", [P, 2 * NB], I32)
        new_idx = sb("new_idx", [P, NC * NB], I32)
        ms_i = sb("ms_i", [P, ST], I32)
        ms_f = sb("ms_f", [P, ST])
        cell_i = sb("cell_i", [P, ST], I32)
        cell_j = sb("cell_j", [P, ST], I32)
        cell_f = sb("cell_f", [P, ST])
        dup = sb("dup", [P, ST])
        atoms = words(R4, 0, [NS], F32, 64)
        eaw = sb("eaw", [NE, 64])
        eaw_s = sb("eaw_s", [NE, 4])
        eaw_t = sb("eaw_t", [64, NE])
        tot = sb("tot", [P, ST, NE])
        ss = sb("ss", [P, 2, NQK])
        rstd = sb("rstd", [P, 2, NQK])
        mhalf = sb("mhalf", [P, NQK])
        mx = sb("mx", [P, 16])
        nmx = sb("nmx", [P, 16])
        sums = sb("sums", [P, 16])
        rsum = sb("rsum", [P, NH])
        junk = sb("junk", [P, 4])
        junk_a = sb("junk_a", [P, 4])
        lg = sb("lg", [P, NT, NE])
        t1 = sb("t1", [P, NT, NE])
        t2 = sb("t2", [P, NT, NE])
        oh1 = sb("oh1", [P, NT, NE])
        oh2 = sb("oh2", [P, NT, NE])
        m1 = sb("m1", [P, NT])
        m2 = sb("m2", [P, NT])
        rr = sb("rr", [P, NT])
        cw1 = sb("cw1", [P, NT])
        cw2 = sb("cw2", [P, NT])
        selb16 = sb("selb16", [P, NT, NE], BF16)
        totl = sb("totl", [P, NT, NE])
        cum = [sb(f"cum{i}", [P, NT, NE]) for i in range(2)]
        nti = sb("nti", [P, NE], I32)
        ntf = [sb(f"ntf{i}", [P, NE]) for i in range(3)]
        slot_f = sb("slot_f", [P, 2, NT])
        slot_i = sb("slot_i", [P, 2, NT], I32)
        ex_c = sb("ex_c", [P, NTILE, NE - 1])
        ex_f = sb("ex_f", [P, NTILE])
        ex_i = sb("ex_i", [P, NTILE], I32)
        tile_io = sb("tile_io", [P, NTILE])
        tile_ii = sb("tile_ii", [P, NTILE], I32)
        jrow_i = words(R3, 6500, [NJ], I32)

        ps = ctx.enter_context(nc.psum_tensor("ps", [P, 8, 512], F32))

        def bank(b, dims=None):
            a = ps[:, b, :]
            if dims is None:
                return a
            n = int(np.prod(dims))
            a = ps[:, b, 0:n]
            if len(dims) == 1:
                return a
            return a.rearrange("p (a b) -> p a b", b=int(dims[-1]))

        S = {}
        for name in ("const_dma p0_dma iota band_ok rope_in rope_r rope_ok p0_done w_eaw w_eawt pe_eawt eaw_e imp_s "
                     "pe_del wgt_ok eqa eql pe_tot tot_ok cell_ok mz zdone mscat kvc pool_c "
                     "s_dot s_mx s_exp s_pt s_pv s_norm ped pea bk0 bk1 bc0 bc1 arow mstage mready m_done "
                     "att_w lg_ok r_exp0 r_exp r_sel r_pre r_ok r_e xs_sc w5 b_dma fc1_d fc2_d "
                     "outs x1w rms_h pst").split():
            S[name] = sem(name)
        S2 = {}
        for name in ("x_in qkv a1 ssd rs p1p p1o p1w kvd q_ld "
                     "l_in l_tx l_xt l_mm l_ye l_st k_in k_tx k_xt k_m1 k_hb k_hg k_th k_ht k_m2 k_ye k_st "
                     "c_in c_x1 c_tx c_xt c_xa c_xe c_h c_x2a c_x2b c_t2 c_t2e c_g c_lg c_st ga_y fin_y f_in f_o f_st").split():
            S2[name] = sem2(name)

        block = ctx.enter_context(nc.Block())

        @block.sync
        def _(sp):
            n0 = 0
            for dst, src in (
                    (lens_i[:], d["lens"].partition_broadcast(P)),
                    (table_bc[:, BLK:BLK + NB * NBLK], d["table"].partition_broadcast(P)),
                    (inv_f[:], d["inv_freq"].partition_broadcast(P)),
                    (gains[:, 0, :], d["q_gain"].partition_broadcast(P)),
                    (gains[:, 1, :], d["k_gain"].partition_broadcast(P)),
                    (adapt_i[:], d["adapter"].partition_broadcast(P)),
                    (scal_bc[:], d["scal"].partition_broadcast(P)),
                    (alpha_bc[:], d["alpha"].partition_broadcast(P)),
                    (mask_bc, d["mask_idx"].partition_broadcast(P)),
                    (ms_i[:], d["mask_idx"].rearrange("(p t) -> p t", t=ST)),
                    (eaw[:], d["eaw"]),
                    (imp, d["imp_t"].rearrange("(p t) e -> p t e", t=ST)),
                    (atoms, d["atoms"])):
                sp.dma_start(dst, src).then_inc(S["p0_dma"], 16)
                n0 += 16
            sp.dma_start(wqkv, d["wqkv_t"].rearrange("(k p) n -> p k n", p=P)).then_inc(S["const_dma"], 16)
            sp.dma_start(gate0[:], d["gate0_t"].rearrange("(k p) n -> p k n", p=P)).then_inc(S["const_dma"], 16)
            sp.dma_start(gate1[:], d["gate1"].rearrange("(k p) n -> p k n", p=P)).then_inc(S["const_dma"], 16)

            xt_v = d["x_t"].rearrange("(k p) (t m) -> p k t m", p=P, m=P)
            qn_v = d["qn"].rearrange("(t p) n -> p t n", p=P)
            np_v = d["new_kv"].rearrange("(t p) n -> p t n", p=P)

            def load_x(t, s):
                sp.dma_start(xt[s], xt_v[:, :, t, :]).then_inc(S2["x_in"][s], 16)

            def store_qkv(t, s):
                sp.dma_start(qn_v[:, t, :], qkv_out[s][:, 0:D]).then_inc(S2["p1w"][s], 16)
                sp.dma_start(np_v[:, t, :], qkv_out[s][:, D:2 * D]).then_inc(S2["p1w"][s], 16)

            load_x(0, 0)
            load_x(1, 1)
            sp.wait_ge(S["mz"], 1)
            mb = d["m_buf"][0:CELLS, :].rearrange("(p a) e -> p (a e)", p=P)
            for i in range(8):
                sp.dma_start(mb[:, 2048 * i:2048 * (i + 1)], zero).then_inc(S["zdone"], 16)
            sp.dma_start(d["m_buf"][CELLS:CELLS + P, :], zero[:, 0:NE]).then_inc(S["zdone"], 16)
            xz = d["xs"].rearrange("(p a) n -> p a n", p=P)
            for i in range(NTILE // 4):
                sp.dma_start(xz[:, 4 * i:4 * i + 4, :], zero).then_inc(S["zdone"], 16)
            with sp.Fori(0, NT // 2 - 1) as i:
                for s in range(2):
                    sp.wait_ge(S2["qkv"][s], i + 1)
                    load_x(2 * i + 2 + s, s)
                for s in range(2):
                    sp.wait_ge(S2["p1o"][s], i + 1)
                    store_qkv(2 * i + s, s)
            for s in range(2):
                sp.wait_ge(S2["p1o"][s], NT // 2)
                store_qkv(NT - 2 + s, s)

            sp.wait_ge(S["tot_ok"], 1)
            sp.dma_start(w_o, d["wo_t"].rearrange("(k p) n -> p k n", p=P)).then_inc(S["att_w"], 16)
            sp.dma_start(w0_t, d["w0_t"].rearrange("(k p) n -> p k n", p=P)).then_inc(S["att_w"], 16)
            for s in range(2):
                sp.wait_ge(S2["p1w"][s], 32 * (NT // 2))
            qb_v = d["qn"].rearrange("(b t p) n -> p b t n", t=2, p=P)
            for s in range(2):
                sp.dma_start(q_in[s], qb_v[:, s, :, :]).then_inc(S2["q_ld"][s], 16)
            with sp.Fori(0, NB // 2 - 1) as i:
                for s in range(2):
                    sp.wait_ge(S["bk1"], 12 * i + 6 * s + 2)
                    sp.dma_start(q_in[s], qb_v[:, 2 * i + 2 + s, :, :]).then_inc(S2["q_ld"][s], 16)

            xs_v = d["xs"].rearrange("(t p) n -> p t n", p=P)
            ys_v = d["ys"].rearrange("(t p) n -> p t n", p=P)

            def expert_io(load, read, made, stored):
                for s in range(2):
                    sp.dma_start(xs_in[s], xs_v[:, s, :]).then_inc(load[s], 16)
                with sp.Fori(0, NTILE // 2 - 1) as i:
                    for s in range(2):
                        sp.wait_ge(read[s], i + 1)
                        sp.dma_start(xs_in[s], xs_v[:, 2 * i + 2 + s, :]).then_inc(load[s], 16)
                    for s in range(2):
                        sp.wait_ge(made[s], i + 1)
                        sp.dma_start(ys_v[:, 2 * i + s, :], y_sb[s]).then_inc(stored[s], 16)
                for s in range(2):
                    sp.wait_ge(made[s], NTILE // 2)
                    sp.dma_start(ys_v[:, NTILE - 2 + s, :], y_sb[s]).then_inc(stored[s], 16)

            sp.wait_ge(S["xs_sc"], 32 * NT)
            sp.dma_start(w1_t, d["w1_t"].rearrange("(k p) n -> p k n", p=P)).then_inc(S["w5"], 16)
            sp.dma_start(lora_a, d["a_t"].rearrange("(k p) n -> p k n", p=P)).then_inc(S["w5"], 16)
            sp.dma_start(lora_b, d["b_t"]).then_inc(S["w5"], 16)
            expert_io(S2["l_in"], S2["l_tx"], S2["l_ye"], S2["l_st"])

            x_v = d["x"].rearrange("(t p) n -> p t n", p=P)
            x1_v = d["x1"].rearrange("(t p) n -> p t n", p=P)
            for s in range(2):
                sp.wait_ge(S2["l_st"][s], 16 * (NTILE // 2))
            for s in range(2):
                sp.dma_start(x_row[s], x_v[:, s, :]).then_inc(S2["c_in"][s], 16)
            fc2_v = d["fc2"].rearrange("e (k p) n -> p k e n", p=P)
            for k in range(KC):
                sp.dma_start(fc2[:, k], fc2_v[:, k]).then_inc(S["fc2_d"], 16)
            with sp.Fori(0, NT // 2 - 1) as i:
                for s in range(2):
                    sp.wait_ge(S2["c_x1"][s], i + 1)
                    sp.dma_start(x_row[s], x_v[:, 2 * i + 2 + s, :]).then_inc(S2["c_in"][s], 16)
                    sp.dma_start(x1_v[:, 2 * i + s, :], x1[s]).then_inc(S2["c_st"][s], 16)
            for s in range(2):
                sp.wait_ge(S2["c_x1"][s], NT // 2)
                sp.dma_start(x1_v[:, NT - 2 + s, :], x1[s]).then_inc(S2["c_st"][s], 16)
            for s in range(2):
                sp.wait_ge(S2["c_h"][s], NT // 2)
            fc1_v = d["fc1"].rearrange("e (k p) n -> p k e n", p=P)
            for k in range(KC):
                sp.dma_start(fc1[:, k], fc1_v[:, k]).then_inc(S["fc1_d"], 16)
            sp.wait_ge(S["xs_sc"], 64 * NT)
            sp.dma_start(b1_bc, d["b1"].partition_broadcast(P)).then_inc(S["b_dma"], 16)
            sp.dma_start(b2_bc, d["b2"].partition_broadcast(P)).then_inc(S["b_dma"], 16)
            expert_io(S2["k_in"], S2["k_tx"], S2["k_ye"], S2["k_st"])

            out_v = d["out"].rearrange("(t p) n -> p t n", p=P)
            for s in range(2):
                sp.wait_ge(S2["c_st"][s], 16 * (NT // 2))
                sp.wait_ge(S2["k_st"][s], 16 * (NTILE // 2))
            for s in range(2):
                sp.dma_start(x_row[s], x1_v[:, s, :]).then_inc(S2["f_in"][s], 16)
            with sp.Fori(0, NT // 2 - 1) as i:
                for s in range(2):
                    sp.wait_ge(S2["f_o"][s], i + 1)
                    sp.dma_start(x_row[s], x1_v[:, 2 * i + 2 + s, :]).then_inc(S2["f_in"][s], 16)
                    sp.dma_start(out_v[:, 2 * i + s, :], x1[s]).then_inc(S2["f_st"][s], 16)
            for s in range(2):
                sp.wait_ge(S2["f_o"][s], NT // 2)
                sp.dma_start(out_v[:, NT - 2 + s, :], x1[s]).then_inc(S2["f_st"][s], 16)
            for s in range(2):
                sp.wait_ge(S2["f_st"][s], 16 * (NT // 2))

        @block.gpsimd
        def _(po):
            po.memset(zero, 0.0)
            po.drain().then_inc(S["mz"], 1)
            po.iota(iot[:, 0:32], [[1, 32]], base=0, channel_multiplier=0)
            po.iota(iot[:, 32:33], [[0, 1]], base=0, channel_multiplier=1)
            po.iota(tile_ii[:], [[1, NTILE]], base=0, channel_multiplier=0)
            po.iota(jrow_i, [[1, NJ]], base=-WIN, channel_multiplier=0)
            po.memset(ident[:], 0.0)
            po.memset(tri[:], 1.0)
            po.memset(ones[:], 1.0)
            po.memset(low[:], 1.0)
            po.memset(band[:], 0.0)
            po.memset(mhalf[:], -0.5)
            po.memset(table_bc[:, 0:BLK], 0)
            po.memset(table_bc[:, BLK + NB * NBLK:], 0)
            po.drain()
            po.affine_select(out=ident[:], in_=ident[:], compare_op=ALU.not_equal, fill=1.0, base=0,
                             pattern=[[-1, P]], channel_multiplier=1)
            po.affine_select(out=tri[:], in_=tri[:], compare_op=ALU.is_gt, fill=0.0, base=0,
                             pattern=[[1, P]], channel_multiplier=-1)
            po.affine_select(out=low[:], in_=low[:], compare_op=ALU.is_gt, fill=0.0, base=0,
                             pattern=[[-1, P]], channel_multiplier=1)
            po.affine_select(out=band[:], in_=band[:], compare_op=ALU.is_gt, fill=-BIG, base=0,
                             pattern=[[1, KW]], channel_multiplier=-1)
            po.drain()
            po.affine_select(out=band[:], in_=band[:], compare_op=ALU.is_ge, fill=-BIG, base=WIN,
                             pattern=[[-1, KW]], channel_multiplier=1)
            po.drain().then_inc(S["iota"], 1)
            po.wait_ge(S["eqa"], 1)
            po.tensor_tensor(eq_low, eq_all, low[:].unsqueeze(1).broadcast_to([P, ST, P]), ALU.mult).then_inc(S["eql"], 1)

            def old_rows(b):
                for c in range(2):
                    col = c * NB + b
                    po.indirect_dma_start(out=kv[b % 2][:, c, :], out_offset=None, in_=d["kv_pool"],
                                          in_offset=bass.IndirectOffsetOnAxis(ap=old_idx[:, col:col + 1], axis=0)
                                          ).then_inc(S["kvc"], 16)

            def new_rows(b):
                for c in (2, 3):
                    col = c * NB + b
                    po.indirect_dma_start(out=kv[b % 2][:, c, :], out_offset=None, in_=d["new_kv"],
                                          in_offset=bass.IndirectOffsetOnAxis(ap=new_idx[:, col:col + 1], axis=0)
                                          ).then_inc(S2["kvd"][b % 2], 16)
                po.wait_ge(S["kvc"], 32 * (b + 1))
                for c in range(2):
                    col = c * NB + b
                    po.indirect_dma_start(out=kv[b % 2][:, c, :], out_offset=None, in_=d["new_kv"],
                                          in_offset=bass.IndirectOffsetOnAxis(ap=new_idx[:, col:col + 1], axis=0),
                                          bounds_check=N - 1, oob_is_err=False).then_inc(S2["kvd"][b % 2], 16)

            def rms(i):
                for s in range(2):
                    po.wait_ge(S2["ssd"][s], i + 1)
                    po.tensor_tensor(rstd[:, s, :], ss[:, s, :], mhalf[:], ALU.pow).then_inc(S2["rs"][s], 1)
            with po.Fori(0, NT // 2) as i:
                rms(i)

            po.wait_ge(S["p0_done"], 1)
            po.wait_ge(S["tot_ok"], 1)
            for b in range(2):
                old_rows(b)
            po.wait_ge(S["cell_ok"], 1)
            po.wait_ge(S["zdone"], 16 * (9 + NTILE // 4))
            for t in range(ST // 2):
                if t:
                    po.wait_ge(S["mscat"], 16 * t)
                po.indirect_dma_start(out=d["m_buf"], out_offset=bass.IndirectOffsetOnAxis(ap=cell_i[:, t:t + 1], axis=0),
                                      in_=tot[:, t, :], in_offset=None, compute_op=ALU.add).then_inc(S["mscat"], 16)
            for s in range(2):
                po.wait_ge(S2["p1w"][s], 32 * (NT // 2))
            for b in range(2):
                new_rows(b)
            for t in range(ST // 2, ST):
                po.wait_ge(S["mscat"], 16 * t)
                po.indirect_dma_start(out=d["m_buf"], out_offset=bass.IndirectOffsetOnAxis(ap=cell_i[:, t:t + 1], axis=0),
                                      in_=tot[:, t, :], in_offset=None, compute_op=ALU.add).then_inc(S["mscat"], 16)
            po.wait_ge(S["mscat"], 16 * ST)
            po.wait_ge(S["att_w"], 32)
            mst = d["m_buf"][0:CELLS, :].rearrange("(k p r) e -> p k (r e)", k=KC, p=P)
            po.dma_start(stage, mst[:, 0, 0:2048]).then_inc(S["mstage"], 16)
            for b in range(NB):
                k, r = b // 2, 256 * (b % 2)
                po.wait_ge(S["mstage"], 16 * (b + 1))
                po.tensor_tensor(m_w[:, k, :, r:r + 256], stage.rearrange("p (r e) -> p e r", e=NE),
                                 w0_t[:, k, r:r + 256].unsqueeze(1).broadcast_to([P, NE, 256]), ALU.add
                                 ).then_inc(S["m_done"], 1)
                if b + 1 < NB:
                    po.wait_ge(S["m_done"], b + 1)
                    po.dma_start(stage, mst[:, (b + 1) // 2, 2048 * ((b + 1) % 2):2048 * ((b + 1) % 2 + 1)]
                                 ).then_inc(S["mstage"], 16)
                for qt in range(2):
                    po.wait_ge(S["bc1"], 6 * b + 3 + 2 * qt)
                    po.tensor_copy(a_rows[:, 2 * b + qt, :], a_row).then_inc(S["arow"], 1)
                if b + 2 < NB:
                    po.wait_ge(S["s_pv"], 16 * (b + 1))
                    old_rows(b + 2)
                    new_rows(b + 2)
            def scatter(rows, before):
                po.wait_ge(S["r_ok"], before + 1)
                for t in range(NT):
                    for c in range(2):
                        po.indirect_dma_start(out=d["xs"],
                                              out_offset=bass.IndirectOffsetOnAxis(ap=slot_i[:, c, t:t + 1], axis=0),
                                              in_=rows[:, t, :], in_offset=None).then_inc(S["xs_sc"], 16)

            def gather(used, ready):
                for t in range(NT):
                    s = t % 2
                    if t >= 2:
                        po.wait_ge(used[s], t // 2)
                    for c, y in enumerate((y1, y2)):
                        po.indirect_dma_start(out=y[s], out_offset=None, in_=d["ys"],
                                              in_offset=bass.IndirectOffsetOnAxis(ap=slot_i[:, c, t:t + 1], axis=0)
                                              ).then_inc(ready[s], 16)

            po.wait_ge(S["arow"], NT)
            scatter(a_rows, 0)
            for s in range(2):
                po.wait_ge(S2["l_st"][s], 16 * (NTILE // 2))
            gather(S2["c_x1"], S2["ga_y"])
            scatter(x2_rows, 1)
            for s in range(2):
                po.wait_ge(S2["k_st"][s], 16 * (NTILE // 2))
            gather(S2["f_o"], S2["fin_y"])

        @block.tensor
        def _(pe):
            pe.wait_ge(S["iota"], 1)
            pe.wait_ge(S["const_dma"], 48)
            pe.wait_ge(S["w_eaw"], 1)
            pe.transpose(ps[0:64, 6, 0:NE], eaw[:], ident[0:NE, 0:NE]).then_inc(S["pe_eawt"], 1)
            pe.wait_ge(S["w_eawt"], 1)
            at_v = atoms.rearrange("a (p t) -> a t p", t=ST)
            for t in range(ST):
                m = pe.matmul(ps[:, 6, t * NE:(t + 1) * NE], at_v[:, t, :], eaw_t[:], start=True, stop=True)
            m.then_inc(S["pe_del"], 1)
            pe.wait_ge(S["wgt_ok"], 1)
            for t in range(ST):
                m = pe.matmul(ps[:, 7, t * NE:(t + 1) * NE], eq_all[:, t, :], wgt[:, t, :], start=True, stop=True)
            m.then_inc(S["pe_tot"], 1)
            with pe.Fori(0, NT // 2) as i:
                for s in range(2):
                    pe.wait_ge(S2["x_in"][s], 16 * i + 16)
                    pe.wait_ge(S2["p1p"][s], i)
                    for h in range(2):
                        for k in range(KC):
                            m = pe.matmul(ps[:, 2 * s + h, :], xt[s][:, k, :], wqkv[:, k, h * D:(h + 1) * D],
                                          start=(k == 0), stop=(k == KC - 1))
                    m.then_inc(S2["qkv"][s], 1)
            for s in range(2):
                pe.wait_ge(S2["p1p"][s], NT // 2)
            pe.wait_ge(S["att_w"], 32)

            def batch(B, s, i):
                kvs = kv[s]
                pe.wait_ge(S2["kvd"][s], 64 * i + 64)
                for p in range(2):
                    pe.wait_ge(S["bc0" if p == 0 else "bc1"], 6 * B)
                    for c in range(NC):
                        m = pe.transpose(ps[:, p, c * P:(c + 1) * P], kvs[:, c, p * P:(p + 1) * P], ident[:])
                    m.then_inc(S["bk0" if p == 0 else "bk1"], 1)
                pe.wait_ge(S2["q_ld"][s], 16 * i + 16)
                for qt in range(2):
                    pe.wait_ge(S["bc0" if qt == 0 else "bc1"], 6 * B + 1)
                    for jj in range(4):
                        m = pe.transpose(ps[:, qt, jj * P:(jj + 1) * P], q_in[s][:, qt, jj * P:(jj + 1) * P], ident[:])
                    m.then_inc(S["bk0" if qt == 0 else "bk1"], 1)

                def dots(u):
                    qt, h = u // NH, u % NH
                    g = h // 2
                    base, p, jj = 64 * (g % 2), g // 2, (g // 2) * 2 + h % 2
                    if u == 0:
                        pe.wait_ge(S["bc0"], 6 * B + 2)
                        pe.wait_ge(S["bc1"], 6 * B + 2)
                    pe.wait_ge(S["s_mx"], 16 * B + max(u - 1, 0))
                    pe.matmul(ps[:, 2 + u % 2, 0:KW], q_t[base:base + 64, jj, qt * P:(qt + 1) * P],
                              k_t[base:base + 64, p, qt * P:qt * P + KW], start=True, stop=True).then_inc(S["s_dot"], 1)

                def turn(u):
                    pe.wait_ge(S["s_exp"], 16 * B + u + 1)
                    pe.wait_ge(S["ped" if u % 2 == 0 else "pea"], 8 * B + u // 2)
                    for c in range(3):
                        m = pe.transpose(ps[:, 4 + u % 2, c * P:(c + 1) * P], prob[u % 3][:, c * P:(c + 1) * P], ident[:])
                    m.then_inc(S["s_pt"], 1)

                def mix(u):
                    qt, h = u // NH, u % NH
                    g = h // 2
                    pe.wait_ge(S["ped" if u % 2 == 0 else "pea"], 8 * B + u // 2 + 1)
                    if h == 0:
                        pe.wait_ge(S["s_norm"], 2 * B)
                    for c in range(3):
                        m = pe.matmul(ps[:, 6 + qt, h * HD:(h + 1) * HD], prob_t[u % 3][:, c * P:(c + 1) * P],
                                      kvs[:, qt + c, (NG + g) * HD:(NG + g + 1) * HD], start=(c == 0), stop=(c == 2))
                    m.then_inc(S["s_pv"], 1)

                def tail(qt, step):
                    n = 2 + 2 * qt
                    if step == 0:
                        pe.wait_ge(S["s_norm"], 2 * B + qt + 1)
                        pe.wait_ge(S["bc0"], 6 * B + n)
                        for k in range(KC):
                            m = pe.transpose(ps[:, 0, k * P:(k + 1) * P], o_sb[:, k * P:(k + 1) * P], ident[:])
                        m.then_inc(S["bk0"], 1)
                    elif step == 1:
                        pe.wait_ge(S["bc0"], 6 * B + n + 1)
                        pe.wait_ge(S["bc1"], 6 * B + n)
                        for k in range(KC):
                            m = pe.matmul(ps[:, 1, :], o_t[:, k, :], w_o[:, k, :], start=(k == 0), stop=(k == KC - 1))
                        m.then_inc(S["bk1"], 1)
                    elif step == 2:
                        pe.wait_ge(S["bc1"], 6 * B + n + 1)
                        for k in range(KC):
                            m = pe.transpose(ps[:, 0, k * P:(k + 1) * P], a_row[:, k * P:(k + 1) * P], ident[:])
                        m.then_inc(S["bk0"], 1)
                    else:
                        pe.wait_ge(S["bc0"], 6 * B + n + 2)
                        for k in range(KC):
                            m = pe.matmul(ps[:, 1, 0:NE], a_t[:, k, :], gate0[:, k, :], start=(k == 0), stop=(k == KC - 1))
                        m.then_inc(S["bk1"], 1)

                for st in range(19):
                    if st < 16:
                        dots(st)
                    if 0 <= st - 2 < 16:
                        turn(st - 2)
                    if 0 <= st - 3 < 16:
                        mix(st - 3)
                    if st in (11, 12, 14, 15):
                        tail(0, (11, 12, 14, 15).index(st))
                for step in range(4):
                    tail(1, step)

            with pe.Fori(0, NB // 2) as i:
                for s in range(2):
                    batch(2 * i + s, s, i)
            def counts(n):
                pe.wait_ge(S["r_sel"], n + 1)
                pe.matmul(ps[:, 6, 0:NT * NE], tri[:], selb16[:].rearrange("p t e -> p (t e)"), start=True, stop=True)
                pe.matmul(ps[:, 7, 0:NT * NE], ones[:], selb16[:].rearrange("p t e -> p (t e)"), start=True, stop=True
                          ).then_inc(S["r_pre"], 1)

            counts(0)
            pe.wait_ge(S["r_ok"], 1)
            pe.wait_ge(S["m_done"], NB)
            with pe.Fori(0, NTILE // 2) as i:
                es = []
                for s in range(2):
                    es.append(pe.value_load(ex_i[0:1, bass.ds(2 * i + s, 1)], min_val=0, max_val=NE - 1))
                    pe.wait_ge(S2["l_in"][s], 16 * i + 16)
                    pe.wait_ge(S2["l_xt"][s], i)
                    for k in range(KC):
                        m = pe.transpose(ps[:, s, k * P:(k + 1) * P], xs_in[s][:, k * P:(k + 1) * P], ident[:])
                    m.then_inc(S2["l_tx"][s], 1)
                for s in range(2):
                    pe.wait_ge(S2["l_xt"][s], i + 1)
                    pe.wait_ge(S2["l_ye"][s], i)
                    for k in range(KC):
                        m = pe.matmul(ps[:, 2 + s, :], xs_t[s][:, k, :], m_w[:, k, es[s], :],
                                      start=(k == 0), stop=(k == KC - 1))
                    m.then_inc(S2["l_mm"][s], 1)

            pe.wait_ge(S["w5"], 48)
            with pe.Fori(0, NT // 2) as i:
                for s in range(2):
                    pe.wait_ge(S2["c_x1"][s], i + 1)
                    pe.wait_ge(S2["c_t2e"][s], i)
                    for k in range(KC):
                        m = pe.transpose(ps[:, s, k * P:(k + 1) * P], x1[s][:, k * P:(k + 1) * P], ident[:])
                    m.then_inc(S2["c_tx"][s], 1)
                for s in range(2):
                    pe.wait_ge(S2["c_xt"][s], i + 1)
                    pe.wait_ge(S2["c_xe"][s], i)
                    for k in range(KC):
                        m = pe.matmul(ps[:, 2 + s, 0:P], lora_a[:, k, :], x1_t[s][:, k, :], start=(k == 0), stop=(k == KC - 1))
                    m.then_inc(S2["c_xa"][s], 1)
                    pe.wait_ge(S2["c_x2a"][s], i)
                    for k in range(KC):
                        pe.matmul(ps[:, 4 + s, :], x1_t[s][:, k, :], w1_t[:, k, :], start=(k == 0), stop=False)
                    pe.wait_ge(S2["c_xe"][s], i + 1)
                    pe.matmul(ps[:, 4 + s, :], xa_t[s], lora_b, start=False, stop=True).then_inc(S2["c_h"][s], 1)
                for s in range(2):
                    pe.wait_ge(S2["c_x2a"][s], i + 1)
                    for k in range(KC):
                        m = pe.transpose(ps[:, s, k * P:(k + 1) * P], x2[s][:, k * P:(k + 1) * P], ident[:])
                    m.then_inc(S2["c_t2"][s], 1)
                for s in range(2):
                    pe.wait_ge(S2["c_t2e"][s], i + 1)
                    pe.wait_ge(S2["c_lg"][s], i)
                    for k in range(KC):
                        m = pe.matmul(ps[:, 6 + s, 0:NE], x2_t[s][:, k, :], gate1[:, k, :], start=(k == 0), stop=(k == KC - 1))
                    m.then_inc(S2["c_g"][s], 1)
            for s in range(2):
                pe.wait_ge(S2["c_lg"][s], NT // 2)
            counts(1)
            pe.wait_ge(S["r_ok"], 2)
            pe.wait_ge(S["fc1_d"], 16 * KC)
            pe.wait_ge(S["fc2_d"], 16 * KC)
            with pe.Fori(0, NTILE // 2) as i:
                es = []
                for s in range(2):
                    es.append(pe.value_load(ex_i[0:1, bass.ds(2 * i + s, 1)], min_val=0, max_val=NE - 1))
                    pe.wait_ge(S2["k_in"][s], 16 * i + 16)
                    pe.wait_ge(S2["k_xt"][s], i)
                    for k in range(KC):
                        m = pe.transpose(ps[:, s, k * P:(k + 1) * P], xs_in[s][:, k * P:(k + 1) * P], ident[:])
                    m.then_inc(S2["k_tx"][s], 1)
                for s in range(2):
                    pe.wait_ge(S2["k_xt"][s], i + 1)
                    pe.wait_ge(S2["k_hb"][s], i)
                    for k in range(KC):
                        m = pe.matmul(ps[:, 2 + s, :], xs_t[s][:, k, :], fc1[:, k, es[s], :],
                                      start=(k == 0), stop=(k == KC - 1))
                    m.then_inc(S2["k_m1"][s], 1)
                for s in range(2):
                    pe.wait_ge(S2["k_hg"][s], i + 1)
                    pe.wait_ge(S2["k_ht"][s], i)
                    for k in range(KC):
                        m = pe.transpose(ps[:, 4 + s, k * P:(k + 1) * P], h_sb[s][:, k * P:(k + 1) * P], ident[:])
                    m.then_inc(S2["k_th"][s], 1)
                    pe.wait_ge(S2["k_ht"][s], i + 1)
                    pe.wait_ge(S2["k_ye"][s], i)
                    for k in range(KC):
                        m = pe.matmul(ps[:, 6 + s, :], h_t[s][:, k, :], fc2[:, k, es[s], :],
                                      start=(k == 0), stop=(k == KC - 1))
                    m.then_inc(S2["k_m2"][s], 1)

        @block.scalar
        def _(ac):
            ac.wait_ge(S["rope_in"], 1)
            ac.activation(sin_t.rearrange("p a b -> p (a b)"), ang.rearrange("p a b -> p (a b)"), ACT.Sin)
            ac.activation(cos_t.rearrange("p a b -> p (a b)"), ang2.rearrange("p a b -> p (a b)"), ACT.Sin
                          ).then_inc(S["rope_r"], 1)
            ac.wait_ge(S["eaw_e"], 1)
            ac.activation(eaw[:], eaw[:], ACT.Exp, bias=eaw_s[:, 0:1], accum_out=eaw_s[:, 1:2]).then_inc(S["imp_s"], 1)
            ac.activation(imp.rearrange("p a b -> p (a b)"), imp.rearrange("p a b -> p (a b)"), ACT.Sigmoid
                          ).then_inc(S["imp_s"], 1)
            ac.wait_ge(S["rope_ok"], 1)
            with ac.Fori(0, NT // 2) as i:
                for s in range(2):
                    ac.wait_ge(S2["qkv"][s], i + 1)
                    ac.wait_ge(S2["ssd"][s], i)
                    ac.activation(sq[s], ps[:, 2 * s:2 * s + 2, :].rearrange("p a b -> p (a b)")[:, 0:QK], ACT.Square)
                    ac.wait_ge(S2["p1w"][s], 32 * i)
                    ac.activation(qkv_out[s][:, QK:2 * D], ps[:, 2 * s + 1, QK - D:D], ACT.Copy).then_inc(S2["a1"][s], 1)
            def batch(B):
                ac.wait_ge(S["bk0"], 6 * B + 1)
                ac.activation(k_t[:, 0, :], ps[:, 0, :], ACT.Copy).then_inc(S["bc0"], 1)
                ac.wait_ge(S["bk1"], 6 * B + 1)
                ac.activation(k_t[:, 1, :], ps[:, 1, :], ACT.Copy).then_inc(S["bc1"], 1)

                def expo(u):
                    ac.wait_ge(S["s_mx"], 16 * B + u + 1)
                    ac.wait_ge(S["s_pt"], 16 * B + max(u - 2, 0))
                    ac.activation(prob[u % 3], msk_s[u % 2], ACT.Exp, bias=nmx[:, u:u + 1], scale=SCALE,
                                  accum_out=sums[:, u:u + 1]).then_inc(S["s_exp"], 1)

                def evac(u):
                    ac.wait_ge(S["s_pt"], 16 * B + u + 1)
                    ac.wait_ge(S["s_pv"], 16 * B + max(u - 2, 0))
                    ac.activation(prob_t[u % 3], ps[:, 4 + u % 2, 0:KW], ACT.Copy).then_inc(S["pea"], 1)

                def tail(qt, step):
                    n = 2 + 2 * qt + step
                    ac.wait_ge(S["bk0"], 6 * B + n + 1)
                    dst = o_t if step == 0 else a_t
                    ac.activation(dst.rearrange("p a b -> p (a b)"), ps[:, 0, :], ACT.Copy).then_inc(S["bc0"], 1)

                for st in range(18):
                    if st < 16:
                        expo(st)
                    if 0 <= st - 2 < 16 and (st - 2) % 2 == 1:
                        evac(st - 2)
                    if st in (11, 14):
                        tail(0, (11, 14).index(st))
                for step in range(2):
                    tail(1, step)

            ac.wait_ge(S2["p1o"][0], NT // 2)
            ac.wait_ge(S2["p1o"][1], NT // 2)
            for s in range(2):
                ac.wait_ge(S2["p1w"][s], 32 * (NT // 2))
            with ac.Fori(0, NB // 2) as i:
                for s in range(2):
                    batch(2 * i + s)
            ac.wait_ge(S["r_e"], 1)
            ac.activation(cw1[:], cw1[:], ACT.Exp).then_inc(S["r_exp"], 1)
            ac.wait_ge(S["xs_sc"], 32 * NT)
            with ac.Fori(0, NTILE // 2) as i:
                for s in range(2):
                    ac.wait_ge(S2["l_tx"][s], i + 1)
                    ac.wait_ge(S2["l_mm"][s], i)
                    ac.activation(xs_t[s].rearrange("p a b -> p (a b)"), ps[:, s, :], ACT.Copy).then_inc(S2["l_xt"][s], 1)
            for s in range(2):
                ac.wait_ge(S2["l_st"][s], 16 * (NTILE // 2))
            with ac.Fori(0, NT // 2) as i:
                for s in range(2):
                    ac.wait_ge(S2["c_tx"][s], i + 1)
                    ac.wait_ge(S2["c_h"][s], i)
                    ac.activation(x1_t[s].rearrange("p a b -> p (a b)"), ps[:, s, :], ACT.Copy).then_inc(S2["c_xt"][s], 1)
                for s in range(2):
                    ac.wait_ge(S2["c_x2a"][s], i + 1)
                    ac.activation(junk_a[:, s:s + 1], ones[:, 0:1], ACT.Copy)
                    ac.activation(x2_rows[:, 2 * i + s, :], x2[s], ACT.Copy).then_inc(S2["c_x2b"][s], 1)
                for s in range(2):
                    ac.wait_ge(S2["c_t2"][s], i + 1)
                    ac.wait_ge(S2["c_g"][s], i)
                    ac.activation(x2_t[s].rearrange("p a b -> p (a b)"), ps[:, s, :], ACT.Copy).then_inc(S2["c_t2e"][s], 1)
            ac.wait_ge(S["r_e"], 2)
            ac.activation(lg[:].rearrange("p a b -> p (a b)"), lg[:].rearrange("p a b -> p (a b)"), ACT.Exp
                          ).then_inc(S["r_exp"], 1)
            for s in range(2):
                ac.wait_ge(S2["c_st"][s], 16 * (NT // 2))
            with ac.Fori(0, NTILE // 2) as i:
                for s in range(2):
                    ac.wait_ge(S2["k_tx"][s], i + 1)
                    ac.wait_ge(S2["k_m1"][s], i)
                    ac.activation(xs_t[s].rearrange("p a b -> p (a b)"), ps[:, s, :], ACT.Copy).then_inc(S2["k_xt"][s], 1)
                for s in range(2):
                    ac.wait_ge(S2["k_hb"][s], i + 1)
                    ac.activation(h_sb[s], h_sb[s], ACT.Gelu).then_inc(S2["k_hg"][s], 1)
                for s in range(2):
                    ac.wait_ge(S2["k_th"][s], i + 1)
                    ac.wait_ge(S2["k_m2"][s], i)
                    ac.activation(h_t[s].rearrange("p a b -> p (a b)"), ps[:, 4 + s, :], ACT.Copy).then_inc(S2["k_ht"][s], 1)

        @block.vector
        def _(ve):
            TT, TS, CP = ve.tensor_tensor, ve.tensor_scalar, ve.tensor_copy

            def red(out, in_, op=ALU.max):
                return ve.tensor_reduce(out, in_, AX, op)

            ve.wait_ge(S["p0_dma"], 16 * 13)
            ve.wait_ge(S["iota"], 1)
            CP(iof[:, 0:33], iot[:, 0:33])
            CP(tile_io[:], tile_ii[:])
            CP(jrow[:], jrow_i)
            CP(lens[:], lens_i[:])
            TS(ints[:, 0:8], lens_i[:], 4, None, ALU.arith_shift_right)
            TS(ints[:, 8:16], lens_i[:], BLK - 1, None, ALU.bitwise_and)
            TS(ints[:, 16:17], iot[:, 32:33], 4, None, ALU.arith_shift_right)
            TS(ints[:, 17:18], iot[:, 32:33], BLK - 1, None, ALU.bitwise_and)
            CP(ms_f[:], ms_i[:])
            TS(cell_i[:], ms_i[:], D - 1, 9, ALU.bitwise_and, ALU.logical_shift_left)
            TS(cell_j[:], ms_i[:], 9, None, ALU.arith_shift_right)
            ve.drain()
            CP(first[:], ints[:, 0:8])
            CP(lo[:], ints[:, 8:16])
            CP(part[:, 0:1], iof[:, 32:33])
            CP(part[:, 1:3], ints[:, 16:18])
            TS(rev[:], iof[:, 0:NE], -1.0, float(NE), ALU.mult, ALU.add)
            TT(cell_i[:], cell_i[:], cell_j[:], ALU.bitwise_or)
            TT(eq_all, mask_bc.rearrange("p (s t) -> p t s", t=ST), ms_f[:].unsqueeze(2).broadcast_to([P, ST, P]),
               ALU.is_equal).then_inc(S["eqa"], 1)
            red(eaw_s[:, 2:3], eaw[:])
            ve.drain()
            TS(eaw_s[:, 0:1], eaw_s[:, 2:3], -1.0, None, ALU.mult).then_inc(S["eaw_e"], 1)
            TS(gains[:], gains[:], 1.0, None, ALU.add)
            for h in range(2):
                TS(pos[:, h:NT:2], lens[:], part[:, 0:1], float(P * h), ALU.add, ALU.add)
            ve.drain()
            TT(ang, pos[:].unsqueeze(2).broadcast_to([P, NT, HD // 2]), inv_f[:].unsqueeze(1).broadcast_to([P, NT, HD // 2]), ALU.mult)
            ve.drain()
            TS(ang2, ang, float(np.float32(1 / (2 * np.pi))), 12582912.0, ALU.mult, ALU.add)
            ve.drain()
            TS(ang2, ang2, 12582912.0, None, ALU.subtract)
            ve.drain()
            c1 = 6.28125
            c2 = float(np.float32(int((2 * np.pi - c1) * 2 ** 20) / 2 ** 20))
            c3 = float(np.float32(2 * np.pi - c1 - c2))
            for c in (c1, c2, c3):
                ve.scalar_tensor_tensor(ang, ang2, -c, ang, ALU.mult, ALU.add)
                ve.drain()
            TS(ang, ang, 3.1415925, -3.1415925, ALU.min, ALU.max)
            ve.drain()
            TS(ang2, ang, -1.0, None, ALU.mult)
            ve.drain()
            TT(ang2, ang2, ang, ALU.min)
            ve.drain()
            TS(ang2, ang2, float(np.float32(np.pi / 2)), None, ALU.add).then_inc(S["rope_in"], 1)
            for b in range(NB):
                s0 = ve.value_load(ints[0:1, b:b + 1], min_val=0, max_val=(SEQ - WIN + P) // BLK + 8)
                CP(win[:, b, :], table_bc[:, bass.ds(s0 + b * NBLK, SB)])
            TS(eqk[:, 0, 0:NE], iof[:, 0:NE], part[:, 1:2], None, ALU.is_equal)
            ve.drain()
            TT(eqk[:, 1, 0:NE], eqk[:, 0, 0:NE], scal_bc[:], ALU.mult)
            CP(sel_b[:], adapt_i[:])
            ve.drain()
            red(part[:, 3:4], eqk[:, 1, 0:NE], ALU.add)
            ve.drain()
            TS(sel_b[:], sel_b[:], part[:, 1:2], part[:, 3:4], ALU.is_equal, ALU.mult)
            TS(carry[:], lo[:], part[:, 2:3], float(BLK), ALU.add, ALU.is_ge)
            TS(off[:], lo[:], part[:, 2:3], None, ALU.add)
            ve.drain()
            ve.scalar_tensor_tensor(off[:], carry[:], -float(BLK), off[:], ALU.mult, ALU.add)
            TS(carry[:], carry[:], part[:, 1:2], None, ALU.add)
            ve.drain()
            TT(eqk, iof[:, 0:9].unsqueeze(1).broadcast_to([P, NB, 9]), carry[:].unsqueeze(2).broadcast_to([P, NB, 9]), ALU.is_equal)
            ve.drain()
            for c in range(NC):
                TT(tmp9, eqk, win[:, :, 8 * c:8 * c + 9], ALU.mult)
                ve.drain()
                red(blk[:, c, :], tmp9, ALU.add)
                ve.drain()
            TT(wr_tok, iof[:, 0:SW].unsqueeze(1).broadcast_to([P, NB, SW]), first[:].unsqueeze(2).broadcast_to([P, NB, SW]), ALU.add)
            ve.drain()
            TS(wr_tok, wr_tok, float(NBLK), None, ALU.is_lt)
            TS(wr_blk, win[:, :, SB - SW:SB], 1.0, None, ALU.add)
            ve.drain()
            TT(wr_blk, wr_blk, wr_tok, ALU.mult)
            ve.drain()
            TS(wr_blk, wr_blk, -1.0, None, ALU.add)
            TS(junk[:, 0:1], part[:, 0:1], 1.0, None, ALU.mult)
            TS(wr_tok, iof[:, 0:SW].unsqueeze(1).broadcast_to([P, NB, SW]), float(BLK), float(BLK), ALU.mult, ALU.add)
            ve.drain()
            TT(wr_tok, wr_tok, lo[:].unsqueeze(2).broadcast_to([P, NB, SW]), ALU.subtract)
            TS(ntf[0][:], iof[:, 0:NB], float(T), None, ALU.mult)
            ve.drain()
            TT(wr_tok, wr_tok, ntf[0][:].unsqueeze(2).broadcast_to([P, NB, SW]), ALU.add)
            TT(edge[:, 0], off[:].unsqueeze(2).broadcast_to([P, NB, NB]), lo[:].unsqueeze(1).broadcast_to([P, NB, NB]), ALU.is_ge)
            ve.drain()
            TS(edge[:, 1], edge[:, 0], -1.0, 1.0, ALU.mult, ALU.add)
            TT(hits, blk[:].rearrange("p c b -> p (c b)").unsqueeze(2).broadcast_to([P, NC * NB, NB * SW]),
               wr_blk.rearrange("p b s -> p (b s)").unsqueeze(1).broadcast_to([P, NC * NB, NB * SW]), ALU.is_equal)
            ve.drain()
            TT(hits, hits, wr_tok.rearrange("p b s -> p (b s)").unsqueeze(1).broadcast_to([P, NC * NB, NB * SW]), ALU.mult)
            ve.drain()
            hv = hits.rearrange("p (c b) (w s) -> p c b w s", c=NC, w=NB)
            for c in range(NC):
                for x, sl in ((0, 0), (1, SW - 1)):
                    TT(hv[:, c, :, :, sl], hv[:, c, :, :, sl], edge[:, x], ALU.mult)
            ve.drain()
            red(best[:].rearrange("p c b -> p (c b)"), hits)
            ve.drain()
            TS(found[:], best[:], 0.0, None, ALU.is_gt)
            ve.drain()
            TS(best[:], best[:], -float(BLK), None, ALU.add)
            ve.drain()
            TT(best[:], best[:], off[:].unsqueeze(1).broadcast_to([P, NC, NB]), ALU.add)
            ve.drain()
            TT(best[:], best[:], found[:], ALU.mult)
            ve.drain()
            TS(found[:, 0:2, :], found[:, 0:2, :], -float(4 * N), float(4 * N), ALU.mult, ALU.add)
            TS(fidx[:, 0:2], blk[:, 0:2], float(BLK), None, ALU.mult)
            ve.drain()
            TT(best[:, 0:2, :], best[:, 0:2, :], found[:, 0:2, :], ALU.add)
            TT(fidx[:, 0:2], fidx[:, 0:2], off[:].unsqueeze(1).broadcast_to([P, 2, NB]), ALU.add)
            ve.drain()
            CP(new_idx[:], best[:].rearrange("p c b -> p (c b)"))
            CP(old_idx[:], fidx[:, 0:2].rearrange("p c b -> p (c b)"))
            ve.drain().then_inc(S["p0_done"], 1)
            ve.wait_ge(S["imp_s"], 2)
            ve.reciprocal(eaw_s[:, 3:4], eaw_s[:, 1:2])
            ve.drain()
            TS(eaw[:], eaw[:], eaw_s[:, 3:4], None, ALU.mult).then_inc(S["w_eaw"], 1)
            ve.wait_ge(S["pe_eawt"], 1)
            CP(eaw_t[:], ps[0:64, 6, 0:NE]).then_inc(S["w_eawt"], 1)
            ve.wait_ge(S["pe_del"], 1)
            TT(wgt.rearrange("p a b -> p (a b)"), ps[:, 6, 0:ST * NE], imp.rearrange("p a b -> p (a b)"), ALU.mult
               ).then_inc(S["wgt_ok"], 1)
            ve.wait_ge(S["rope_r"], 1)
            hh = HD // 2
            for w in range(2):
                for h in range(2):
                    TT(tab_a[:, :, w, h * hh:(h + 1) * hh], cos_t, gains[:, w, h * hh:(h + 1) * hh].unsqueeze(1).broadcast_to([P, NT, hh]), ALU.mult)
                TT(tab_b[:, :, w, 0:hh], sin_t, gains[:, w, hh:HD].unsqueeze(1).broadcast_to([P, NT, hh]), ALU.mult)
                TT(tab_b[:, :, w, hh:HD], sin_t, gains[:, w, 0:hh].unsqueeze(1).broadcast_to([P, NT, hh]), ALU.mult)
            ve.drain()
            TS(tab_b[:, :, :, 0:hh], tab_b[:, :, :, 0:hh], -1.0, None, ALU.mult)
            ve.drain().then_inc(S["rope_ok"], 1)
            ve.wait_ge(S["eql"], 1)
            red(dup[:], eq_low)
            CP(cell_f[:], cell_i[:])
            ve.drain()
            TS(ms_f[:], cell_f[:], -1.0, float(CELLS), ALU.mult, ALU.add)
            ve.drain()
            TS(ms_f[:], ms_f[:], part[:, 0:1], None, ALU.add)
            ve.drain()
            TT(ms_f[:], ms_f[:], dup[:], ALU.mult)
            ve.drain()
            TT(cell_f[:], cell_f[:], ms_f[:], ALU.add)
            ve.drain()
            CP(cell_i[:], cell_f[:])
            ve.wait_ge(S["pe_tot"], 1)
            CP(tot[:].rearrange("p a b -> p (a b)"), ps[:, 7, 0:ST * NE])
            ve.drain().then_inc(S["cell_ok"], 1)
            ve.drain().then_inc(S["tot_ok"], 1)

            with ve.Fori(0, NT // 2) as i:
                for s in range(2):
                    ve.wait_ge(S2["a1"][s], i + 1)
                    red(ss[:, s, :], sq[s].rearrange("p (h d) -> p h d", d=HD), ALU.add)
                    ve.drain()
                    TS(ss[:, s, :], ss[:, s, :], 1.0 / HD, RMS_EPS, ALU.mult, ALU.add).then_inc(S2["ssd"][s], 1)
                for s in range(2):
                    t = 2 * i + s
                    ve.wait_ge(S2["rs"][s], i + 1)
                    TT(nrm.rearrange("p (h d) -> p h d", d=HD),
                       ps[:, 2 * s:2 * s + 2, :].rearrange("p a b -> p (a b)")[:, 0:QK].rearrange("p (h d) -> p h d", d=HD),
                       rstd[:, s, :].unsqueeze(2).broadcast_to([P, NQK, HD]), ALU.mult).then_inc(S2["p1p"][s], 1)
                    ve.drain()
                    nv = nrm.rearrange("p (h x d) -> p h x d", x=2, d=hh)
                    bv = rot_b.rearrange("p (h x d) -> p h x d", x=2, d=hh)
                    av = rot_a.rearrange("p (h d) -> p h d", d=HD)
                    for w, h0, h1 in ((0, 0, NH), (1, NH, NQK)):
                        TT(av[:, h0:h1], nrm.rearrange("p (h d) -> p h d", d=HD)[:, h0:h1],
                           tab_a[:, t, w, :].unsqueeze(1).broadcast_to([P, h1 - h0, HD]), ALU.mult)
                        for x in range(2):
                            TT(bv[:, h0:h1, x], nv[:, h0:h1, 1 - x],
                               tab_b[:, t, w, x * hh:(x + 1) * hh].unsqueeze(1).broadcast_to([P, h1 - h0, hh]), ALU.mult)
                    ve.drain()
                    TT(qkv_out[s][:, 0:QK], rot_a, rot_b, ALU.add).then_inc(S2["p1o"][s], 1)
                    ve.drain()
            def batch(B):
                TS(key_bias, jrow[:], lens[:, bass.ds(B, 1)], 0.0, ALU.add, ALU.is_ge)
                TS(mask[:].rearrange("p a b -> p (a b)")[:, 0:NJ] , jrow[:], lens[:, bass.ds(B, 1)], float(SEQ), ALU.add, ALU.is_lt)
                ve.drain()
                TT(key_bias, key_bias, mask[:].rearrange("p a b -> p (a b)")[:, 0:NJ], ALU.mult)
                ve.drain()
                TS(key_bias, key_bias, -1.0, BIG, ALU.add, ALU.mult)
                ve.drain()
                for qt in range(2):
                    TT(mask[:, qt, :], band[:], key_bias[:, qt * P:qt * P + KW], ALU.add)
                for qt in range(2):
                    ve.wait_ge(S["bk0" if qt == 0 else "bk1"], 6 * B + 2)
                    CP(q_t[:, :, qt * P:(qt + 1) * P], ps[:, qt, :].rearrange("p (a b) -> p a b", b=P)
                       ).then_inc(S["bc0" if qt == 0 else "bc1"], 1)
                ve.drain()

                def top(u):
                    ve.wait_ge(S["s_dot"], 16 * B + u + 1)
                    ve.memset(junk[:, 0:1], 0.0)
                    ve.wait_ge(S["s_exp"], 16 * B + max(u - 1, 0))
                    ve.memset(junk[:, 1:2], 0.0)
                    ve.tensor_tensor_reduce(out=msk_s[u % 2], in0=ps[:, 2 + u % 2, 0:KW], in1=mask[:, u // NH, :], scale=1.0,
                                            scalar=-3e38, op0=ALU.add, op1=ALU.max, accum_out=mx[:, u:u + 1])
                    ve.drain()
                    TS(nmx[:, u:u + 1], mx[:, u:u + 1], -SCALE, None, ALU.mult).then_inc(S["s_mx"], 1)

                def evac(u):
                    ve.wait_ge(S["s_pt"], 16 * B + u + 1)
                    ve.wait_ge(S["s_pv"], 16 * B + max(u - 2, 0))
                    CP(prob_t[u % 3], ps[:, 4 + u % 2, 0:KW]).then_inc(S["ped"], 1)

                def norm(qt):
                    ve.wait_ge(S["s_pv"], 16 * B + 8 * qt + 8)
                    ve.reciprocal(rsum[:], sums[:, 8 * qt:8 * qt + 8])
                    ve.drain()
                    TT(o_sb.rearrange("p (h d) -> p h d", d=HD), ps[:, 6 + qt, :].rearrange("p (h d) -> p h d", d=HD),
                       rsum[:].unsqueeze(2).broadcast_to([P, NH, HD]), ALU.mult).then_inc(S["s_norm"], 1)

                def row(qt):
                    ve.wait_ge(S["bk1"], 6 * B + 3 + 2 * qt)
                    ve.memset(junk[:, 2:3], 0.0)
                    ve.wait_ge(S["arow"], 2 * B + qt)
                    CP(a_row, ps[:, 1, :]).then_inc(S["bc1"], 1)

                def logit(qt):
                    ve.wait_ge(S["bk1"], 6 * B + 4 + 2 * qt)
                    TS(lg[:, 2 * B + qt, :], ps[:, 1, 0:NE], 50.0, -50.0, ALU.min, ALU.max).then_inc(S["bc1"], 1)

                for st in range(18):
                    if st < 16:
                        top(st)
                    if 0 <= st - 2 < 16 and st % 2 == 0:
                        evac(st - 2)
                    if st == 10:
                        norm(0)
                    if st == 13:
                        row(0)
                    if st == 15:
                        logit(0)
                norm(1)
                row(1)
                logit(1)
                ve.drain()

            with ve.Fori(0, NB // 2) as i:
                for s in range(2):
                    batch(2 * i + s)
            def b3(a):
                return a.unsqueeze(2).broadcast_to([P, NT, NE])

            def rb(a):
                return a.unsqueeze(1).broadcast_to([P, NT, NE])

            def step(ins):
                ve.drain()
                return ins

            def route(layer):
                if layer == 1:
                    red(m1[:], lg[:])
                    ve.drain()
                    step(TT(lg[:], lg[:], b3(m1[:]), ALU.subtract).then_inc(S["r_e"], 1))
                    ve.wait_ge(S["r_exp"], 2)
                    step(red(rr[:], lg[:], ALU.add))
                    step(ve.reciprocal(m2[:], rr[:]))
                    step(TT(lg[:], lg[:], b3(m2[:]), ALU.mult))
                src = lg
                for m, oh in ((m1, oh1), (m2, oh2)):
                    step(red(m[:], src[:]))
                    step(TT(t1[:], src[:], b3(m[:]), ALU.is_equal))
                    step(TT(t1[:], t1[:], rb(rev[:]), ALU.mult))
                    step(red(rr[:], t1[:]))
                    step(TT(oh[:], rb(rev[:]), b3(rr[:]), ALU.is_equal))
                    if oh is oh1:
                        step(ve.scalar_tensor_tensor(t2[:].rearrange("p a b -> p (a b)"), oh[:].rearrange("p a b -> p (a b)"), -BIG,
                                                     lg[:].rearrange("p a b -> p (a b)"), ALU.mult, ALU.add))
                        src = t2
                step(TT(selb16[:], oh1[:], oh2[:], ALU.add).then_inc(S["r_sel"], 1))
                if layer == 0:
                    step(TT(cw1[:], m2[:], m1[:], ALU.subtract).then_inc(S["r_e"], 1))
                    ve.wait_ge(S["r_exp"], 1)
                    step(TS(rr[:], cw1[:], 1.0, None, ALU.add))
                    step(ve.reciprocal(m1[:], rr[:]))
                    TT(cw2[:], cw1[:], m1[:], ALU.mult)
                    step(CP(m2[:], m1[:]))
                    step(CP(cw1[:], m2[:]))
                else:
                    step(TT(rr[:], m1[:], m2[:], ALU.add))
                    step(ve.reciprocal(cw1[:], rr[:]))
                    TT(cw2[:], cw1[:], m2[:], ALU.mult)
                    step(TT(rr[:], cw1[:], m1[:], ALU.mult))
                    step(CP(cw1[:], rr[:]))
                    for cw, oh in ((cw1, oh1), (cw2, oh2)):
                        step(TT(t1[:], oh[:], rb(alpha_bc[:]), ALU.mult))
                        step(red(rr[:], t1[:], ALU.add))
                        step(TT(cw[:], cw[:], rr[:], ALU.mult))
                ve.wait_ge(S["r_pre"], layer + 1)
                flat = "p a b -> p (a b)"
                CP(totl[:].rearrange(flat), ps[:, 7, 0:NT * NE])
                step(CP(cum[0][:].rearrange(flat), ps[:, 7, 0:NT * NE]))
                a, b = cum
                for sh in (1, 2, 4, 8):
                    TT(b[:, sh:, :], a[:, sh:, :], a[:, :NT - sh, :], ALU.add)
                    step(CP(b[:, :sh, :], a[:, :sh, :]))
                    a, b = b, a
                step(TS(ntf[0][:], a[:, NT - 1, :], float(P - 1), None, ALU.add))
                step(CP(nti[:], ntf[0][:]))
                step(TS(nti[:], nti[:], 7, None, ALU.arith_shift_right))
                CP(ntf[2][:], nti[:])
                step(CP(ntf[0][:], nti[:]))
                u, v = ntf[0], ntf[1]
                for sh in (1, 2, 4):
                    TT(v[:, sh:], u[:, sh:], u[:, :NE - sh], ALU.add)
                    step(CP(v[:, :sh], u[:, :sh]))
                    u, v = v, u
                step(TT(v[:], u[:], ntf[2][:], ALU.subtract))
                step(TT(ex_c[:], v[:, 1:NE].unsqueeze(1).broadcast_to([P, NTILE, NE - 1]),
                        tile_io[:].unsqueeze(2).broadcast_to([P, NTILE, NE - 1]), ALU.is_le))
                step(red(ex_f[:], ex_c[:], ALU.add))
                step(CP(ex_i[:], ex_f[:]))
                step(TS(u[:], v[:], float(P), None, ALU.mult))
                step(TT(t1[:], a[:], totl[:], ALU.subtract))
                step(TT(t2[:], t1[:], rb(u[:]), ALU.add))
                step(TT(t1[:].rearrange(flat), t2[:].rearrange(flat), ps[:, 6, 0:NT * NE], ALU.add))
                for c, oh in ((0, oh1), (1, oh2)):
                    step(TT(t2[:], t1[:], oh[:], ALU.mult))
                    step(red(slot_f[:, c, :], t2[:], ALU.add))
                CP(slot_i[:], slot_f[:])
                ve.drain().then_inc(S["r_ok"], 1)

            route(0)
            ve.wait_ge(S["xs_sc"], 32 * NT)
            with ve.Fori(0, NTILE // 2) as i:
                for s in range(2):
                    ve.wait_ge(S2["l_mm"][s], i + 1)
                    ve.wait_ge(S2["l_st"][s], 16 * i)
                    CP(y_sb[s], ps[:, 2 + s, :]).then_inc(S2["l_ye"][s], 1)
            for s in range(2):
                ve.wait_ge(S2["l_st"][s], 16 * (NTILE // 2))

            def add_two(t, s, i, y_ready):
                ve.wait_ge(y_ready[s], 32 * i + 32)
                ve.scalar_tensor_tensor(x1[s], y1[s], cw1[:, bass.ds(t, 1)], x_row[s], ALU.mult, ALU.add)
                ve.drain()
                return ve.scalar_tensor_tensor(x1[s], y2[s], cw2[:, bass.ds(t, 1)], x1[s], ALU.mult, ALU.add)

            with ve.Fori(0, NT // 2) as i:
                for s in range(2):
                    ve.wait_ge(S2["c_in"][s], 16 * i + 16)
                    ve.memset(junk[:, 0:1], 0.0)
                    ve.wait_ge(S2["c_st"][s], 16 * i)
                    ve.memset(junk[:, 1:2], 0.0)
                    add_two(2 * i + s, s, i, S2["ga_y"]).then_inc(S2["c_x1"][s], 1)
                for s in range(2):
                    ve.wait_ge(S2["c_xa"][s], i + 1)
                    TS(xa_t[s], ps[:, 2 + s, 0:P], sel_b[:, bass.ds(i, 1)], None, ALU.mult).then_inc(S2["c_xe"][s], 1)
                for s in range(2):
                    ve.wait_ge(S2["c_h"][s], i + 1)
                    ve.wait_ge(S2["c_x2b"][s], i)
                    CP(x2[s], ps[:, 4 + s, :]).then_inc(S2["c_x2a"][s], 1)
                for s in range(2):
                    ve.wait_ge(S2["c_g"][s], i + 1)
                    TS(lg[:, 2 * i + s, :], ps[:, 6 + s, 0:NE], 1.0, None, ALU.mult).then_inc(S2["c_lg"][s], 1)
            ve.drain()
            route(1)
            ve.wait_ge(S["b_dma"], 32)
            for s in range(2):
                ve.wait_ge(S2["c_st"][s], 16 * (NT // 2))
            with ve.Fori(0, NTILE // 2) as i:
                es = []
                for s in range(2):
                    es.append(ve.value_load(ex_i[0:1, bass.ds(2 * i + s, 1)], min_val=0, max_val=NE - 1))
                for s in range(2):
                    ve.wait_ge(S2["k_m1"][s], i + 1)
                    TT(h_sb[s], ps[:, 2 + s, :], b1_bc[:, es[s], :], ALU.add).then_inc(S2["k_hb"][s], 1)
                for s in range(2):
                    ve.wait_ge(S2["k_m2"][s], i + 1)
                    ve.wait_ge(S2["k_st"][s], 16 * i)
                    TT(y_sb[s], ps[:, 6 + s, :], b2_bc[:, es[s], :], ALU.add).then_inc(S2["k_ye"][s], 1)
            for s in range(2):
                ve.wait_ge(S2["k_st"][s], 16 * (NTILE // 2))
            with ve.Fori(0, NT // 2) as i:
                for s in range(2):
                    ve.wait_ge(S2["f_in"][s], 16 * i + 16)
                    ve.memset(junk[:, 0:1], 0.0)
                    ve.wait_ge(S2["f_st"][s], 16 * i)
                    ve.memset(junk[:, 1:2], 0.0)
                    add_two(2 * i + s, s, i, S2["fin_y"]).then_inc(S2["f_o"][s], 1)


def kernel(**inputs):
    import concourse.bacc as bacc
    from concourse.bass_utils import run_bass_kernel_spmd

    a = {k: np.asarray(v) for k, v in inputs.items()}
    t = np.ascontiguousarray
    x = a["x"].reshape(N, D)
    half = HD // 2
    wq = a["L0_cond_Wq"].reshape(2, 2, 2, HD, D).transpose(0, 2, 1, 3, 4).reshape(NH * HD, D)
    ins = {
        "x": x,
        "x_t": x.T,
        "wqkv_t": np.concatenate([wq, a["L0_cond_Wk"], a["L0_cond_Wv"]], 0).T,
        "wo_t": a["L0_cond_Wo"].T,
        "w0_t": a["L0_ffn_W"].T,
        "kv_pool": np.stack([a["L0_cond_k_blocks"].transpose(0, 2, 1, 3), a["L0_cond_v_blocks"].transpose(0, 2, 1, 3)],
                            2).reshape(NPHYS * BLK, 2 * NG * HD),
        "table": a["itok_Bx257_0_4111"].reshape(-1),
        "lens": a["itok_B_37_3939"],
        "adapter": a["itok_B_0_6"],
        "q_gain": a["L0_cond_q_norm_scale"],
        "k_gain": a["L0_cond_k_norm_scale"],
        "inv_freq": (1.0 / THETA ** (np.arange(half) / half)).astype(np.float32),
        "gate0_t": a["L0_ffn_gate_w"].T,
        "atoms": a["L0_ffn_atoms"],
        "eaw": a["L0_ffn_expert_atom_weights"],
        "imp_t": a["L0_ffn_importance"].T,
        "mask_idx": a["L0_ffn_mask_idx"],
        "w1_t": a["L1_cond_W"].T,
        "a_t": a["L1_cond_A"].reshape(NE * RANK, D).T,
        "b_t": a["L1_cond_Bm"].transpose(0, 2, 1).reshape(NE * RANK, D),
        "scal": a["L1_cond_scalings"],
        "gate1": a["L1_ffn_gate_w"],
        "fc1": a["L1_ffn_fc1_w"],
        "b1": a["L1_ffn_fc1_b"].reshape(-1),
        "fc2": a["L1_ffn_fc2_w"],
        "b2": a["L1_ffn_fc2_b"].reshape(-1),
        "alpha": a["L1_ffn_alpha"],
    }
    nc = bacc.Bacc("TRN2", target_bir_lowering=False, num_devices=1)
    arrays, d = {}, {}
    for name, v in ins.items():
        v = t(v)
        arrays["in_" + name] = v
        d[name] = nc.dram_tensor("in_" + name, v.shape, mybir.dt.from_np(v.dtype), kind="ExternalInput").ap()
    for name, shape in (("new_kv", [N, D]), ("qn", [N, D]), ("m_buf", [CELLS + P, NE]), ("xs", [NTILE * P, D]),
                        ("ys", [NTILE * P, D]), ("x1", [N, D])):
        d[name] = nc.dram_tensor(name, shape, F32, kind="Internal").ap()
    d["out"] = nc.dram_tensor("out_x", [N, D], F32, kind="ExternalOutput").ap()
    program(nc, d)
    r = run_bass_kernel_spmd(nc, [arrays], core_ids=[0])
    return r.results[0]["out_x"].reshape(NB, T, D)
```

```python
import numpy as np

import concourse.bass as bass
from concourse import mybir
from contextlib import ExitStack

F32 = mybir.dt.float32
BF16 = mybir.dt.bfloat16
I32 = mybir.dt.int32
ALU = mybir.AluOpType
ACT = mybir.ActivationFunctionType
AX = mybir.AxisListType.X

P = 128
NB, T, D = 8, 256, 512
N = NB * T
NT = N // P
KC = D // P
NH, NG, HD = 8, 4, 64
BLK, NBLK = 16, 257
NPHYS = 16 * NBLK
SEQ = BLK * NBLK
WIN = 256
NJ = 2 * WIN
NC = NJ // P
KW = WIN + P
SB = NJ // BLK + 1
SW = T // BLK + 1
SCALE = 256.0 ** -0.5
RMS_EPS = 1e-6
THETA = 10000.0
NE = 8
NS = 4096
ST = NS // P
NTILE = 2 * N // P + NE
ROWS = (NE - 1) * N + NTILE * P
CELLS = D * D
RANK = 16
BIG = 1e30
NQK = NH + NG
QK = NQK * HD
HEADS = (0, 2, 1, 3, 4, 6, 5, 7)


def words(region, off, dims, dt=F32, parts=P):
    n = int(np.prod(dims))
    a = region[0:parts, off:off + n]
    if dt != F32:
        a = a.bitcast(dt)
    if len(dims) == 1:
        return a
    names = "abcd"[:len(dims)]
    return a.rearrange(f"p ({' '.join(names)}) -> p {' '.join(names)}",
                       **{c: int(d) for c, d in zip(names[1:], dims[1:])})


def program(nc, d):
    ctx = ExitStack()
    with ctx:
        def sb(name, shape, dt=F32):
            return ctx.enter_context(nc.sbuf_tensor(name, shape, dt))

        def sem(name):
            return ctx.enter_context(nc.semaphore(name))

        def sem2(name):
            return [sem(name + "_0"), sem(name + "_1")]

        R1 = sb("R1", [P, 16384])
        R2 = sb("R2", [P, 16384])
        R3 = sb("R3", [P, 8192])
        R4 = sb("R4", [P, 8192])
        zero = words(R1, 0, [2048])
        mask_bc = words(R1, 2048, [NS], I32)
        eq_low = words(R1, 2048, [ST, P])
        eq_all = words(R1, 6144, [ST, P])
        atoms = words(R1, 10240, [NS], F32, 64)
        imp = words(R1, 14336, [ST, NE])
        wgt = words(R1, 14592, [ST, NE])
        table_bc = words(R3, 0, [BLK + NB * NBLK + 24], I32)
        hits = words(R3, 2112, [NC * NB, NB * SW])
        jrow_i = words(R3, 6500, [NJ], I32)
        win = words(R3, 7012, [NB, SB])
        eqk = words(R3, 7276, [NB, 9])
        tmp9 = words(R3, 7348, [NB, 9])
        wr_blk = words(R3, 7420, [NB, SW])
        wr_tok = words(R3, 7556, [NB, SW])
        raw_wo = words(R4, 0, [KC, D])
        raw_w1 = words(R4, 2048, [KC, D])
        raw_b = words(R4, 4096, [KC, P])
        wqkv = words(R2, 0, [KC, 2 * D])
        tab_a = words(R2, 4096, [NT, 2, HD])
        tab_b = words(R2, 6144, [NT, 2, HD])
        xt = [words(R2, 8192 + 512 * s, [KC, P]) for s in range(2)] + [words(R1, 14848 + 512 * s, [KC, P]) for s in range(2)]
        sq = [words(R2, 9216, [QK]), words(R2, 14336, [QK])]
        nrm = words(R2, 9984, [QK])
        rot_a = words(R2, 10752, [QK])
        rot_b = words(R2, 11520, [QK])
        qkv_out = [words(R2, 12288 + 1024 * s, [2 * D]) for s in range(2)]
        ang = words(R2, 14336, [NT, HD // 2])
        ang2 = words(R2, 14848, [NT, HD // 2])
        sin_t = words(R2, 15360, [NT, HD // 2])
        cos_t = words(R2, 15872, [NT, HD // 2])
        k_t = [words(R2, 1024 * s, [2, NJ]) for s in range(2)]
        q_in = words(R2, 2048, [2, D])
        q_t = [words(R2, 3072 + 1024 * s, [4, T]) for s in range(2)]
        msk_s = [words(R2, 5120 + KW * s, [KW]) for s in range(2)]
        prob = [words(R2, 5888 + KW * s, [KW]) for s in range(4)]
        prob_t = [words(R2, 7424 + KW * s, [KW]) for s in range(4)]
        mask = words(R2, 8960, [2, KW])
        key_bias = words(R2, 9728, [2, KW])
        o_sb = words(R2, 10496, [D])
        o_t = words(R2, 11008, [KC, P])
        stage = words(R2, 11520, [2048])
        w_o = words(R4, 0, [KC, D])
        w0_t = words(R4, 2048, [KC, D])
        kv = [words(R4, 4096 + 2048 * s, [NC, D]) for s in range(2)]
        m_w = words(R1, 0, [KC, NE, D])
        a_rows = words(R3, 0, [NT, D])
        xs_in = [words(R3, 512 * s, [D]) for s in range(2)]
        xs_t = [words(R3, 1024 + 512 * s, [KC, P]) for s in range(2)]
        h_sb = [words(R3, 2048 + 512 * s, [D]) for s in range(2)]
        h_t = [words(R3, 3072 + 512 * s, [KC, P]) for s in range(2)]
        y_sb = [words(R3, 4096 + 512 * s, [D]) for s in range(2)]
        fc1 = words(R2, 0, [KC, NE, D])
        fc2 = words(R1, 0, [KC, NE, D])
        b1_bc = words(R4, 0, [NE, D])
        b2_bc = words(R4, 4096, [NE, D])
        x_row = [words(R3, 512 * s, [D]) for s in range(2)]
        y1 = [words(R3, 1024 + 512 * s, [D]) for s in range(2)]
        y2 = [words(R3, 2048 + 512 * s, [D]) for s in range(2)]
        x1 = [words(R3, 3072 + 512 * s, [D]) for s in range(2)]
        x1_t = [words(R3, 4096 + 512 * s, [KC, P]) for s in range(2)]
        xa_t = [words(R3, 5120 + 128 * s, [P]) for s in range(2)]
        w1_t = words(R3, 5376, [KC, D])
        lora_a = words(R3, 7424, [KC, P])
        lora_b = sb("lora_b", [P, D])
        x2_rows = words(R4, 0, [NT, D])

        ident = sb("ident", [P, P])
        tri = sb("tri", [P, P], BF16)
        ones = sb("ones", [P, P], BF16)
        low = sb("low", [P, P])
        band = sb("band", [P, KW], BF16)
        jrow = sb("jrow", [P, NJ], BF16)
        gate0 = sb("gate0", [P, KC, NE])
        gate1 = sb("gate1", [P, KC, NE])
        wo_g = sb("wo_g", [P, KC, NE])
        w1_g = sb("w1_g", [P, KC, NE])
        b_g = sb("b_g", [P, NE])
        lens_i = sb("lens_i", [P, NB], I32)
        ints = sb("ints", [P, 64], I32)
        lens = sb("lens", [P, NB])
        lo = sb("lo", [P, NB])
        first = sb("first", [P, NB])
        adapt_i = sb("adapt_i", [P, NB], I32)
        scal_bc = sb("scal_bc", [P, NE])
        alpha_bc = sb("alpha_bc", [P, NE])
        part = sb("part", [P, 4])
        iot = sb("iot", [P, 64], I32)
        iof = sb("iof", [P, 64])
        rev = sb("rev", [P, NE])
        sel_b = sb("sel_b", [P, NB])
        gains = sb("gains", [P, 2, HD])
        inv_f = sb("inv_f", [P, HD // 2])
        pos = sb("pos", [P, NT])
        carry = sb("carry", [P, NB])
        off = sb("off", [P, NB])
        blk = sb("blk", [P, NC, NB])
        edge = sb("edge", [P, 2, NB, NB])
        best = sb("best", [P, NC, NB])
        fidx = sb("fidx", [P, NC, NB])
        found = sb("found", [P, NC, NB])
        old_idx = sb("old_idx", [P, 2 * NB], I32)
        new_idx = sb("new_idx", [P, NC * NB], I32)
        ms_i = sb("ms_i", [P, ST], I32)
        ms_f = sb("ms_f", [P, ST])
        cell_i = sb("cell_i", [P, ST], I32)
        cell_j = sb("cell_j", [P, ST], I32)
        cell_f = sb("cell_f", [P, ST])
        dup = sb("dup", [P, ST])
        eaw = sb("eaw", [NE, 64])
        eaw_s = sb("eaw_s", [NE, 4])
        eaw_t = sb("eaw_t", [64, NE])
        tot = sb("tot", [P, ST, NE])
        ss = sb("ss", [P, 2, NQK])
        rstd = sb("rstd", [P, 2, NQK])
        root = sb("root", [P, 2, NQK])
        mx = sb("mx", [P, 16])
        nmx = sb("nmx", [P, 16])
        sums = sb("sums", [P, 16])
        rsum = sb("rsum", [P, NH])
        junk = sb("junk", [P, 8])
        junk_a = sb("junk_a", [P, 4])
        lg = sb("lg", [P, 2, NE])
        t1 = sb("t1", [P, 2, NE])
        t2 = sb("t2", [P, 2, NE])
        oh1 = sb("oh1", [P, 2, NE])
        oh2 = sb("oh2", [P, 2, NE])
        rr = sb("rr", [P, 2])
        rs2 = sb("rs2", [P, 2])
        m1 = sb("m1", [P, NT])
        m2 = sb("m2", [P, NT])
        al1 = sb("al1", [P, NT])
        al2 = sb("al2", [P, NT])
        cw1 = sb("cw1", [P, NT])
        cw2 = sb("cw2", [P, NT])
        cwt = sb("cwt", [P, NT])
        selb16 = sb("selb16", [P, 2, NE], BF16)
        run = sb("run", [P, NE])
        region0 = sb("region0", [P, NE])
        nti = sb("nti", [P, NE], I32)
        ntf = [sb(f"ntf{i}", [P, NE]) for i in range(4)]
        slot_f = sb("slot_f", [P, 2, 2])
        slot_i = sb("slot_i", [P, 2, NT], I32)
        slot_y = sb("slot_y", [P, 2, NT], I32)
        ex_c = sb("ex_c", [P, NTILE, NE - 1])
        rg = sb("rg", [P, 2 * NT])
        ex_f = sb("ex_f", [P, NTILE])
        ex_i = sb("ex_i", [P, NTILE], I32)
        row_i = sb("row_i", [P, NTILE], I32)
        tile_io = sb("tile_io", [P, NTILE])
        tile_ii = sb("tile_ii", [P, NTILE], I32)

        ps = ctx.enter_context(nc.psum_tensor("ps", [P, 8, 512], F32))

        def bank(b, dims=None):
            a = ps[:, b, :]
            if dims is None:
                return a
            n = int(np.prod(dims))
            a = ps[:, b, 0:n]
            if len(dims) == 1:
                return a
            return a.rearrange("p (a b) -> p a b", b=int(dims[-1]))

        S = {}
        for name in ("p0_dma w_qkv raw_dma consts zero_ok eqa eql rope_in rope_r rope_ok idx_ok eaw_in imp_s eaw_ok eaw_p eaw_c "
                     "delta wgt_ok tot_p cell_ok pre_w pre_c zdone zrows mscat "
                     "s_dot s_mx s_exp s_pt s_pe s_pv s_norm mstage m_done att_w q_ld "
                     "r_sel r_slot r_ok r_e r_exp r_l r_lexp xs_sc w5 b1_d b2_d fc1_d fc2_d c_rt c_rtc outs").split():
            S[name] = sem(name)
        S2 = {}
        for name in ("bk bc ssd rec root p1o p1w kvd kvc "
                     "l_in l_tx l_xt l_mm l_ye l_st k_in k_tx k_xt k_m1 k_hb k_hg k_th k_ht k_m2 k_ye k_st "
                     "c_in c_x1 c_tx c_xt c_xa c_xe c_h c_x2 c_g c_lg c_st ga_y fin_y f_in f_o f_st").split():
            S2[name] = sem2(name)
        S4 = {name: [sem(f"{name}_{i}") for i in range(4)] for name in ("x_in", "qkv", "a1", "p1p")}

        def wait(eng, semaphore, value):
            if not isinstance(value, int) or value > 0:
                eng.wait_ge(semaphore, value)

        ORDER = (("o1", 0), ("a1", 1), ("g1", 0), ("q0", 0), ("q1", 1), ("rt", 0), ("k0", 0), ("k1", 1),
                 ("o0", 0), ("a0", 1), ("g0", 0))
        KINDS = {"first": ("q0", "q1", "k0", "k1", "o0", "a0", "g0"),
                 "mid": tuple(x for x, _ in ORDER),
                 "last": ("o1", "a1", "g1", "rt", "o0", "a0", "g0"),
                 "after": ("o1", "a1", "g1", "rt")}

        def uses(B, kind):
            base = {"first": (2, 2), "mid": (7 * B - 1, 4 * B + 1), "last": (7 * B - 1, 4 * B + 1),
                    "after": (7 * NB - 3, 4 * NB - 1)}[kind]
            n, out = [0, 0], {}
            for x, bk in ORDER:
                if x in KINDS[kind]:
                    out[x] = (bk, base[bk] + n[bk])
                    n[bk] += 1
            return out

        def periods(eng, period):
            period(0, "first", 0, 0)
            with eng.Fori(0, NB // 2 - 1) as i:
                period(2 * i + 1, "mid", 1, i)
                period(2 * i + 2, "mid", 0, i)
            period(NB - 1, "last", 1, 0)

        block = ctx.enter_context(nc.Block())

        @block.sync
        def _(sp):
            for dst, src in (
                    (lens_i[:], d["lens"].partition_broadcast(P)),
                    (table_bc[:, BLK:BLK + NB * NBLK], d["table"].partition_broadcast(P)),
                    (inv_f[:], d["inv_freq"].partition_broadcast(P)),
                    (gains[:, 0, :], d["q_gain"].partition_broadcast(P)),
                    (gains[:, 1, :], d["k_gain"].partition_broadcast(P)),
                    (adapt_i[:], d["adapter"].partition_broadcast(P)),
                    (scal_bc[:], d["scal"].partition_broadcast(P)),
                    (alpha_bc[:], d["alpha"].partition_broadcast(P)),
                    (ms_i[:], d["mask_idx"].rearrange("(p t) -> p t", t=ST)),
                    (eaw[:], d["eaw"]),
                    (imp, d["imp_t"].rearrange("(p t) e -> p t e", t=ST)),
                    (mask_bc, d["mask_idx"].partition_broadcast(P)),
                    (atoms, d["atoms"])):
                sp.dma_start(dst, src).then_inc(S["p0_dma"], 16)
            chunked = "(k p) n -> p k n"
            xt_v = d["x_t"].rearrange("(k p) (t m) -> p k t m", p=P, m=P)
            qn_v = d["qn"].rearrange("(t p) n -> p t n", p=P)
            np_v = d["new_kv"].rearrange("(t p) n -> p t n", p=P)

            def load_x(t, s):
                sp.dma_start(xt[s], xt_v[:, :, t, :]).then_inc(S4["x_in"][s], 16)

            def store_qkv(t, s):
                sp.dma_start(np_v[:, t, :], qkv_out[s][:, D:2 * D]).then_inc(S2["p1w"][s], 16)
                sp.dma_start(qn_v[:, t, :], qkv_out[s][:, 0:D]).then_inc(S2["p1w"][s], 16)

            sp.wait_ge(S["zero_ok"], 1)
            mb = d["m_buf"][0:CELLS, :].rearrange("(p a) e -> p (a e)", p=P)
            for i in range(8):
                sp.dma_start(mb[:, 2048 * i:2048 * (i + 1)], zero).then_inc(S["zdone"], 16)
            sp.dma_start(d["m_buf"][CELLS:CELLS + P, :], zero[:, 0:NE]).then_inc(S["zdone"], 16)
            xz = d["xs"][0:NE * N, :].rearrange("(e b p a) n -> p b e (a n)", e=NE, b=NB, p=P)

            def zero_rows(b):
                sp.dma_start(xz[:, b], zero[:, 0:2 * D].unsqueeze(1).broadcast_to([P, NE, 2 * D])).then_inc(S["zrows"], 16)

            zero_rows(0)
            with sp.Fori(0, NT // 4 - 1) as i:
                for s in range(4):
                    sp.wait_ge(S4["qkv"][s], i + 1)
                    load_x(4 * i + 4 + s, s)
                    sp.wait_ge(S2["p1o"][s % 2], 2 * i + s // 2 + 1)
                    store_qkv(4 * i + s, s % 2)
            for s in range(4):
                sp.wait_ge(S2["p1o"][s % 2], NT // 2 - 1 + s // 2)
                store_qkv(NT - 4 + s, s % 2)

            sp.wait_ge(S["pre_w"], 1)
            sp.dma_start(w_o, d["wo_t"].rearrange(chunked, p=P)).then_inc(S["att_w"], 16)
            sp.dma_start(w0_t, d["w0_t"].rearrange(chunked, p=P)).then_inc(S["att_w"], 16)
            for s in range(2):
                sp.wait_ge(S2["p1w"][s], 32 * (NT // 2))
            qb_v = d["qn"].rearrange("(b t p) n -> p b t n", t=2, p=P)
            sp.dma_start(q_in, qb_v[:, 0, :, :]).then_inc(S["q_ld"], 16)
            sp.wait_ge(S2["bk"][1], 2)
            sp.dma_start(q_in, qb_v[:, 1, :, :]).then_inc(S["q_ld"], 16)
            zero_rows(1)
            with sp.Fori(0, NB - 2) as b:
                sp.wait_ge(S2["bk"][1], 4 * b + 3)
                sp.dma_start(q_in, qb_v[:, b + 2, :, :]).then_inc(S["q_ld"], 16)
                zero_rows(b + 2)
            sp.dma_start(d["xs"][NE * N:ROWS, :].rearrange("(p a) n -> p (a n)", p=P),
                         zero[:, 0:D].unsqueeze(1).broadcast_to([P, (ROWS - NE * N) // P, D])
                         ).then_inc(S["zrows"], 16)
            ys_v = d["ys"].rearrange("(t p) n -> p t n", p=P)

            def expert_io(load, read, made, stored):
                def fetch(t, s):
                    row = sp.value_load(row_i[0:1, bass.ds(t, 1)], min_val=0, max_val=ROWS - P)
                    sp.dma_start(xs_in[s], d["xs"][bass.ds(row, P), :]).then_inc(load[s], 16)

                def put(t, s):
                    sp.dma_start(ys_v[:, t, :], y_sb[s]).then_inc(stored[s], 16)
                for s in range(2):
                    fetch(s, s)
                yield
                with sp.Fori(0, NTILE // 2 - 1) as i:
                    for s in range(2):
                        sp.wait_ge(read[s], i + 1)
                        fetch(2 * i + 2 + s, s)
                    for s in range(2):
                        sp.wait_ge(made[s], i + 1)
                        put(2 * i + s, s)
                for s in range(2):
                    sp.wait_ge(made[s], NTILE // 2)
                    put(NTILE - 2 + s, s)

            sp.wait_ge(S["r_ok"], 1)
            sp.wait_ge(S["xs_sc"], 32 * NT)
            sp.wait_ge(S["zrows"], 16 * (NB + 1))
            io = expert_io(S2["l_in"], S2["l_tx"], S2["l_ye"], S2["l_st"])
            next(io)
            sp.wait_ge(S["m_done"], 2 * KC)
            fc1_v = d["fc1"].rearrange("e (k p) n -> p k e n", p=P)
            for k in range(KC):
                sp.dma_start(fc1[:, k], fc1_v[:, k]).then_inc(S["fc1_d"], 16)
            sp.dma_start(w1_t, d["w1_t"].rearrange(chunked, p=P)).then_inc(S["w5"], 16)
            sp.dma_start(lora_a, d["a_t"].rearrange(chunked, p=P)).then_inc(S["w5"], 16)
            sp.dma_start(lora_b[:], d["b_t"]).then_inc(S["w5"], 16)
            for _ in io:
                pass

            x_v = d["x"].rearrange("(t p) n -> p t n", p=P)
            x1_v = d["x1"].rearrange("(t p) n -> p t n", p=P)
            for s in range(2):
                sp.wait_ge(S2["l_st"][s], 16 * (NTILE // 2))
            for s in range(2):
                sp.dma_start(x_row[s], x_v[:, s, :]).then_inc(S2["c_in"][s], 16)
            fc2_v = d["fc2"].rearrange("e (k p) n -> p k e n", p=P)

            def x_io(c0, c1):
                with sp.Fori(c0, c1) as i:
                    for s in range(2):
                        sp.wait_ge(S2["c_x1"][s], i + 1)
                        sp.dma_start(x_row[s], x_v[:, 2 * i + 2 + s, :]).then_inc(S2["c_in"][s], 16)
                        sp.dma_start(x1_v[:, 2 * i + s, :], x1[s]).then_inc(S2["c_st"][s], 16)

            for k in range(KC):
                sp.dma_start(fc2[:, k], fc2_v[:, k]).then_inc(S["fc2_d"], 16)
            x_io(0, 6)
            sp.wait_ge(S["xs_sc"], 32 * NT + 16 * NT)
            sp.dma_start(b1_bc, d["b1"].partition_broadcast(P)).then_inc(S["b1_d"], 16)
            x_io(6, NT // 2 - 1)
            for s in range(2):
                sp.wait_ge(S2["c_x1"][s], NT // 2)
                sp.dma_start(x1_v[:, NT - 2 + s, :], x1[s]).then_inc(S2["c_st"][s], 16)
            sp.wait_ge(S["r_ok"], 2)
            sp.wait_ge(S["xs_sc"], 64 * NT)
            for s in range(2):
                sp.wait_ge(S2["c_tx"][s], NT // 2)
            io = expert_io(S2["k_in"], S2["k_tx"], S2["k_ye"], S2["k_st"])
            next(io)
            sp.dma_start(b2_bc, d["b2"].partition_broadcast(P)).then_inc(S["b2_d"], 16)
            for _ in io:
                pass

            out_v = d["out"].rearrange("(t p) n -> p t n", p=P)
            for s in range(2):
                sp.wait_ge(S2["c_st"][s], 16 * (NT // 2))
                sp.wait_ge(S2["k_tx"][s], NTILE // 2)
            for s in range(2):
                sp.dma_start(x_row[s], x1_v[:, s, :]).then_inc(S2["f_in"][s], 16)
            with sp.Fori(0, NT // 2 - 1) as i:
                for s in range(2):
                    sp.wait_ge(S2["f_o"][s], i + 1)
                    sp.dma_start(x_row[s], x1_v[:, 2 * i + 2 + s, :]).then_inc(S2["f_in"][s], 16)
                    sp.dma_start(out_v[:, 2 * i + s, :], x1[s]).then_inc(S2["f_st"][s], 16)
            for s in range(2):
                sp.wait_ge(S2["f_o"][s], NT // 2)
                sp.dma_start(out_v[:, NT - 2 + s, :], x1[s]).then_inc(S2["f_st"][s], 16)
            for s in range(2):
                sp.wait_ge(S2["f_st"][s], 16 * (NT // 2))

        @block.gpsimd
        def _(po):
            po.iota(iot[:, 0:32], [[1, 32]], base=0, channel_multiplier=0)
            po.iota(iot[:, 32:33], [[0, 1]], base=0, channel_multiplier=1)
            po.iota(tile_ii[:], [[1, NTILE]], base=0, channel_multiplier=0)
            po.iota(jrow_i, [[1, NJ]], base=-WIN, channel_multiplier=0)
            po.memset(ident[:], 0.0)
            po.memset(table_bc[:, 0:BLK], 0)
            po.memset(table_bc[:, BLK + NB * NBLK:], 0)
            po.drain()
            po.affine_select(out=ident[:], in_=ident[:], compare_op=ALU.not_equal, fill=1.0, base=0,
                             pattern=[[-1, P]], channel_multiplier=1)
            po.drain().then_inc(S["consts"], 1)
            po.memset(zero, 0.0)
            po.drain().then_inc(S["zero_ok"], 1)
            po.memset(tri[:], 1.0)
            po.memset(ones[:], 1.0)
            po.memset(low[:], 1.0)
            po.memset(band[:], 0.0)
            po.drain()
            po.affine_select(out=tri[:], in_=tri[:], compare_op=ALU.is_gt, fill=0.0, base=0,
                             pattern=[[1, P]], channel_multiplier=-1)
            po.affine_select(out=low[:], in_=low[:], compare_op=ALU.is_gt, fill=0.0, base=0,
                             pattern=[[-1, P]], channel_multiplier=1)
            po.affine_select(out=band[:], in_=band[:], compare_op=ALU.is_gt, fill=-BIG, base=0,
                             pattern=[[1, KW]], channel_multiplier=-1)
            po.drain()
            po.affine_select(out=band[:], in_=band[:], compare_op=ALU.is_ge, fill=-BIG, base=WIN,
                             pattern=[[-1, KW]], channel_multiplier=1)
            po.drain().then_inc(S["consts"], 1)
            po.wait_ge(S["eqa"], 1)
            po.tensor_tensor(eq_low, eq_all, low[:].unsqueeze(1).broadcast_to([P, ST, P]), ALU.mult).then_inc(S["eql"], 1)

            def old_rows(b):
                for c in range(2):
                    col = c * NB + b
                    po.indirect_dma_start(out=kv[b % 2][:, c, :], out_offset=None, in_=d["kv_pool"],
                                          in_offset=bass.IndirectOffsetOnAxis(ap=old_idx[:, col:col + 1], axis=0)
                                          ).then_inc(S2["kvc"][b % 2], 16)

            def new_rows(b):
                for c in (2, 3):
                    col = c * NB + b
                    po.indirect_dma_start(out=kv[b % 2][:, c, :], out_offset=None, in_=d["new_kv"],
                                          in_offset=bass.IndirectOffsetOnAxis(ap=new_idx[:, col:col + 1], axis=0)
                                          ).then_inc(S2["kvd"][b % 2], 16)
                po.wait_ge(S2["kvc"][b % 2], 32 * (b // 2 + 1))
                for c in range(2):
                    col = c * NB + b
                    po.indirect_dma_start(out=kv[b % 2][:, c, :], out_offset=None, in_=d["new_kv"],
                                          in_offset=bass.IndirectOffsetOnAxis(ap=new_idx[:, col:col + 1], axis=0),
                                          bounds_check=N - 1, oob_is_err=False).then_inc(S2["kvd"][b % 2], 16)

            def scatter(rows, b, n):
                po.wait_ge(S["r_slot"], n)
                for t in (2 * b, 2 * b + 1):
                    for c in range(2):
                        po.indirect_dma_start(out=d["xs"],
                                              out_offset=bass.IndirectOffsetOnAxis(ap=slot_i[:, c, t:t + 1], axis=0),
                                              in_=rows[:, t, :], in_offset=None).then_inc(S["xs_sc"], 16)

            po.wait_ge(S["idx_ok"], 1)
            po.wait_ge(S["pre_w"], 1)
            for b in range(2):
                old_rows(b)
            for s in range(2):
                po.wait_ge(S2["p1w"][s], 32 * (NT // 2))
            for b in range(2):
                new_rows(b)
            po.wait_ge(S["cell_ok"], 1)
            po.wait_ge(S["zdone"], 16 * 9)
            mst = d["m_buf"][0:CELLS, :].rearrange("(k p r) e -> p k (r e)", k=KC, p=P)
            for b in range(NB):
                if 2 <= b + 1 < NB:
                    po.wait_ge(S["s_pv"], 16 * b)
                    old_rows(b + 1)
                    new_rows(b + 1)
                if b < NB // 2:
                    for t in range(b * ST // 4, (b + 1) * ST // 4):
                        if t:
                            po.wait_ge(S["mscat"], 16 * t)
                        po.indirect_dma_start(out=d["m_buf"],
                                              out_offset=bass.IndirectOffsetOnAxis(ap=cell_i[:, t:t + 1], axis=0),
                                              in_=tot[:, t, :], in_offset=None, compute_op=ALU.add
                                              ).then_inc(S["mscat"], 16)
                if b == NB // 2 - 1:
                    po.wait_ge(S["mscat"], 16 * ST)
                    po.wait_ge(S["att_w"], 32)
                    po.wait_ge(S["tot_p"], 1)
                    po.dma_start(stage, mst[:, KC - 1, 0:2048]).then_inc(S["mstage"], 16)
                if b >= 1:
                    po.wait_ge(S["zrows"], 16 * b)
                    scatter(a_rows, b - 1, b)
                if b >= NB // 2:
                    for m in range(2 * (b - NB // 2), 2 * (b - NB // 2) + 2):
                        k, r = KC - 1 - m // 2, 256 * (m % 2)
                        if m == 2 * KC - 2:
                            po.wait_ge(S["zrows"], 16 * (NB + 1))
                        po.wait_ge(S["mstage"], 16 * (m + 1))
                        po.tensor_tensor(m_w[:, k, :, r:r + 256], stage.rearrange("p (r e) -> p e r", e=NE),
                                         w0_t[:, k, r:r + 256].unsqueeze(1).broadcast_to([P, NE, 256]), ALU.add
                                         ).then_inc(S["m_done"], 1)
                        if m + 1 < 2 * KC:
                            m += 1
                            po.wait_ge(S["m_done"], m)
                            po.dma_start(stage, mst[:, KC - 1 - m // 2, 2048 * (m % 2):2048 * (m % 2 + 1)]
                                         ).then_inc(S["mstage"], 16)
            po.wait_ge(S["zrows"], 16 * NB)
            scatter(a_rows, NB - 1, NB)
            def gather(t, used, ready):
                s = t % 2
                if t >= 2:
                    po.wait_ge(used[s], t // 2)
                for c, y in enumerate((y1, y2)):
                    po.indirect_dma_start(out=y[s], out_offset=None, in_=d["ys"],
                                          in_offset=bass.IndirectOffsetOnAxis(ap=slot_y[:, c, t:t + 1], axis=0)
                                          ).then_inc(ready[s], 16)

            for s in range(2):
                po.wait_ge(S2["l_st"][s], 16 * (NTILE // 2))
            gather(0, S2["c_x1"], S2["ga_y"])
            gather(1, S2["c_x1"], S2["ga_y"])
            for b in range(NB):
                if b + 1 < NB:
                    gather(2 * b + 2, S2["c_x1"], S2["ga_y"])
                    gather(2 * b + 3, S2["c_x1"], S2["ga_y"])
                if b >= 1:
                    scatter(x2_rows, b - 1, NB + b)
            scatter(x2_rows, NB - 1, 2 * NB)
            for s in range(2):
                po.wait_ge(S2["k_st"][s], 16 * (NTILE // 2))
            for t in range(NT):
                gather(t, S2["f_o"], S2["fin_y"])

        @block.tensor
        def _(pe):
            def chunks(out, lhs, rhs, first=True, last=True):
                for k in range(KC):
                    m = pe.matmul(out, lhs(k), rhs(k), start=(k == 0 and first), stop=(k == KC - 1 and last))
                return m

            def turn4(out, src):
                for k in range(KC):
                    m = pe.transpose(out[:, k * P:(k + 1) * P], src[:, k * P:(k + 1) * P], ident[:])
                return m

            pe.wait_ge(S["consts"], 1)
            pe.wait_ge(S["raw_dma"], 16 * 5)
            for k in range(KC):
                chunks(ps[:, 7, k * NE:(k + 1) * NE], lambda o: raw_wo[:, o, k * P:(k + 1) * P], lambda o: gate0[:, o, :])
                chunks(ps[:, 7, 64 + k * NE:64 + (k + 1) * NE], lambda o: raw_w1[:, o, k * P:(k + 1) * P],
                       lambda o: gate1[:, o, :])
            chunks(ps[:, 7, 128:128 + NE], lambda o: raw_b[:, o, :], lambda o: gate1[:, o, :]).then_inc(S["pre_w"], 1)
            pe.wait_ge(S["w_qkv"], 16)
            pe.wait_ge(S["pre_c"], 1)
            with pe.Fori(0, NT // 4) as i:
                for s in range(4):
                    pe.wait_ge(S4["x_in"][s], 16 * i + 16)
                    pe.wait_ge(S4["p1p"][s], i)
                    for h in range(2):
                        m = chunks(ps[:, 2 * s + h, :], lambda k: xt[s][:, k, :], lambda k: wqkv[:, k, h * D:(h + 1) * D])
                    m.then_inc(S4["qkv"][s], 1)
            pe.wait_ge(S["eaw_ok"], 1)
            for s in range(4):
                pe.wait_ge(S4["p1p"][s], NT // 4)
            pe.transpose(ps[0:64, 6, 0:NE], eaw[:], ident[0:NE, 0:NE]).then_inc(S["eaw_p"], 1)
            pe.wait_ge(S["eaw_c"], 1)
            at_v = atoms.rearrange("a (p t) -> a t p", t=ST)
            for t in range(ST):
                m = pe.matmul(ps[:, 6, t * NE:(t + 1) * NE], at_v[:, t, :], eaw_t[:], start=True, stop=True)
            m.then_inc(S["delta"], 1)
            pe.wait_ge(S["wgt_ok"], 1)
            for t in range(ST):
                m = pe.matmul(ps[:, 7, t * NE:(t + 1) * NE], eq_all[:, t, :], wgt[:, t, :], start=True, stop=True)
            m.then_inc(S["tot_p"], 1)
            bk, bc = S2["bk"], S2["bc"]

            def turn_q(s, banks):
                for qt in range(2):
                    b, n = banks[qt]
                    wait(pe, bc[b], n)
                    turn4(ps[:, b, :], q_in[:, qt, :]).then_inc(bk[b], 1)

            def turn_k(s, banks):
                for p in range(2):
                    b, n = banks[p]
                    wait(pe, bc[b], n)
                    for c in range(NC):
                        m = pe.transpose(ps[:, b, c * P:(c + 1) * P], kv[s][:, c, p * P:(p + 1) * P], ident[:])
                    m.then_inc(bk[b], 1)

            def dots(B, u, s):
                qt, h = u // NH, HEADS[u % NH]
                g = h // 2
                base, p, jj = 64 * (g % 2), g // 2, (g // 2) * 2 + h % 2
                wait(pe, S["s_mx"], 16 * B + u - 1)
                pe.matmul(ps[:, 2 + u % 2, 0:KW], q_t[s][base:base + 64, jj, qt * P:(qt + 1) * P],
                          k_t[s][base:base + 64, p, qt * P:qt * P + KW], start=True, stop=True).then_inc(S["s_dot"], 1)

            def turn_p(B, u):
                wait(pe, S["s_exp"], 16 * B + u + 1)
                wait(pe, S["s_pe"], 16 * B + u - 1)
                for c in range(3):
                    m = pe.transpose(ps[:, 4 + u % 2, c * P:(c + 1) * P], prob[u % 4][:, c * P:(c + 1) * P], ident[:])
                m.then_inc(S["s_pt"], 1)

            def mix(B, u, s):
                qt, h = u // NH, HEADS[u % NH]
                wait(pe, S["s_pe"], 16 * B + u + 1)
                if u % NH == 0:
                    wait(pe, S["s_norm"], 2 * B + qt - 1)
                for c in range(3):
                    m = pe.matmul(ps[:, 6 + qt, h * HD:(h + 1) * HD], prob_t[u % 4][:, c * P:(c + 1) * P],
                                  kv[s][:, qt + c, (NG + h // 2) * HD:(NG + h // 2 + 1) * HD], start=(c == 0), stop=(c == 2))
                m.then_inc(S["s_pv"], 1)

            def tail(at, x, norms):
                b, n = at["o" + x]
                wait(pe, S["s_norm"], norms)
                wait(pe, bc[b], n)
                turn4(ps[:, b, :], o_sb).then_inc(bk[b], 1)

            def project(at, x):
                b, n = at["a" + x]
                wait(pe, bc[0], at["o" + x][1] + 1)
                wait(pe, bc[b], n)
                chunks(ps[:, b, :], lambda k: o_t[:, k, :], lambda k: w_o[:, k, :]).then_inc(bk[b], 1)
                b, n = at["g" + x]
                chunks(ps[:, b, 0:NE], lambda k: o_t[:, k, :], lambda k: wo_g[:, k, :]).then_inc(bk[b], 1)

            def count(at, n):
                b, m = at["rt"]
                wait(pe, S["r_sel"], n)
                wait(pe, bc[b], m)
                sel = selb16[:].rearrange("p t e -> p (t e)")
                pe.matmul(ps[:, b, 0:2 * NE], tri[:], sel, start=True, stop=True)
                pe.matmul(ps[:, b, 2 * NE:4 * NE], ones[:], sel, start=True, stop=True).then_inc(bk[b], 1)

            def period(B, kind, s, i):
                at = uses(B, kind)
                for u in range(2 * NH):
                    if u == 0:
                        wait(pe, bc[0], 7 * B - 3 if kind != "first" else 2)
                        wait(pe, bc[1], 4 * B if kind != "first" else 2)
                    dots(B, u, s)
                    if u >= 2 or kind != "first":
                        turn_p(B if u >= 2 else B - 1, (u - 2) % 16)
                    if u >= 3 or kind != "first":
                        mix(B if u >= 3 else B - 1, (u - 3) % 16, s if u >= 3 else 1 - s)
                    if u == 4 and "o1" in at:
                        tail(at, "1", 2 * B)
                    if u == 5 and "a1" in at:
                        project(at, "1")
                    if u == 7 and "q0" in at:
                        wait(pe, S["q_ld"], 16 * (B + 2))
                        turn_q(1 - s, (at["q0"], at["q1"]))
                    if u == 9 and "rt" in at:
                        count(at, B)
                    if u == 10 and "k0" in at:
                        wait(pe, S2["kvd"][1 - s], 64 * (i + 2) if kind != "first" else 64)
                        turn_k(1 - s, (at["k0"], at["k1"]))
                    if u == 12:
                        tail(at, "0", 2 * B + 1)
                    if u == 13:
                        project(at, "0")

            pe.wait_ge(S2["kvd"][0], 64)
            turn_k(0, ((0, 0), (1, 0)))
            pe.wait_ge(S["q_ld"], 16)
            turn_q(0, ((0, 1), (1, 1)))
            pe.wait_ge(S["att_w"], 32)
            periods(pe, period)
            turn_p(NB - 1, 14)
            mix(NB - 1, 13, 1)
            turn_p(NB - 1, 15)
            mix(NB - 1, 14, 1)
            mix(NB - 1, 15, 1)
            at = uses(NB, "after")
            tail(at, "1", 2 * NB)
            project(at, "1")
            count(at, NB)
            pe.wait_ge(S["r_ok"], 1)
            pe.wait_ge(S["m_done"], NB)

            def turn_x(load, done, turned, i, s):
                pe.wait_ge(load[s], 16 * i + 16)
                wait(pe, done[s], i)
                turn4(ps[:, s, :], xs_in[s]).then_inc(turned[s], 1)

            def layer0(i, more):
                es = [pe.value_load(ex_i[0:1, bass.ds(2 * i + s, 1)], min_val=0, max_val=NE - 1) for s in range(2)]
                for s in range(2):
                    pe.wait_ge(S2["l_xt"][s], i + 1)
                    wait(pe, S2["l_ye"][s], i)
                    chunks(ps[:, 2 + s, :], lambda k: xs_t[s][:, k, :], lambda k: m_w[:, k, es[s], :]
                           ).then_inc(S2["l_mm"][s], 1)
                    if more:
                        turn_x(S2["l_in"], S2["l_xt"], S2["l_tx"], i + 1, s)

            for s in range(2):
                turn_x(S2["l_in"], S2["l_xt"], S2["l_tx"], 0, s)
            with pe.Fori(0, NTILE // 2 - 1) as i:
                layer0(i, True)
            layer0(NTILE // 2 - 1, False)

            pe.wait_ge(S["w5"], 48)

            def turn_x1(i, s):
                pe.wait_ge(S2["c_x1"][s], i + 1)
                wait(pe, S2["c_xt"][s], i)
                turn4(ps[:, s, :], x1[s]).then_inc(S2["c_tx"][s], 1)

            def count1(n):
                wait(pe, S["r_sel"], NB + n)
                wait(pe, S2["c_lg"][0], n)
                sel = selb16[:].rearrange("p t e -> p (t e)")
                pe.matmul(ps[:, 6, 64:64 + 2 * NE], tri[:], sel, start=True, stop=True)
                pe.matmul(ps[:, 6, 64 + 2 * NE:64 + 4 * NE], ones[:], sel, start=True, stop=True).then_inc(S["c_rt"], 1)

            def linear(i, first, more):
                for s in range(2):
                    pe.wait_ge(S2["c_xt"][s], i + 1)
                    wait(pe, S2["c_xe"][s], i)
                    chunks(ps[:, 2 + s, 0:P], lambda k: lora_a[:, k, :], lambda k: x1_t[s][:, k, :]).then_inc(S2["c_xa"][s], 1)
                for s in range(2):
                    wait(pe, S2["c_x2"][s], i)
                    chunks(ps[:, 4 + s, :], lambda k: x1_t[s][:, k, :], lambda k: w1_t[:, k, :], last=False)
                    pe.wait_ge(S2["c_xe"][s], i + 1)
                    pe.matmul(ps[:, 4 + s, :], xa_t[s], lora_b[:], start=False, stop=True).then_inc(S2["c_h"][s], 1)
                    if s == 0 and not first:
                        wait(pe, S["c_rtc"], i)
                    wait(pe, S2["c_lg"][s], i)
                    chunks(ps[:, 6 + s, 0:NE], lambda k: x1_t[s][:, k, :], lambda k: w1_g[:, k, :], last=False)
                    pe.matmul(ps[:, 6 + s, 0:NE], xa_t[s], b_g[:], start=False, stop=True).then_inc(S2["c_g"][s], 1)
                    if more:
                        turn_x1(i + 1, s)

            for s in range(2):
                turn_x1(0, s)
            linear(0, True, True)
            with pe.Fori(1, NT // 2 - 1) as i:
                count1(i)
                linear(i, False, True)
            count1(NT // 2 - 1)
            linear(NT // 2 - 1, False, False)
            count1(NT // 2)
            pe.wait_ge(S["r_ok"], 2)
            pe.wait_ge(S["fc1_d"], 16 * KC)
            pe.wait_ge(S["fc2_d"], 16 * KC)

            def layer1(i, more):
                es = [pe.value_load(ex_i[0:1, bass.ds(2 * i + s, 1)], min_val=0, max_val=NE - 1) for s in range(2)]
                for s in range(2):
                    pe.wait_ge(S2["k_xt"][s], i + 1)
                    wait(pe, S2["k_hb"][s], i)
                    chunks(ps[:, 2 + s, :], lambda k: xs_t[s][:, k, :], lambda k: fc1[:, k, es[s], :]
                           ).then_inc(S2["k_m1"][s], 1)
                for s in range(2):
                    pe.wait_ge(S2["k_hg"][s], i + 1)
                    wait(pe, S2["k_ht"][s], i)
                    turn4(ps[:, 4 + s, :], h_sb[s]).then_inc(S2["k_th"][s], 1)
                    if more:
                        turn_x(S2["k_in"], S2["k_xt"], S2["k_tx"], i + 1, s)
                    pe.wait_ge(S2["k_ht"][s], i + 1)
                    wait(pe, S2["k_ye"][s], i)
                    chunks(ps[:, 6 + s, :], lambda k: h_t[s][:, k, :], lambda k: fc2[:, k, es[s], :]
                           ).then_inc(S2["k_m2"][s], 1)

            for s in range(2):
                turn_x(S2["k_in"], S2["k_xt"], S2["k_tx"], 0, s)
            with pe.Fori(0, NTILE // 2 - 1) as i:
                layer1(i, True)
            layer1(NTILE // 2 - 1, False)

        @block.scalar
        def _(ac):
            chunked = "(k p) n -> p k n"
            ac.dma_start(gate0[:], d["gate0_t"].rearrange(chunked, p=P)).then_inc(S["raw_dma"], 16)
            ac.dma_start(gate1[:], d["gate1"].rearrange(chunked, p=P)).then_inc(S["raw_dma"], 16)
            ac.dma_start(raw_wo, d["wo"].rearrange(chunked, p=P)).then_inc(S["raw_dma"], 16)
            ac.dma_start(raw_w1, d["w1"].rearrange(chunked, p=P)).then_inc(S["raw_dma"], 16)
            ac.dma_start(raw_b, d["b_o"].rearrange(chunked, p=P)).then_inc(S["raw_dma"], 16)
            ac.dma_start(wqkv, d["wqkv_t"].rearrange(chunked, p=P)).then_inc(S["w_qkv"], 16)
            xt_v = d["x_t"].rearrange("(k p) (t m) -> p k t m", p=P, m=P)
            for s in range(4):
                ac.dma_start(xt[s], xt_v[:, :, s, :]).then_inc(S4["x_in"][s], 16)
            ac.wait_ge(S["rope_in"], 1)
            ac.activation(sin_t.rearrange("p a b -> p (a b)"), ang.rearrange("p a b -> p (a b)"), ACT.Sin)
            ac.activation(cos_t.rearrange("p a b -> p (a b)"), ang2.rearrange("p a b -> p (a b)"), ACT.Sin
                          ).then_inc(S["rope_r"], 1)
            ac.wait_ge(S["eaw_in"], 1)
            ac.activation(eaw[:], eaw[:], ACT.Exp, bias=eaw_s[:, 0:1], accum_out=eaw_s[:, 1:2])
            ac.activation(imp.rearrange("p a b -> p (a b)"), imp.rearrange("p a b -> p (a b)"), ACT.Sigmoid
                          ).then_inc(S["imp_s"], 1)
            ac.wait_ge(S["rope_ok"], 1)
            flat = "p a b -> p (a b)"
            with ac.Fori(0, NT // 4) as i:
                for pair in range(2):
                    for x in range(2):
                        s = 2 * pair + x
                        ac.wait_ge(S4["qkv"][s], i + 1)
                        ac.wait_ge(S2["ssd"][x], 2 * i + pair)
                        ac.activation(sq[x], ps[:, 2 * s:2 * s + 2, :].rearrange(flat)[:, 0:QK], ACT.Square)
                        ac.wait_ge(S2["p1w"][x], 64 * i + 32 * pair)
                        ac.activation(qkv_out[x][:, QK:2 * D], ps[:, 2 * s + 1, QK - D:D], ACT.Copy).then_inc(S4["a1"][s], 1)
                    ac.wait_ge(S2["rec"][0], 2 * i + pair + 1)
                    ac.activation(root[:].rearrange(flat), rstd[:].rearrange(flat), ACT.Sqrt).then_inc(S2["root"][0], 1)
            bk, bc = S2["bk"], S2["bc"]

            def out_of(use, dst):
                b, n = use
                wait(ac, bk[b], n + 1)
                ac.activation(dst, ps[:, b, :] if len(dst.shape) == 2 else ps[:, b, :].rearrange("p (a b) -> p a b", b=P),
                              ACT.Copy).then_inc(bc[b], 1)

            def expo(B, u):
                wait(ac, S["s_mx"], 16 * B + u + 1)
                wait(ac, S["s_pt"], 16 * B + u - 3)
                ac.activation(prob[u % 4], msk_s[u % 2], ACT.Exp, bias=nmx[:, u:u + 1], scale=SCALE,
                              accum_out=sums[:, u:u + 1]).then_inc(S["s_exp"], 1)

            def evac(B, u):
                wait(ac, S["s_pt"], 16 * B + u + 1)
                wait(ac, S["s_pv"], 16 * B + u - 3)
                ac.activation(prob_t[u % 4], ps[:, 4 + u % 2, 0:KW], ACT.Copy).then_inc(S["s_pe"], 1)

            def period(B, kind, s, i):
                at = uses(B, kind)
                for u in range(2 * NH):
                    expo(B, u)
                    if u >= 2 or kind != "first":
                        evac(B if u >= 2 else B - 1, (u - 2) % 16)
                    if u == 4 and "o1" in at:
                        out_of(at["o1"], o_t.rearrange(flat))
                    if u == 8 and "q0" in at:
                        for qt in range(2):
                            out_of(at[f"q{qt}"], q_t[1 - s][:, :, qt * P:(qt + 1) * P])
                    if u == 11 and "k0" in at:
                        for p in range(2):
                            out_of(at[f"k{p}"], k_t[1 - s][:, p, :])
                    if u == 12:
                        out_of(at["o0"], o_t.rearrange(flat))

            for s in range(2):
                ac.wait_ge(S2["p1w"][s], 32 * (NT // 2))
            for p in range(2):
                out_of((p, 0), k_t[0][:, p, :])
            for qt in range(2):
                out_of((qt, 1), q_t[0][:, :, qt * P:(qt + 1) * P])
            periods(ac, period)
            evac(NB - 1, 14)
            evac(NB - 1, 15)
            out_of(uses(NB, "after")["o1"], o_t.rearrange(flat))
            ac.wait_ge(S["xs_sc"], 32 * NT)

            def layer0(i):
                for s in range(2):
                    ac.wait_ge(S2["l_tx"][s], i + 1)
                    wait(ac, S2["l_mm"][s], i)
                    ac.activation(xs_t[s].rearrange(flat), ps[:, s, :], ACT.Copy).then_inc(S2["l_xt"][s], 1)
            layer0(0)
            ac.wait_ge(S["r_e"], 1)
            ac.activation(cwt[:], cwt[:], ACT.Exp).then_inc(S["r_exp"], 1)
            with ac.Fori(1, NTILE // 2) as i:
                layer0(i)
            for s in range(2):
                ac.wait_ge(S2["l_st"][s], 16 * (NTILE // 2))

            def turned(i):
                for s in range(2):
                    ac.wait_ge(S2["c_tx"][s], i + 1)
                    wait(ac, S2["c_h"][s], i)
                    ac.activation(x1_t[s].rearrange(flat), ps[:, s, :], ACT.Copy).then_inc(S2["c_xt"][s], 1)

            def soft(i):
                ac.wait_ge(S["r_l"], i + 1)
                ac.activation(lg[:].rearrange(flat), lg[:].rearrange(flat), ACT.Exp).then_inc(S["r_lexp"], 1)
            turned(0)
            with ac.Fori(0, NT // 2 - 1) as i:
                turned(i + 1)
                soft(i)
            soft(NT // 2 - 1)
            for s in range(2):
                ac.wait_ge(S2["c_st"][s], 16 * (NT // 2))
            with ac.Fori(0, NTILE // 2) as i:
                for s in range(2):
                    ac.wait_ge(S2["k_tx"][s], i + 1)
                    ac.wait_ge(S2["k_m1"][s], i)
                    ac.activation(xs_t[s].rearrange(flat), ps[:, s, :], ACT.Copy).then_inc(S2["k_xt"][s], 1)
                for s in range(2):
                    ac.wait_ge(S2["k_hb"][s], i + 1)
                    ac.activation(h_sb[s], h_sb[s], ACT.Gelu).then_inc(S2["k_hg"][s], 1)
                for s in range(2):
                    ac.wait_ge(S2["k_th"][s], i + 1)
                    ac.wait_ge(S2["k_m2"][s], i)
                    ac.activation(h_t[s].rearrange(flat), ps[:, 4 + s, :], ACT.Copy).then_inc(S2["k_ht"][s], 1)

        @block.vector
        def _(ve):
            TT, TS, CP = ve.tensor_tensor, ve.tensor_scalar, ve.tensor_copy

            def red(out, in_, op=ALU.max):
                return ve.tensor_reduce(out, in_, AX, op)

            ve.wait_ge(S["p0_dma"], 16 * 13)
            ve.wait_ge(S["consts"], 1)
            CP(iof[:, 0:33], iot[:, 0:33])
            CP(tile_io[:], tile_ii[:])
            CP(jrow[:], jrow_i)
            CP(lens[:], lens_i[:])
            TS(ints[:, 0:8], lens_i[:], 4, None, ALU.arith_shift_right)
            TS(ints[:, 8:16], lens_i[:], BLK - 1, None, ALU.bitwise_and)
            TS(ints[:, 16:17], iot[:, 32:33], 4, None, ALU.arith_shift_right)
            TS(ints[:, 17:18], iot[:, 32:33], BLK - 1, None, ALU.bitwise_and)
            CP(ms_f[:], ms_i[:])
            TS(cell_i[:], ms_i[:], D - 1, 9, ALU.bitwise_and, ALU.logical_shift_left)
            TS(cell_j[:], ms_i[:], 9, None, ALU.arith_shift_right)
            ve.drain()
            CP(first[:], ints[:, 0:8])
            CP(lo[:], ints[:, 8:16])
            CP(part[:, 0:1], iof[:, 32:33])
            CP(part[:, 1:3], ints[:, 16:18])
            TS(rev[:], iof[:, 0:NE], -1.0, float(NE), ALU.mult, ALU.add)
            TT(cell_i[:], cell_i[:], cell_j[:], ALU.bitwise_or)
            red(eaw_s[:, 2:3], eaw[:])
            ve.drain()
            TS(eaw_s[:, 0:1], eaw_s[:, 2:3], -1.0, None, ALU.mult).then_inc(S["eaw_in"], 1)
            TS(gains[:], gains[:], 1.0, None, ALU.add)
            for h in range(2):
                TS(pos[:, h:NT:2], lens[:], part[:, 0:1], float(P * h), ALU.add, ALU.add)
            ve.drain()
            TT(ang, pos[:].unsqueeze(2).broadcast_to([P, NT, HD // 2]), inv_f[:].unsqueeze(1).broadcast_to([P, NT, HD // 2]), ALU.mult)
            ve.drain()
            TS(ang2, ang, float(np.float32(1 / (2 * np.pi))), 12582912.0, ALU.mult, ALU.add)
            ve.drain()
            TS(ang2, ang2, 12582912.0, None, ALU.subtract)
            ve.drain()
            c1 = 6.28125
            c2 = float(np.float32(int((2 * np.pi - c1) * 2 ** 20) / 2 ** 20))
            c3 = float(np.float32(2 * np.pi - c1 - c2))
            for c in (c1, c2, c3):
                ve.scalar_tensor_tensor(ang, ang2, -c, ang, ALU.mult, ALU.add)
                ve.drain()
            TS(ang, ang, 3.1415925, -3.1415925, ALU.min, ALU.max)
            ve.drain()
            TS(ang2, ang, -1.0, None, ALU.mult)
            ve.drain()
            TT(ang2, ang2, ang, ALU.min)
            ve.drain()
            TS(ang2, ang2, float(np.float32(np.pi / 2)), None, ALU.add).then_inc(S["rope_in"], 1)
            for b in range(NB):
                s0 = ve.value_load(ints[0:1, b:b + 1], min_val=0, max_val=(SEQ - WIN + P) // BLK + 8)
                CP(win[:, b, :], table_bc[:, bass.ds(s0 + b * NBLK, SB)])
            TS(eqk[:, 0, 0:NE], iof[:, 0:NE], part[:, 1:2], None, ALU.is_equal)
            ve.drain()
            TT(eqk[:, 1, 0:NE], eqk[:, 0, 0:NE], scal_bc[:], ALU.mult)
            CP(sel_b[:], adapt_i[:])
            ve.drain()
            red(part[:, 3:4], eqk[:, 1, 0:NE], ALU.add)
            ve.drain()
            TS(sel_b[:], sel_b[:], part[:, 1:2], part[:, 3:4], ALU.is_equal, ALU.mult)
            TS(carry[:], lo[:], part[:, 2:3], float(BLK), ALU.add, ALU.is_ge)
            TS(off[:], lo[:], part[:, 2:3], None, ALU.add)
            ve.drain()
            ve.scalar_tensor_tensor(off[:], carry[:], -float(BLK), off[:], ALU.mult, ALU.add)
            TS(carry[:], carry[:], part[:, 1:2], None, ALU.add)
            ve.drain()
            TT(eqk, iof[:, 0:9].unsqueeze(1).broadcast_to([P, NB, 9]), carry[:].unsqueeze(2).broadcast_to([P, NB, 9]), ALU.is_equal)
            ve.drain()
            for c in range(NC):
                TT(tmp9, eqk, win[:, :, 8 * c:8 * c + 9], ALU.mult)
                ve.drain()
                red(blk[:, c, :], tmp9, ALU.add)
                ve.drain()
            TT(wr_tok, iof[:, 0:SW].unsqueeze(1).broadcast_to([P, NB, SW]), first[:].unsqueeze(2).broadcast_to([P, NB, SW]), ALU.add)
            ve.drain()
            TS(wr_tok, wr_tok, float(NBLK), None, ALU.is_lt)
            TS(wr_blk, win[:, :, SB - SW:SB], 1.0, None, ALU.add)
            ve.drain()
            TT(wr_blk, wr_blk, wr_tok, ALU.mult)
            ve.drain()
            TS(wr_blk, wr_blk, -1.0, None, ALU.add)
            TS(junk[:, 0:1], part[:, 0:1], 1.0, None, ALU.mult)
            TS(wr_tok, iof[:, 0:SW].unsqueeze(1).broadcast_to([P, NB, SW]), float(BLK), float(BLK), ALU.mult, ALU.add)
            ve.drain()
            TT(wr_tok, wr_tok, lo[:].unsqueeze(2).broadcast_to([P, NB, SW]), ALU.subtract)
            TS(ntf[0][:], iof[:, 0:NB], float(T), None, ALU.mult)
            ve.drain()
            TT(wr_tok, wr_tok, ntf[0][:].unsqueeze(2).broadcast_to([P, NB, SW]), ALU.add)
            TT(edge[:, 0], off[:].unsqueeze(2).broadcast_to([P, NB, NB]), lo[:].unsqueeze(1).broadcast_to([P, NB, NB]), ALU.is_ge)
            ve.drain()
            TS(edge[:, 1], edge[:, 0], -1.0, 1.0, ALU.mult, ALU.add)
            TT(hits, blk[:].rearrange("p c b -> p (c b)").unsqueeze(2).broadcast_to([P, NC * NB, NB * SW]),
               wr_blk.rearrange("p b s -> p (b s)").unsqueeze(1).broadcast_to([P, NC * NB, NB * SW]), ALU.is_equal)
            ve.drain()
            TT(hits, hits, wr_tok.rearrange("p b s -> p (b s)").unsqueeze(1).broadcast_to([P, NC * NB, NB * SW]), ALU.mult)
            ve.drain()
            hv = hits.rearrange("p (c b) (w s) -> p c b w s", c=NC, w=NB)
            for c in range(NC):
                for x, sl in ((0, 0), (1, SW - 1)):
                    TT(hv[:, c, :, :, sl], hv[:, c, :, :, sl], edge[:, x], ALU.mult)
            ve.drain()
            red(best[:].rearrange("p c b -> p (c b)"), hits)
            ve.drain()
            TS(found[:], best[:], 0.0, None, ALU.is_gt)
            ve.drain()
            TS(best[:], best[:], -float(BLK), None, ALU.add)
            ve.drain()
            TT(best[:], best[:], off[:].unsqueeze(1).broadcast_to([P, NC, NB]), ALU.add)
            ve.drain()
            TT(best[:], best[:], found[:], ALU.mult)
            ve.drain()
            TS(found[:, 0:2, :], found[:, 0:2, :], -float(4 * N), float(4 * N), ALU.mult, ALU.add)
            TS(fidx[:, 0:2], blk[:, 0:2], float(BLK), None, ALU.mult)
            ve.drain()
            TT(best[:, 0:2, :], best[:, 0:2, :], found[:, 0:2, :], ALU.add)
            TT(fidx[:, 0:2], fidx[:, 0:2], off[:].unsqueeze(1).broadcast_to([P, 2, NB]), ALU.add)
            ve.drain()
            CP(new_idx[:], best[:].rearrange("p c b -> p (c b)"))
            CP(old_idx[:], fidx[:, 0:2].rearrange("p c b -> p (c b)"))
            ve.drain().then_inc(S["idx_ok"], 1)

            ve.wait_ge(S["rope_r"], 1)
            hh = HD // 2
            for w in range(2):
                for h in range(2):
                    TT(tab_a[:, :, w, h * hh:(h + 1) * hh], cos_t, gains[:, w, h * hh:(h + 1) * hh].unsqueeze(1).broadcast_to([P, NT, hh]), ALU.mult)
                TT(tab_b[:, :, w, 0:hh], sin_t, gains[:, w, hh:HD].unsqueeze(1).broadcast_to([P, NT, hh]), ALU.mult)
                TT(tab_b[:, :, w, hh:HD], sin_t, gains[:, w, 0:hh].unsqueeze(1).broadcast_to([P, NT, hh]), ALU.mult)
            ve.drain()
            TS(tab_b[:, :, :, 0:hh], tab_b[:, :, :, 0:hh], -1.0, None, ALU.mult)
            ve.drain().then_inc(S["rope_ok"], 1)
            ve.wait_ge(S["pre_w"], 1)
            CP(wo_g[:].rearrange("p a b -> p (a b)"), ps[:, 7, 0:KC * NE])
            CP(w1_g[:].rearrange("p a b -> p (a b)"), ps[:, 7, 64:64 + KC * NE])
            CP(b_g[:], ps[:, 7, 128:128 + NE])
            ve.drain().then_inc(S["pre_c"], 1)
            ve.wait_ge(S["imp_s"], 1)
            ve.reciprocal(eaw_s[:, 3:4], eaw_s[:, 1:2])
            ve.drain()
            TS(eaw[:], eaw[:], eaw_s[:, 3:4], None, ALU.mult).then_inc(S["eaw_ok"], 1)

            TT(eq_all, mask_bc.rearrange("p (s t) -> p t s", t=ST), ms_f[:].unsqueeze(2).broadcast_to([P, ST, P]),
               ALU.is_equal).then_inc(S["eqa"], 1)

            flat = "p a b -> p (a b)"
            with ve.Fori(0, NT // 4) as i:
                for pair in range(2):
                    for x in range(2):
                        ve.wait_ge(S4["a1"][2 * pair + x], i + 1)
                        red(ss[:, x, :], sq[x].rearrange("p (h d) -> p h d", d=HD), ALU.add).then_inc(S2["ssd"][x], 1)
                    ve.drain()
                    TS(ss[:], ss[:], 1.0 / HD, RMS_EPS, ALU.mult, ALU.add)
                    ve.drain()
                    ve.reciprocal(rstd[:], ss[:]).then_inc(S2["rec"][0], 1)
                    ve.wait_ge(S2["root"][0], 2 * i + pair + 1)
                    TT(rstd[:], root[:], root[:], ALU.mult)
                    ve.drain()
                    TT(rstd[:], rstd[:], ss[:], ALU.mult)
                    ve.drain()
                    TS(rstd[:], rstd[:], -0.5, 1.5, ALU.mult, ALU.add)
                    ve.drain()
                    TT(rstd[:], rstd[:], root[:], ALU.mult)
                    ve.drain()
                    for x in range(2):
                        s = 2 * pair + x
                        t = 4 * i + s
                        TT(nrm.rearrange("p (h d) -> p h d", d=HD),
                           ps[:, 2 * s:2 * s + 2, :].rearrange(flat)[:, 0:QK].rearrange("p (h d) -> p h d", d=HD),
                           rstd[:, x, :].unsqueeze(2).broadcast_to([P, NQK, HD]), ALU.mult).then_inc(S4["p1p"][s], 1)
                        ve.drain()
                        nv = nrm.rearrange("p (h x d) -> p h x d", x=2, d=hh)
                        bv = rot_b.rearrange("p (h x d) -> p h x d", x=2, d=hh)
                        av = rot_a.rearrange("p (h d) -> p h d", d=HD)
                        for w, h0, h1 in ((0, 0, NH), (1, NH, NQK)):
                            TT(av[:, h0:h1], nrm.rearrange("p (h d) -> p h d", d=HD)[:, h0:h1],
                               tab_a[:, t, w, :].unsqueeze(1).broadcast_to([P, h1 - h0, HD]), ALU.mult)
                            for y in range(2):
                                TT(bv[:, h0:h1, y], nv[:, h0:h1, 1 - y],
                                   tab_b[:, t, w, y * hh:(y + 1) * hh].unsqueeze(1).broadcast_to([P, h1 - h0, hh]), ALU.mult)
                        ve.drain()
                        TT(qkv_out[x][:, 0:QK], rot_a, rot_b, ALU.add).then_inc(S2["p1o"][x], 1)
                        ve.drain()

            ve.wait_ge(S["eaw_p"], 1)
            CP(eaw_t[:], ps[0:64, 6, 0:NE]).then_inc(S["eaw_c"], 1)
            ve.wait_ge(S["eql"], 1)
            red(dup[:], eq_low)
            CP(cell_f[:], cell_i[:])
            ve.wait_ge(S["delta"], 1)
            TT(wgt.rearrange(flat), ps[:, 6, 0:ST * NE], imp.rearrange(flat), ALU.mult).then_inc(S["wgt_ok"], 1)
            ve.drain()
            TS(ms_f[:], cell_f[:], -1.0, float(CELLS), ALU.mult, ALU.add)
            ve.drain()
            TS(ms_f[:], ms_f[:], part[:, 0:1], None, ALU.add)
            ve.drain()
            TT(ms_f[:], ms_f[:], dup[:], ALU.mult)
            ve.drain()
            TT(cell_f[:], cell_f[:], ms_f[:], ALU.add)
            ve.drain()
            CP(cell_i[:], cell_f[:])
            ve.wait_ge(S["tot_p"], 1)
            CP(tot[:].rearrange(flat), ps[:, 7, 0:ST * NE])
            ve.drain().then_inc(S["cell_ok"], 1)
            bk, bc = S2["bk"], S2["bc"]

            def build_mask(B, qt):
                kb, tmp = key_bias[:, 0, :], key_bias[:, 1, :]
                jr = jrow[:, qt * P:qt * P + KW]
                TS(kb, jr, lens[:, bass.ds(B, 1)], 0.0, ALU.add, ALU.is_ge)
                TS(tmp, jr, lens[:, bass.ds(B, 1)], float(SEQ), ALU.add, ALU.is_lt)
                ve.drain()
                TT(kb, kb, tmp, ALU.mult)
                ve.drain()
                TS(kb, kb, -1.0, BIG, ALU.add, ALU.mult)
                ve.drain()
                TT(mask[:, qt, :], band[:], kb, ALU.add)
                ve.drain()

            def top(B, u):
                wait(ve, S["s_dot"], 16 * B + u + 1)
                ve.memset(junk[:, 0:1], 0.0)
                if not isinstance(B, int) or 16 * B + u - 1 > 0:
                    wait(ve, S["s_exp"], 16 * B + u - 1)
                    ve.memset(junk[:, 1:2], 0.0)
                ve.tensor_tensor_reduce(out=msk_s[u % 2], in0=ps[:, 2 + u % 2, 0:KW], in1=mask[:, u // NH, :], scale=1.0,
                                        scalar=-3e38, op0=ALU.add, op1=ALU.max, accum_out=mx[:, u:u + 1])
                ve.drain()
                TS(nmx[:, u:u + 1], mx[:, u:u + 1], -SCALE, None, ALU.mult).then_inc(S["s_mx"], 1)

            def norm(B, qt):
                wait(ve, S["s_pv"], 16 * B + 8 * qt + 8)
                ve.reciprocal(rsum[:], sums[:, 8 * qt:8 * qt + 8])
                ve.drain()
                for y in range(2):
                    TT(o_sb.rearrange("p (g y x d) -> p g y x d", g=2, y=2, x=2)[:, :, y],
                       ps[:, 6 + qt, :].rearrange("p (g y x d) -> p g y x d", g=2, y=2, x=2)[:, :, y],
                       rsum[:].rearrange("p (g x y) -> p g x y", g=2, x=2)[:, :, :, y].unsqueeze(3).broadcast_to([P, 2, 2, HD]),
                       ALU.mult)
                ve.drain().then_inc(S["s_norm"], 1)

            def row(at, x, t):
                b, n = at["a" + x]
                wait(ve, bk[b], n + 1)
                ve.memset(junk[:, 2:3], 0.0)
                CP(a_rows[:, t, :], ps[:, b, :]).then_inc(bc[b], 1)
                b, n = at["g" + x]
                wait(ve, bk[b], n + 1)
                TS(lg[:, int(x), :], ps[:, b, 0:NE], 50.0, -50.0, ALU.min, ALU.max).then_inc(bc[b], 1)

            def b3(a):
                return a.unsqueeze(2).broadcast_to([P, 2, NE])

            def rb(a):
                return a.unsqueeze(1).broadcast_to([P, 2, NE])

            def choose(t, layer):
                ve.drain()
                src = lg
                for m, oh in ((m1, oh1), (m2, oh2)):
                    red(rr[:], src[:])
                    ve.drain()
                    CP(m[:, bass.ds(t, 2)], rr[:])
                    TT(t1[:], src[:], b3(rr[:]), ALU.is_equal)
                    ve.drain()
                    TT(t1[:], t1[:], rb(rev[:]), ALU.mult)
                    ve.drain()
                    red(rr[:], t1[:])
                    ve.drain()
                    TT(oh[:], rb(rev[:]), b3(rr[:]), ALU.is_equal)
                    ve.drain()
                    if oh is oh1:
                        ve.scalar_tensor_tensor(t2[:].rearrange(flat), oh[:].rearrange(flat), -BIG, lg[:].rearrange(flat),
                                                ALU.mult, ALU.add)
                        ve.drain()
                        src = t2
                TT(selb16[:], oh1[:], oh2[:], ALU.add).then_inc(S["r_sel"], 1)
                if layer == 1:
                    for oh, al in ((oh1, al1), (oh2, al2)):
                        ve.drain()
                        TT(t1[:], oh[:], rb(alpha_bc[:]), ALU.mult)
                        ve.drain()
                        red(rr[:], t1[:], ALU.add)
                        ve.drain()
                        CP(al[:, bass.ds(t, 2)], rr[:])

            def place(t, pre, tot_b, done):
                ve.drain()
                TT(t1[:], pre.rearrange("p (t e) -> p t e", e=NE), rb(run[:]), ALU.add)
                CP(t2[:], tot_b.rearrange("p (t e) -> p t e", e=NE)).then_inc(*done)
                ve.drain()
                TT(t1[:, 1, :], t1[:, 1, :], t2[:, 0, :], ALU.add)
                TT(run[:], run[:], t2[:, 0, :], ALU.add)
                ve.drain()
                TT(run[:], run[:], t2[:, 1, :], ALU.add)
                for c, oh in ((0, oh1), (1, oh2)):
                    ve.drain()
                    TT(t2[:], t1[:], oh[:], ALU.mult)
                    ve.drain()
                    red(slot_f[:, c, :], t2[:], ALU.add)
                ve.drain()
                CP(slot_i[:, :, bass.ds(t, 2)], slot_f[:])
                ve.drain().then_inc(S["r_slot"], 1)

            def place0(at, t):
                b, n = at["rt"]
                wait(ve, bk[b], n + 1)
                ve.memset(junk[:, 3:4], 0.0)
                place(t, ps[:, b, 0:2 * NE], ps[:, b, 2 * NE:4 * NE], (bc[b], 1))

            def tiles():
                def step(ins):
                    ve.drain()
                    return ins
                ve.drain()
                step(TT(ntf[0][:], run[:], region0[:], ALU.subtract))
                step(TS(ntf[0][:], ntf[0][:], float(P - 1), None, ALU.add))
                step(CP(nti[:], ntf[0][:]))
                step(TS(nti[:], nti[:], 7, None, ALU.arith_shift_right))
                CP(ntf[2][:], nti[:])
                step(CP(ntf[0][:], nti[:]))
                u, v = ntf[0], ntf[1]
                for sh in (1, 2, 4):
                    TT(v[:, sh:], u[:, sh:], u[:, :NE - sh], ALU.add)
                    step(CP(v[:, :sh], u[:, :sh]))
                    u, v = v, u
                TS(ntf[3][:], ntf[2][:], -float(P), float(N), ALU.mult, ALU.add)
                step(TT(v[:], u[:], ntf[2][:], ALU.subtract))
                step(TT(ex_c[:], v[:, 1:NE].unsqueeze(1).broadcast_to([P, NTILE, NE - 1]),
                        tile_io[:].unsqueeze(2).broadcast_to([P, NTILE, NE - 1]), ALU.is_le))
                step(red(ex_f[:], ex_c[:], ALU.add))
                CP(ex_i[:], ex_f[:])
                step(TT(ex_c[:], ex_c[:], ntf[3][:, 0:NE - 1].unsqueeze(1).broadcast_to([P, NTILE, NE - 1]), ALU.mult))
                step(red(ex_f[:], ex_c[:], ALU.add))
                step(ve.scalar_tensor_tensor(ex_f[:], tile_io[:], float(P), ex_f[:], ALU.mult, ALU.add))
                CP(row_i[:], ex_f[:])
                ve.drain().then_inc(S["r_ok"], 1)
                CP(run[:], region0[:])
                places, gaps = ex_f[:, 0:2 * NT], ex_c[:, 0:2 * NT, :]
                step(CP(places, slot_i[:].rearrange("p c t -> p (c t)")))
                step(TT(gaps, places.unsqueeze(2).broadcast_to([P, 2 * NT, NE - 1]),
                        region0[:, 1:NE].unsqueeze(1).broadcast_to([P, 2 * NT, NE - 1]), ALU.is_ge))
                step(TT(gaps, gaps, ntf[3][:, 0:NE - 1].unsqueeze(1).broadcast_to([P, 2 * NT, NE - 1]), ALU.mult))
                step(red(rg[:], gaps, ALU.add))
                step(TT(places, places, rg[:], ALU.subtract))
                step(CP(slot_y[:].rearrange("p c t -> p (c t)"), places))

            def period(B, kind, s, i):
                at = uses(B, kind)
                for u in range(2 * NH):
                    top(B, u)
                    if u == 0:
                        build_mask(B, 1)
                    if u == 3 and "o1" in at:
                        norm(B - 1, 1)
                    if u == 6 and "a1" in at:
                        row(at, "1", 2 * B - 1)
                    if u == 7 and "rt" in at:
                        choose(2 * B - 2, 0)
                    if u == 8 and kind != "last":
                        build_mask(B + 1, 0)
                    if u == 10 and "rt" in at:
                        place0(at, 2 * B - 2)
                    if u == 11:
                        norm(B, 0)
                    if u == 14:
                        row(at, "0", 2 * B)

            TS(region0[:], iof[:, 0:NE], float(N), None, ALU.mult)
            ve.drain()
            CP(run[:], region0[:])
            for s in range(2):
                ve.wait_ge(S2["p1w"][s], 32 * (NT // 2))
            build_mask(0, 0)
            periods(ve, period)
            norm(NB - 1, 1)
            at = uses(NB, "after")
            row(at, "1", NT - 1)
            choose(NT - 2, 0)
            place0(at, NT - 2)
            tiles()
            TT(cwt[:], m2[:], m1[:], ALU.subtract).then_inc(S["r_e"], 1)
            ve.wait_ge(S["r_exp"], 1)
            TS(m1[:], cwt[:], 1.0, None, ALU.add)
            ve.drain()
            ve.reciprocal(cw1[:], m1[:])
            ve.drain()
            TT(cw2[:], cwt[:], cw1[:], ALU.mult)
            ve.wait_ge(S["xs_sc"], 32 * NT)
            with ve.Fori(0, NTILE // 2) as i:
                for s in range(2):
                    ve.wait_ge(S2["l_mm"][s], i + 1)
                    ve.wait_ge(S2["l_st"][s], 16 * i)
                    CP(y_sb[s], ps[:, 2 + s, :]).then_inc(S2["l_ye"][s], 1)
            for s in range(2):
                ve.wait_ge(S2["l_st"][s], 16 * (NTILE // 2))

            def add_two(t, s, i, y_ready):
                ve.wait_ge(y_ready[s], 32 * i + 32)
                ve.scalar_tensor_tensor(x1[s], y1[s], cw1[:, bass.ds(t, 1)], x_row[s], ALU.mult, ALU.add)
                ve.drain()
                return ve.scalar_tensor_tensor(x1[s], y2[s], cw2[:, bass.ds(t, 1)], x1[s], ALU.mult, ALU.add)

            def make_x1(i, s):
                ve.wait_ge(S2["c_in"][s], 16 * i + 16)
                ve.memset(junk[:, 0:1], 0.0)
                if not isinstance(i, int) or i > 0:
                    ve.wait_ge(S2["c_st"][s], 16 * i)
                    ve.memset(junk[:, 1:2], 0.0)
                    ve.wait_ge(S2["c_tx"][s], i)
                    ve.memset(junk[:, 4:5], 0.0)
                add_two(2 * i + s, s, i, S2["ga_y"]).then_inc(S2["c_x1"][s], 1)

            def place1(i):
                ve.wait_ge(S["c_rt"], i + 1)
                ve.memset(junk[:, 3:4], 0.0)
                place(2 * i, ps[:, 6, 64:64 + 2 * NE], ps[:, 6, 64 + 2 * NE:64 + 4 * NE], (S["c_rtc"], 1))

            def linear(i, first, more):
                for s in range(2):
                    ve.wait_ge(S2["c_xa"][s], i + 1)
                    TS(xa_t[s], ps[:, 2 + s, 0:P], sel_b[:, bass.ds(i, 1)], None, ALU.mult).then_inc(S2["c_xe"][s], 1)
                if more:
                    make_x1(i + 1, 0)
                if not first:
                    place1(i - 1)
                if more:
                    make_x1(i + 1, 1)
                for s in range(2):
                    ve.wait_ge(S2["c_h"][s], i + 1)
                    ve.memset(junk[:, 5 + s:6 + s], 0.0)
                    CP(x2_rows[:, 2 * i + s, :], ps[:, 4 + s, :]).then_inc(S2["c_x2"][s], 1)
                    ve.wait_ge(S2["c_g"][s], i + 1)
                    CP(lg[:, s, :], ps[:, 6 + s, 0:NE]).then_inc(S2["c_lg"][s], 1)
                ve.drain()
                red(rr[:], lg[:])
                ve.drain()
                TT(lg[:], lg[:], b3(rr[:]), ALU.subtract).then_inc(S["r_l"], 1)
                ve.wait_ge(S["r_lexp"], i + 1)
                red(rr[:], lg[:], ALU.add)
                ve.drain()
                ve.reciprocal(rs2[:], rr[:])
                ve.drain()
                TT(lg[:], lg[:], b3(rs2[:]), ALU.mult)
                choose(2 * i, 1)

            make_x1(0, 0)
            make_x1(0, 1)
            linear(0, True, True)
            with ve.Fori(1, NT // 2 - 1) as i:
                linear(i, False, True)
            linear(NT // 2 - 1, False, False)
            place1(NT // 2 - 1)
            tiles()
            TT(cwt[:], m1[:], m2[:], ALU.add)
            ve.drain()
            ve.reciprocal(cw1[:], cwt[:])
            ve.drain()
            TT(cw2[:], cw1[:], m2[:], ALU.mult)
            TT(cwt[:], cw1[:], m1[:], ALU.mult)
            ve.drain()
            TT(cw1[:], cwt[:], al1[:], ALU.mult)
            TT(m2[:], cw2[:], al2[:], ALU.mult)
            ve.drain()
            CP(cw2[:], m2[:])
            ve.wait_ge(S["b1_d"], 16)
            for s in range(2):
                ve.wait_ge(S2["c_st"][s], 16 * (NT // 2))

            def layer1(i):
                es = [ve.value_load(ex_i[0:1, bass.ds(2 * i + s, 1)], min_val=0, max_val=NE - 1) for s in range(2)]
                for s in range(2):
                    ve.wait_ge(S2["k_m1"][s], i + 1)
                    TT(h_sb[s], ps[:, 2 + s, :], b1_bc[:, es[s], :], ALU.add).then_inc(S2["k_hb"][s], 1)
                if isinstance(i, int):
                    ve.wait_ge(S["b2_d"], 16)
                for s in range(2):
                    ve.wait_ge(S2["k_m2"][s], i + 1)
                    wait(ve, S2["k_st"][s], 16 * i)
                    TT(y_sb[s], ps[:, 6 + s, :], b2_bc[:, es[s], :], ALU.add).then_inc(S2["k_ye"][s], 1)
            layer1(0)
            with ve.Fori(1, NTILE // 2) as i:
                layer1(i)
            for s in range(2):
                ve.wait_ge(S2["k_st"][s], 16 * (NTILE // 2))
            with ve.Fori(0, NT // 2) as i:
                for s in range(2):
                    ve.wait_ge(S2["f_in"][s], 16 * i + 16)
                    ve.memset(junk[:, 0:1], 0.0)
                    ve.wait_ge(S2["f_st"][s], 16 * i)
                    ve.memset(junk[:, 1:2], 0.0)
                    add_two(2 * i + s, s, i, S2["fin_y"]).then_inc(S2["f_o"][s], 1)


def kernel(**inputs):
    import concourse.bacc as bacc
    from concourse.bass_utils import run_bass_kernel_spmd

    a = {k: np.asarray(v) for k, v in inputs.items()}
    t = np.ascontiguousarray
    x = a["x"].reshape(N, D)
    half = HD // 2
    wq = a["L0_cond_Wq"].reshape(2, 2, 2, HD, D).transpose(0, 2, 1, 3, 4).reshape(NH * HD, D)
    ins = {
        "x": x,
        "x_t": x.T,
        "wqkv_t": np.concatenate([wq, a["L0_cond_Wk"], a["L0_cond_Wv"]], 0).T,
        "wo_t": a["L0_cond_Wo"].T,
        "wo": a["L0_cond_Wo"],
        "w1": a["L1_cond_W"],
        "b_o": a["L1_cond_Bm"].transpose(1, 0, 2).reshape(D, NE * RANK),
        "w0_t": a["L0_ffn_W"].T,
        "kv_pool": np.stack([a["L0_cond_k_blocks"].transpose(0, 2, 1, 3), a["L0_cond_v_blocks"].transpose(0, 2, 1, 3)],
                            2).reshape(NPHYS * BLK, 2 * NG * HD),
        "table": a["itok_Bx257_0_4111"].reshape(-1),
        "lens": a["itok_B_37_3939"],
        "adapter": a["itok_B_0_6"],
        "q_gain": a["L0_cond_q_norm_scale"],
        "k_gain": a["L0_cond_k_norm_scale"],
        "inv_freq": (1.0 / THETA ** (np.arange(half) / half)).astype(np.float32),
        "gate0_t": a["L0_ffn_gate_w"].T,
        "atoms": a["L0_ffn_atoms"],
        "eaw": a["L0_ffn_expert_atom_weights"],
        "imp_t": a["L0_ffn_importance"].T,
        "mask_idx": a["L0_ffn_mask_idx"],
        "w1_t": a["L1_cond_W"].T,
        "a_t": a["L1_cond_A"].reshape(NE * RANK, D).T,
        "b_t": a["L1_cond_Bm"].transpose(0, 2, 1).reshape(NE * RANK, D),
        "scal": a["L1_cond_scalings"],
        "gate1": a["L1_ffn_gate_w"],
        "fc1": a["L1_ffn_fc1_w"],
        "b1": a["L1_ffn_fc1_b"].reshape(-1),
        "fc2": a["L1_ffn_fc2_w"],
        "b2": a["L1_ffn_fc2_b"].reshape(-1),
        "alpha": a["L1_ffn_alpha"],
    }
    nc = bacc.Bacc("TRN2", target_bir_lowering=False, num_devices=1)
    arrays, d = {}, {}
    for name, v in ins.items():
        v = t(v)
        arrays["in_" + name] = v
        d[name] = nc.dram_tensor("in_" + name, v.shape, mybir.dt.from_np(v.dtype), kind="ExternalInput").ap()
    for name, shape in (("new_kv", [N, D]), ("qn", [N, D]), ("m_buf", [CELLS + P, NE]), ("xs", [ROWS, D]),
                        ("ys", [NTILE * P, D]), ("x1", [N, D])):
        d[name] = nc.dram_tensor(name, shape, F32, kind="Internal").ap()
    d["out"] = nc.dram_tensor("out_x", [N, D], F32, kind="ExternalOutput").ap()
    program(nc, d)
    r = run_bass_kernel_spmd(nc, [arrays], core_ids=[0])
    return r.results[0]["out_x"].reshape(NB, T, D)
```

```python
import numpy as np

import concourse.bass as bass
from concourse import mybir
from contextlib import ExitStack

F32 = mybir.dt.float32
BF16 = mybir.dt.bfloat16
I32 = mybir.dt.int32
ALU = mybir.AluOpType
ACT = mybir.ActivationFunctionType
AX = mybir.AxisListType.X

P = 128
NB, T, D = 8, 256, 512
N = NB * T
NT = N // P
KC = D // P
NH, NG, HD = 8, 4, 64
BLK, NBLK = 16, 257
NPHYS = 16 * NBLK
SEQ = BLK * NBLK
WIN = 256
NJ = 2 * WIN
NC = NJ // P
KW = WIN + P
SB = NJ // BLK + 1
SW = T // BLK + 1
SCALE = 256.0 ** -0.5
RMS_EPS = 1e-6
THETA = 10000.0
NE = 8
NS = 4096
ST = NS // P
NTILE = (2 * N + NE * (P - 1)) // P
PAIRS = (NTILE + 1) // 2
BOTH, LAST = (0, 1), tuple(range(NTILE - 2 * (PAIRS - 1)))
REGION = N + P
ROWS = NE * REGION + NE * P
CELLS = D * D
MW = 3
RANK = 16
BIG = 1e30
NQK = NH + NG
QK = NQK * HD
HEADS = (0, 2, 1, 3, 4, 6, 5, 7)


def words(region, off, dims, dt=F32, parts=P):
    n = int(np.prod(dims))
    a = region[0:parts, off:off + n]
    if dt != F32:
        a = a.bitcast(dt)
    if len(dims) == 1:
        return a
    names = "abcd"[:len(dims)]
    return a.rearrange(f"p ({' '.join(names)}) -> p {' '.join(names)}",
                       **{c: int(d) for c, d in zip(names[1:], dims[1:])})


def program(nc, d):
    ctx = ExitStack()
    with ctx:
        def sb(name, shape, dt=F32):
            return ctx.enter_context(nc.sbuf_tensor(name, shape, dt))

        def sem(name):
            return ctx.enter_context(nc.semaphore(name))

        def sem2(name):
            return [sem(name + "_0"), sem(name + "_1")]

        R1 = sb("R1", [P, 16384])
        R2 = sb("R2", [P, 16384])
        R3 = sb("R3", [P, 8192])
        R4 = sb("R4", [P, 8192])
        zero = words(R1, 0, [2048])
        mask_bc = words(R1, 2048, [NS], I32)
        eq_low = words(R1, 2048, [ST, P])
        eq_all = words(R1, 6144, [ST, P])
        atoms = words(R1, 10240, [NS], F32, 64)
        imp = words(R1, 14336, [ST, NE])
        wgt = words(R1, 14592, [ST, NE])
        table_bc = words(R3, 0, [BLK + NB * NBLK + 24], I32)
        hits = words(R3, 2112, [NC * NB, NB * SW])
        jrow_i = words(R3, 6500, [NJ], I32)
        win = words(R3, 7012, [NB, SB])
        eqk = words(R3, 7276, [NB, 9])
        tmp9 = words(R3, 7348, [NB, 9])
        wr_blk = words(R3, 7420, [NB, SW])
        wr_tok = words(R3, 7556, [NB, SW])
        tile_ii = words(R3, 7700, [NTILE], I32)
        raw_wo = words(R4, 0, [KC, D])
        raw_w1 = words(R4, 2048, [KC, D])
        raw_b = words(R4, 4096, [KC, P])
        wqkv = words(R2, 0, [KC, 2 * D])
        tab_a = words(R2, 4096, [NT, 2, HD])
        tab_b = words(R2, 6144, [NT, 2, HD])
        xt = [words(R2, 8192 + 512 * s, [KC, P]) for s in range(2)] + [words(R1, 14848 + 512 * s, [KC, P]) for s in range(2)]
        sq = [words(R2, 9216, [QK]), words(R2, 14336, [QK])]
        nrm = words(R2, 9984, [QK])
        rot_a = words(R2, 10752, [QK])
        rot_b = words(R2, 11520, [QK])
        qkv_out = [words(R2, 12288 + 1024 * s, [2 * D]) for s in range(2)]
        ang = words(R2, 14336, [NT, HD // 2])
        ang2 = words(R2, 14848, [NT, HD // 2])
        sin_t = words(R2, 15360, [NT, HD // 2])
        cos_t = words(R2, 15872, [NT, HD // 2])
        k_t = [words(R2, 1024 * s, [2, NJ]) for s in range(2)]
        q_in = words(R2, 2048, [2, D])
        q_t = [words(R2, 3072 + 1024 * s, [4, T]) for s in range(2)]
        msk_s = [words(R2, 5120 + KW * s, [KW]) for s in range(2)]
        prob = [words(R2, 5888 + KW * s, [KW]) for s in range(4)]
        prob_t = [words(R2, 7424 + KW * s, [KW]) for s in range(4)]
        mask = words(R2, 8960, [2, KW])
        key_bias = words(R2, 9728, [2, KW])
        o_sb = words(R2, 10496, [D])
        o_t = words(R2, 11008, [KC, P])
        stage = words(R2, 11520, [2048])
        w_o = words(R4, 0, [KC, D])
        w0_t = words(R4, 2048, [KC, D])
        kv = [words(R4, 4096 + 2048 * s, [NC, D]) for s in range(2)]
        m_w = words(R1, 0, [KC, NE, D])
        a_rows = words(R3, 0, [NT, D])
        xs_in = [words(R3, 512 * s, [D]) for s in range(2)]
        xs_t = [words(R3, 1024 + 512 * s, [KC, P]) for s in range(2)]
        h_sb = [words(R3, 2048 + 512 * s, [D]) for s in range(2)]
        h_t = [words(R3, 3072 + 512 * s, [KC, P]) for s in range(2)]
        y_sb = [words(R3, 4096 + 512 * s, [D]) for s in range(2)]
        yb = [words(R3, 5120 + 512 * s, [D]) for s in range(2)]
        fc1 = words(R2, 0, [KC, NE, D])
        fc2 = words(R1, 0, [KC, NE, D])
        b1_bc = words(R4, 0, [NE, D])
        b2_bc = words(R4, 4096, [NE, D])
        x_row = [words(R3, 512 * s, [D]) for s in range(2)]
        y1 = [words(R3, 1024 + 512 * s, [D]) for s in range(2)]
        x1 = [words(R3, 3072 + 512 * s, [D]) for s in range(2)]
        x1_t = [words(R3, 4096 + 512 * s, [KC, P]) for s in range(2)]
        xa_t = [words(R3, 5120 + 128 * s, [P]) for s in range(2)]
        w1_t = words(R3, 5376, [KC, D])
        lora_a = words(R3, 7424, [KC, P])
        lora_b = sb("lora_b", [P, D])
        zrow = sb("zrow", [P, D // 2])
        end_i = sb("end_i", [P, NE], I32)
        x2_rows = words(R4, 0, [NT, D])

        ident = sb("ident", [P, P])
        tri = sb("tri", [P, P], BF16)
        ones = sb("ones", [P, P], BF16)
        low = sb("low", [P, P])
        band = sb("band", [P, KW], BF16)
        jrow = sb("jrow", [P, NJ], BF16)
        gate0 = sb("gate0", [P, KC, NE])
        gate1 = sb("gate1", [P, KC, NE])
        wo_g = sb("wo_g", [P, KC, NE])
        w1_g = sb("w1_g", [P, KC, NE])
        b_g = sb("b_g", [P, NE])
        lens_i = sb("lens_i", [P, NB], I32)
        ints = sb("ints", [P, 64], I32)
        lens = sb("lens", [P, NB])
        lo = sb("lo", [P, NB])
        neg_len = sb("neg_len", [P, NB])
        room = sb("room", [P, NB])
        first = sb("first", [P, NB])
        adapt_i = sb("adapt_i", [P, NB], I32)
        scal_bc = sb("scal_bc", [P, NE])
        alpha_bc = sb("alpha_bc", [P, NE])
        part = sb("part", [P, 4])
        iot = sb("iot", [P, 64], I32)
        iof = sb("iof", [P, 64])
        rev = sb("rev", [P, NE])
        sel_b = sb("sel_b", [P, NB])
        gains = sb("gains", [P, 2, HD])
        inv_f = sb("inv_f", [P, HD // 2])
        pos = sb("pos", [P, NT])
        carry = sb("carry", [P, NB])
        off = sb("off", [P, NB])
        blk = sb("blk", [P, NC, NB])
        edge = sb("edge", [P, 2, NB, NB])
        best = sb("best", [P, NC, NB])
        fidx = sb("fidx", [P, NC, NB])
        found = sb("found", [P, NC, NB])
        old_idx = sb("old_idx", [P, 2 * NB], I32)
        new_idx = sb("new_idx", [P, NC * NB], I32)
        ms_i = sb("ms_i", [P, ST], I32)
        ms_f = sb("ms_f", [P, ST])
        cell_i = sb("cell_i", [P, ST], I32)
        cell_j = sb("cell_j", [P, ST], I32)
        cell_f = sb("cell_f", [P, ST])
        dup = sb("dup", [P, ST])
        eaw = sb("eaw", [NE, 64])
        eaw_s = sb("eaw_s", [NE, 4])
        eaw_t = sb("eaw_t", [64, NE])
        tot = sb("tot", [P, ST, NE])
        ss = sb("ss", [P, 2, NQK])
        rstd = sb("rstd", [P, 2, NQK])
        root = sb("root", [P, 2, NQK])
        mx = sb("mx", [P, 16])
        nmx = sb("nmx", [P, 16])
        sums = sb("sums", [P, 16])
        rsum = sb("rsum", [P, NH])
        junk = sb("junk", [P, 16])
        junk_a = sb("junk_a", [P, 4])
        lg = sb("lg", [P, 2, NE])
        t1 = sb("t1", [P, 2, NE])
        t2 = sb("t2", [P, 2, NE])
        chosen_e = sb("chosen_e", [P, 2, 2, NE])
        t3 = dup[:].rearrange("p (c t e) -> p c t e", c=2, t=2)
        rr = sb("rr", [P, 2])
        rs2 = sb("rs2", [P, 2])
        best2 = sb("best2", [P, 2, 2])
        diff = sb("diff", [P, 2])
        al = sb("al", [P, 2, 2])
        meta = sb("meta", [P, 2, NT, MW])
        meta_in = sb("meta_in", [P, 2, MW])
        ew = sb("ew", [P, 2, 2])
        tok_f = sb("tok_f", [P, 2])
        w_row = sb("w_row", [P, 2])
        tok_i = sb("tok_i", [P, 2], I32)
        selb16 = sb("selb16", [P, 2, NE], BF16)
        run = sb("run", [P, NE])
        region0 = sb("region0", [P, NE])
        nti = sb("nti", [P, NE], I32)
        ntf = [sb(f"ntf{i}", [P, NE]) for i in range(4)]
        slot_f = sb("slot_f", [P, 2, 2])
        slot_i = sb("slot_i", [P, 2, NT], I32)
        ex_c = sb("ex_c", [P, NTILE, NE])
        ex_f = sb("ex_f", [P, NTILE])
        ex_i = sb("ex_i", [P, NTILE], I32)
        row_i = sb("row_i", [P, NTILE], I32)
        tile_io = sb("tile_io", [P, NTILE])

        ps = ctx.enter_context(nc.psum_tensor("ps", [P, 8, 512], F32))

        def bank(b, dims=None):
            a = ps[:, b, :]
            if dims is None:
                return a
            n = int(np.prod(dims))
            a = ps[:, b, 0:n]
            if len(dims) == 1:
                return a
            return a.rearrange("p (a b) -> p a b", b=int(dims[-1]))

        S = {}
        for name in ("rope_d p0_dma sparse_d w_qkv raw_dma consts zero_ok eqa eql rope_in rope_r rope_ok idx_ok eaw_in imp_s eaw_ok eaw_p eaw_c "
                     "delta wgt_ok tot_p cell_ok pre_w pre_c zdone r_end zrows mscat "
                     "s_dot s_mx s_exp s_pt s_pe s_pv s_norm mstage m_done att_w q_ld "
                     "r_sel r_slot r_ok l_ex l_mi k_mi l_mt k_mt r_l r_lexp acc_z xs_sc x2_sc x2_sc2 mt_sc mt2_sc w5 b1_d b2_d fc1_d fc2_d c_rt c_rtc outs").split():
            S[name] = sem(name)
        S2 = {}
        for name in ("bk bc ssd rec root p1o p1w kvd kvc "
                     "l_in l_tx l_xt l_mm l_ye l_st k_in k_tx k_xt k_m1 k_hb k_hg k_th k_ht k_m2 k_ye k_yb k_st "
                     "c_in c_x1 c_tx c_xt c_xa c_xe c_h c_x2 c_g c_lg c_st").split():
            S2[name] = sem2(name)
        S4 = {name: [sem(f"{name}_{i}") for i in range(4)] for name in ("x_in", "qkv", "a1", "p1p")}

        def wait(eng, semaphore, value):
            if not isinstance(value, int) or value > 0:
                eng.wait_ge(semaphore, value)

        ORDER = (("o1", 0), ("a1", 1), ("g1", 0), ("q0", 0), ("q1", 1), ("k0", 0), ("k1", 1), ("rt", 1),
                 ("o0", 0), ("a0", 1), ("g0", 0))
        KINDS = {"first": ("q0", "q1", "k0", "k1", "o0", "a0", "g0"),
                 "mid": tuple(x for x, _ in ORDER),
                 "last": ("o1", "a1", "g1", "rt", "o0", "a0", "g0"),
                 "after": ("o1", "a1", "g1", "rt")}

        def uses(B, kind):
            base = {"first": (2, 2), "mid": (6 * B, 5 * B), "last": (6 * B, 5 * B), "after": (6 * NB - 2, 5 * NB - 2)}[kind]
            n, out = [0, 0], {}
            for x, bk in ORDER:
                if x in KINDS[kind]:
                    out[x] = (bk, base[bk] + n[bk])
                    n[bk] += 1
            return out

        def periods(eng, period):
            period(0, "first", 0, 0)
            with eng.Fori(0, NB // 2 - 1) as i:
                period(2 * i + 1, "mid", 1, i)
                period(2 * i + 2, "mid", 0, i)
            period(NB - 1, "last", 1, 0)

        block = ctx.enter_context(nc.Block())

        @block.sync
        def _(sp):
            for dst, src in (
                    (lens_i[:], d["lens"].partition_broadcast(P)),
                    (inv_f[:], d["inv_freq"].partition_broadcast(P)),
                    (gains[:, 0, :], d["q_gain"].partition_broadcast(P)),
                    (gains[:, 1, :], d["k_gain"].partition_broadcast(P))):
                sp.dma_start(dst, src).then_inc(S["rope_d"], 16)
            for dst, src in (
                    (table_bc[:, BLK:BLK + NB * NBLK], d["table"].partition_broadcast(P)),
                    (adapt_i[:], d["adapter"].partition_broadcast(P)),
                    (scal_bc[:], d["scal"].partition_broadcast(P)),
                    (alpha_bc[:], d["alpha"].partition_broadcast(P)),
                    (ms_i[:], d["mask_idx"].rearrange("(p t) -> p t", t=ST)),
                    (eaw[:], d["eaw"])):
                sp.dma_start(dst, src).then_inc(S["p0_dma"], 16)
            sp.wait_ge(S["w_qkv"], 16)
            for dst, src in (
                    (imp, d["imp_t"].rearrange("(p t) e -> p t e", t=ST)),
                    (mask_bc, d["mask_idx"].partition_broadcast(P)),
                    (atoms, d["atoms"])):
                sp.dma_start(dst, src).then_inc(S["sparse_d"], 16)
            chunked = "(k p) n -> p k n"
            xt_v = d["x_t"].rearrange("(k p) (t m) -> p k t m", p=P, m=P)
            qn_v = d["qn"].rearrange("(t p) n -> p t n", p=P)
            np_v = d["new_kv"].rearrange("(t p) n -> p t n", p=P)

            def load_x(t, s):
                sp.dma_start(xt[s], xt_v[:, :, t, :]).then_inc(S4["x_in"][s], 16)

            def store_qkv(t, s):
                sp.dma_start(np_v[:, t, :], qkv_out[s][:, D:2 * D]).then_inc(S2["p1w"][s], 16)
                sp.dma_start(qn_v[:, t, :], qkv_out[s][:, 0:D]).then_inc(S2["p1w"][s], 16)

            sp.wait_ge(S["zero_ok"], 1)
            mb = d["m_buf"][0:CELLS, :].rearrange("(p a) e -> p (a e)", p=P)
            for i in range(8):
                sp.dma_start(mb[:, 2048 * i:2048 * (i + 1)], zero).then_inc(S["zdone"], 16)
            sp.dma_start(d["m_buf"][CELLS:CELLS + P, :], zero[:, 0:NE]).then_inc(S["zdone"], 16)
            for x in range(2):
                sp.dma_start(d[f"meta{x}"].rearrange("(p a) n -> p (a n)", p=P), zero[:, 0:ROWS // P * MW]
                             ).then_inc(S["zdone"], 16)
            sp.dma_start(d["xs"][NE * REGION:ROWS, :].rearrange("(p a) n -> p a n", p=P),
                         zero[:, 0:D].unsqueeze(1).broadcast_to([P, NE, D])).then_inc(S["zdone"], 16)
            with sp.Fori(0, NT // 4 - 1) as i:
                for s in range(4):
                    sp.wait_ge(S4["qkv"][s], i + 1)
                    load_x(4 * i + 4 + s, s)
                    sp.wait_ge(S2["p1o"][s % 2], 2 * i + s // 2 + 1)
                    store_qkv(4 * i + s, s % 2)
            for s in range(4):
                sp.wait_ge(S2["p1o"][s % 2], NT // 2 - 1 + s // 2)
                store_qkv(NT - 4 + s, s % 2)

            sp.wait_ge(S["pre_w"], 1)
            sp.dma_start(w_o, d["wo_t"].rearrange(chunked, p=P)).then_inc(S["att_w"], 16)
            sp.dma_start(w0_t, d["w0_t"].rearrange(chunked, p=P)).then_inc(S["att_w"], 16)
            for s in range(2):
                sp.wait_ge(S2["p1w"][s], 32 * (NT // 2))
            qb_v = d["qn"].rearrange("(b t p) n -> p b t n", t=2, p=P)
            sp.dma_start(q_in, qb_v[:, 0, :, :]).then_inc(S["q_ld"], 16)
            sp.wait_ge(S2["bk"][1], 1)
            sp.dma_start(q_in, qb_v[:, 1, :, :]).then_inc(S["q_ld"], 16)
            whole = "(p a) n -> p (a n)"
            sp.dma_start(d["acc0"].rearrange(whole, p=P), d["x"].rearrange(whole, p=P)).then_inc(S["acc_z"], 16)
            sp.dma_start(d["acc1"].rearrange("(p a) n -> p a n", p=P).rearrange("p (c e) n -> p c (e n)", e=4),
                         zero.unsqueeze(1).broadcast_to([P, NT // 4, 2048])).then_inc(S["acc_z"], 16)
            with sp.Fori(0, NB - 2) as b:
                sp.wait_ge(S2["bk"][1], 5 * b + 3)
                sp.dma_start(q_in, qb_v[:, b + 2, :, :]).then_inc(S["q_ld"], 16)
            def zero_ends(n):
                sp.wait_ge(S["r_end"], n)
                for e in range(NE):
                    end = sp.value_load(end_i[0:1, e:e + 1], min_val=0, max_val=ROWS - P * NE)
                    sp.dma_start(d["xs"][bass.ds(end, P), :].rearrange("p (h n) -> p h n", h=2),
                                 zrow[:].unsqueeze(1).broadcast_to([P, 2, D // 2])).then_inc(S["zrows"], 16)
                sp.wait_ge(S["zrows"], 16 * NE * n)

            def expert_io(meta_d, load, read, meta_sent, meta_load, meta_read):
                def fetch(row, s):
                    sp.dma_start(xs_in[s], d["xs"][bass.ds(row, P), :]).then_inc(load[s], 16)

                def fetch_meta(row, s):
                    sp.dma_start(meta_in[:, s, :], meta_d[bass.ds(row, P), :]).then_inc(meta_load, 16)

                def rows_of(t, slots=BOTH):
                    return [sp.value_load(row_i[0:1, bass.ds(t + s, 1)], min_val=0, max_val=ROWS - P) for s in slots]

                def following(i, slots):
                    rows = rows_of(2 * i + 2, slots)
                    for s in slots:
                        sp.wait_ge(read[s], i + 1)
                        fetch(rows[s], s)
                    sp.wait_ge(meta_read, i + 1)
                    for s in slots:
                        fetch_meta(rows[s], s)

                rows = rows_of(0)
                for s in range(2):
                    fetch(rows[s], s)
                sp.wait_ge(meta_sent, 32 * NT)
                for s in range(2):
                    fetch_meta(rows[s], s)
                yield
                with sp.Fori(0, PAIRS - 2) as i:
                    following(i, BOTH)
                following(PAIRS - 2, LAST)

            zero_ends(1)
            sp.wait_ge(S["r_ok"], 1)
            sp.wait_ge(S["xs_sc"], 32 * NT)
            io = expert_io(d["meta0"], S2["l_in"], S2["l_tx"], S["mt_sc"], S["l_mi"], S["l_mt"])
            next(io)
            for _ in io:
                pass

            acc_v = [d[f"acc{x}"].rearrange("(t p) n -> p t n", p=P) for x in range(2)]
            out_v = d["out"].rearrange("(t p) n -> p t n", p=P)

            def load_sums(t, s):
                sp.dma_start(x_row[s], acc_v[0][:, t, :]).then_inc(S2["c_in"][s], 16)
                sp.dma_start(y1[s], acc_v[1][:, t, :]).then_inc(S2["c_in"][s], 16)

            for s in range(2):
                sp.wait_ge(S2["l_st"][s], 16 * ((NTILE + 1 - s) // 2))
            for s in range(2):
                load_sums(s, s)
            def x_io(c0, c1):
                with sp.Fori(c0, c1) as i:
                    for s in range(2):
                        sp.wait_ge(S2["c_x1"][s], i + 1)
                        load_sums(2 * i + 2 + s, s)
                        sp.dma_start(out_v[:, 2 * i + s, :], x1[s]).then_inc(S2["c_st"][s], 16)

            x_io(0, NT // 2 - 1)
            for s in range(2):
                sp.wait_ge(S2["c_x1"][s], NT // 2)
                sp.dma_start(out_v[:, NT - 2 + s, :], x1[s]).then_inc(S2["c_st"][s], 16)
            for s in range(2):
                sp.wait_ge(S2["c_tx"][s], NT // 2)
            zero_ends(2)
            sp.wait_ge(S["r_ok"], 2)
            sp.wait_ge(S["x2_sc2"], 16 * NT)
            io = expert_io(d["meta1"], S2["k_in"], S2["k_tx"], S["mt2_sc"], S["k_mi"], S["k_mt"])
            next(io)
            sp.dma_start(b2_bc, d["b2"].partition_broadcast(P)).then_inc(S["b2_d"], 16)
            for _ in io:
                pass

        @block.gpsimd
        def _(po):
            po.iota(iot[:, 0:32], [[1, 32]], base=0, channel_multiplier=0)
            po.iota(iot[:, 32:33], [[0, 1]], base=0, channel_multiplier=1)
            po.iota(tile_ii, [[1, NTILE]], base=0, channel_multiplier=0)
            po.iota(jrow_i, [[1, NJ]], base=-WIN, channel_multiplier=0)
            po.memset(ident[:], 0.0)
            po.memset(table_bc[:, 0:BLK], 0)
            po.memset(table_bc[:, BLK + NB * NBLK:], 0)
            po.drain()
            po.affine_select(out=ident[:], in_=ident[:], compare_op=ALU.not_equal, fill=1.0, base=0,
                             pattern=[[-1, P]], channel_multiplier=1)
            po.drain().then_inc(S["consts"], 1)
            po.memset(zero, 0.0)
            po.memset(zrow[:], 0.0)
            po.drain().then_inc(S["zero_ok"], 1)
            po.memset(tri[:], 1.0)
            po.memset(ones[:], 1.0)
            po.memset(low[:], 1.0)
            po.memset(band[:], 0.0)
            po.drain()
            po.affine_select(out=tri[:], in_=tri[:], compare_op=ALU.is_gt, fill=0.0, base=0,
                             pattern=[[1, P]], channel_multiplier=-1)
            po.affine_select(out=low[:], in_=low[:], compare_op=ALU.is_gt, fill=0.0, base=0,
                             pattern=[[-1, P]], channel_multiplier=1)
            po.affine_select(out=band[:], in_=band[:], compare_op=ALU.is_gt, fill=1.0, base=0,
                             pattern=[[1, KW]], channel_multiplier=-1)
            po.drain()
            po.affine_select(out=band[:], in_=band[:], compare_op=ALU.is_ge, fill=1.0, base=WIN,
                             pattern=[[-1, KW]], channel_multiplier=1)
            po.drain().then_inc(S["consts"], 1)
            po.wait_ge(S["eqa"], 1)
            po.tensor_tensor(eq_low, eq_all, low[:].unsqueeze(1).broadcast_to([P, ST, P]), ALU.mult).then_inc(S["eql"], 1)

            def old_rows(b):
                for c in range(2):
                    col = c * NB + b
                    po.indirect_dma_start(out=kv[b % 2][:, c, :], out_offset=None, in_=d["kv_pool"],
                                          in_offset=bass.IndirectOffsetOnAxis(ap=old_idx[:, col:col + 1], axis=0)
                                          ).then_inc(S2["kvc"][b % 2], 16)

            def new_rows(b):
                for c in (2, 3):
                    col = c * NB + b
                    po.indirect_dma_start(out=kv[b % 2][:, c, :], out_offset=None, in_=d["new_kv"],
                                          in_offset=bass.IndirectOffsetOnAxis(ap=new_idx[:, col:col + 1], axis=0)
                                          ).then_inc(S2["kvd"][b % 2], 16)
                po.wait_ge(S2["kvc"][b % 2], 32 * (b // 2 + 1))
                for c in range(2):
                    col = c * NB + b
                    po.indirect_dma_start(out=kv[b % 2][:, c, :], out_offset=None, in_=d["new_kv"],
                                          in_offset=bass.IndirectOffsetOnAxis(ap=new_idx[:, col:col + 1], axis=0),
                                          bounds_check=N - 1, oob_is_err=False).then_inc(S2["kvd"][b % 2], 16)

            def scatter(rows, meta_d, b, n, done, meta_done):
                po.wait_ge(S["r_slot"], n)
                for dst, src, signal in ((d["xs"], lambda t, c: rows[:, t, :], done), (meta_d, lambda t, c: meta[:, c, t, :], meta_done)):
                    for t in (2 * b, 2 * b + 1):
                        for c in range(2):
                            po.indirect_dma_start(out=dst,
                                                  out_offset=bass.IndirectOffsetOnAxis(ap=slot_i[:, c, t:t + 1], axis=0),
                                                  in_=src(t, c), in_offset=None).then_inc(signal, 16)

            po.wait_ge(S["idx_ok"], 1)
            po.wait_ge(S["pre_w"], 1)
            for b in range(2):
                old_rows(b)
            for s in range(2):
                po.wait_ge(S2["p1w"][s], 32 * (NT // 2))
            for b in range(2):
                new_rows(b)
            po.wait_ge(S["cell_ok"], 1)
            po.wait_ge(S["zdone"], 16 * 12)
            mst = d["m_buf"][0:CELLS, :].rearrange("(k p r) e -> p k (r e)", k=KC, p=P)
            for b in range(NB):
                if 2 <= b + 1 < NB:
                    po.wait_ge(S["s_pv"], 16 * b)
                    old_rows(b + 1)
                    new_rows(b + 1)
                if b < NB // 2:
                    for t in range(b * ST // 4, (b + 1) * ST // 4):
                        if t:
                            po.wait_ge(S["mscat"], 16 * t)
                        po.indirect_dma_start(out=d["m_buf"],
                                              out_offset=bass.IndirectOffsetOnAxis(ap=cell_i[:, t:t + 1], axis=0),
                                              in_=tot[:, t, :], in_offset=None, compute_op=ALU.add
                                              ).then_inc(S["mscat"], 16)
                if b == NB // 2 - 1:
                    po.wait_ge(S["mscat"], 16 * ST)
                    po.wait_ge(S["att_w"], 32)
                    po.wait_ge(S["tot_p"], 1)
                    po.dma_start(stage, mst[:, KC - 1, 0:2048]).then_inc(S["mstage"], 16)
                if b >= NB // 2:
                    for m in range(2 * (b - NB // 2), 2 * (b - NB // 2) + 2):
                        k, r = KC - 1 - m // 2, 256 * (m % 2)
                        if m == 2 * KC - 2:
                            po.wait_ge(S["acc_z"], 32)
                        po.wait_ge(S["mstage"], 16 * (m + 1))
                        po.tensor_tensor(m_w[:, k, :, r:r + 256], stage.rearrange("p (r e) -> p e r", e=NE),
                                         w0_t[:, k, r:r + 256].unsqueeze(1).broadcast_to([P, NE, 256]), ALU.add
                                         ).then_inc(S["m_done"], 1)
                        if m + 1 < 2 * KC:
                            m += 1
                            po.wait_ge(S["m_done"], m)
                            po.dma_start(stage, mst[:, KC - 1 - m // 2, 2048 * (m % 2):2048 * (m % 2 + 1)]
                                         ).then_inc(S["mstage"], 16)
                if b >= 1:
                    scatter(a_rows, d["meta0"], b - 1, b, S["xs_sc"], S["mt_sc"])
            scatter(a_rows, d["meta0"], NB - 1, NB, S["xs_sc"], S["mt_sc"])
            def accumulate(sums, made, stored):
                for t in range(NTILE):
                    s = t % 2
                    if t and sums[0] is sums[1]:
                        po.wait_ge(stored[1 - s], 16 * ((t + 1) // 2))
                    elif t > 1:
                        po.wait_ge(stored[s], 16 * (t // 2))
                    po.wait_ge(made[s], t // 2 + 1)
                    po.indirect_dma_start(out=sums[s],
                                          out_offset=bass.IndirectOffsetOnAxis(ap=tok_i[:, s:s + 1], axis=0),
                                          in_=y_sb[s], in_offset=None, bounds_check=N - 1, oob_is_err=False,
                                          compute_op=ALU.add).then_inc(stored[s], 16)

            po.wait_ge(S["acc_z"], 32)
            accumulate((d["acc0"], d["acc1"]), S2["l_ye"], S2["l_st"])
            for b in range(NB):
                if b == NB - 2:
                    po.wait_ge(S["x2_sc"], 16 * NT)
                    po.dma_start(b1_bc, d["b1"].partition_broadcast(P)).then_inc(S["b1_d"], 16)
                for s in range(2):
                    po.wait_ge(S2["c_x2"][s], b + 1)
                scatter(x2_rows, d["meta1"], b, NB + b + 1, S["x2_sc" if b < NB // 2 else "x2_sc2"], S["mt2_sc"])
            for s in range(2):
                po.wait_ge(S2["c_st"][s], 16 * (NT // 2))
            accumulate((d["out"], d["out"]), S2["k_ye"], S2["k_st"])
            for s in range(2):
                po.wait_ge(S2["k_st"][s], 16 * ((NTILE + 1 - s) // 2))

        @block.tensor
        def _(pe):
            def chunks(out, lhs, rhs, first=True, last=True):
                for k in range(KC):
                    m = pe.matmul(out, lhs(k), rhs(k), start=(k == 0 and first), stop=(k == KC - 1 and last))
                return m

            def turn4(out, src):
                for k in range(KC):
                    m = pe.transpose(out[:, k * P:(k + 1) * P], src[:, k * P:(k + 1) * P], ident[:])
                return m

            pe.wait_ge(S["consts"], 1)
            pe.wait_ge(S["raw_dma"], 16 * 5)
            for k in range(KC):
                chunks(ps[:, 7, k * NE:(k + 1) * NE], lambda o: raw_wo[:, o, k * P:(k + 1) * P], lambda o: gate0[:, o, :])
                chunks(ps[:, 7, 64 + k * NE:64 + (k + 1) * NE], lambda o: raw_w1[:, o, k * P:(k + 1) * P],
                       lambda o: gate1[:, o, :])
            chunks(ps[:, 7, 128:128 + NE], lambda o: raw_b[:, o, :], lambda o: gate1[:, o, :]).then_inc(S["pre_w"], 1)
            pe.wait_ge(S["w_qkv"], 16)
            with pe.Fori(0, NT // 4) as i:
                for s in range(4):
                    pe.wait_ge(S4["x_in"][s], 16 * i + 16)
                    pe.wait_ge(S4["p1p"][s], i)
                    if s == 3:
                        pe.wait_ge(S["pre_c"], 1)
                    for h in range(2):
                        m = chunks(ps[:, 2 * s + h, :], lambda k: xt[s][:, k, :], lambda k: wqkv[:, k, h * D:(h + 1) * D])
                    m.then_inc(S4["qkv"][s], 1)
            pe.wait_ge(S["eaw_ok"], 1)
            for s in range(2):
                pe.wait_ge(S4["p1p"][s], NT // 4)
            pe.transpose(ps[0:64, 2, 0:NE], eaw[:], ident[0:NE, 0:NE]).then_inc(S["eaw_p"], 1)
            pe.wait_ge(S["eaw_c"], 1)
            at_v = atoms.rearrange("a (p t) -> a t p", t=ST)
            for t in range(ST):
                m = pe.matmul(ps[:, 2, t * NE:(t + 1) * NE], at_v[:, t, :], eaw_t[:], start=True, stop=True)
            m.then_inc(S["delta"], 1)
            pe.wait_ge(S["wgt_ok"], 1)
            for t in range(ST):
                m = pe.matmul(ps[:, 3, t * NE:(t + 1) * NE], eq_all[:, t, :], wgt[:, t, :], start=True, stop=True)
            m.then_inc(S["tot_p"], 1)
            bk, bc = S2["bk"], S2["bc"]

            def turn_q(s, banks):
                for qt in range(2):
                    b, n = banks[qt]
                    wait(pe, bc[b], n)
                    turn4(ps[:, b, :], q_in[:, qt, :]).then_inc(bk[b], 1)

            def turn_k(s, banks):
                for p in range(2):
                    b, n = banks[p]
                    wait(pe, bc[b], n)
                    for c in range(NC):
                        m = pe.transpose(ps[:, b, c * P:(c + 1) * P], kv[s][:, c, p * P:(p + 1) * P], ident[:])
                    m.then_inc(bk[b], 1)

            def dots(B, u, s):
                qt, h = u // NH, HEADS[u % NH]
                g = h // 2
                base, p, jj = 64 * (g % 2), g // 2, (g // 2) * 2 + h % 2
                wait(pe, S["s_mx"], 16 * B + u - 1)
                pe.matmul(ps[:, 2 + u % 2, 0:KW], q_t[s][base:base + 64, jj, qt * P:(qt + 1) * P],
                          k_t[s][base:base + 64, p, qt * P:qt * P + KW], start=True, stop=True).then_inc(S["s_dot"], 1)

            def turn_p(B, u):
                wait(pe, S["s_exp"], 16 * B + u + 1)
                wait(pe, S["s_pe"], 16 * B + u - 1)
                for c in range(3):
                    m = pe.transpose(ps[:, 4 + u % 2, c * P:(c + 1) * P], prob[u % 4][:, c * P:(c + 1) * P], ident[:])
                m.then_inc(S["s_pt"], 1)

            def mix(B, u, s):
                qt, h = u // NH, HEADS[u % NH]
                wait(pe, S["s_pe"], 16 * B + u + 1)
                if u % NH == 0:
                    wait(pe, S["s_norm"], 2 * B + qt - 1)
                for c in range(3):
                    m = pe.matmul(ps[:, 6 + qt, h * HD:(h + 1) * HD], prob_t[u % 4][:, c * P:(c + 1) * P],
                                  kv[s][:, qt + c, (NG + h // 2) * HD:(NG + h // 2 + 1) * HD], start=(c == 0), stop=(c == 2))
                m.then_inc(S["s_pv"], 1)

            def tail(at, x, norms):
                b, n = at["o" + x]
                wait(pe, S["s_norm"], norms)
                wait(pe, bc[b], n)
                turn4(ps[:, b, :], o_sb).then_inc(bk[b], 1)

            def project(at, x):
                b, n = at["a" + x]
                wait(pe, bc[0], at["o" + x][1] + 1)
                wait(pe, bc[b], n)
                chunks(ps[:, b, :], lambda k: o_t[:, k, :], lambda k: w_o[:, k, :]).then_inc(bk[b], 1)
                b, n = at["g" + x]
                chunks(ps[:, b, 0:NE], lambda k: o_t[:, k, :], lambda k: wo_g[:, k, :]).then_inc(bk[b], 1)

            def count(at, n):
                b, m = at["rt"]
                wait(pe, S["r_sel"], n)
                wait(pe, bc[b], m)
                sel = selb16[:].rearrange("p t e -> p (t e)")
                pe.matmul(ps[:, b, 0:2 * NE], tri[:], sel, start=True, stop=True)
                pe.matmul(ps[:, b, 2 * NE:4 * NE], ones[:], sel, start=True, stop=True).then_inc(bk[b], 1)

            def period(B, kind, s, i):
                at = uses(B, kind)
                for u in range(2 * NH):
                    if u == 0:
                        wait(pe, bc[0], 6 * B - 2 if kind != "first" else 2)
                        wait(pe, bc[1], 5 * B - 1 if kind != "first" else 2)
                    dots(B, u, s)
                    if u >= 2 or kind != "first":
                        turn_p(B if u >= 2 else B - 1, (u - 2) % 16)
                    if u >= 3 or kind != "first":
                        mix(B if u >= 3 else B - 1, (u - 3) % 16, s if u >= 3 else 1 - s)
                    if u == 5 and "o1" in at:
                        tail(at, "1", 2 * B)
                    if u == 6 and "a1" in at:
                        project(at, "1")
                    if u == 7 and "q0" in at:
                        wait(pe, S["q_ld"], 16 * (B + 2))
                        turn_q(1 - s, (at["q0"], at["q1"]))
                    if u == 12 and "rt" in at:
                        count(at, B)
                    if u == 10 and "k0" in at:
                        wait(pe, S2["kvd"][1 - s], 64 * (i + 2) if kind != "first" else 64)
                        turn_k(1 - s, (at["k0"], at["k1"]))
                    if u == 13:
                        tail(at, "0", 2 * B + 1)
                    if u == 14:
                        project(at, "0")

            pe.wait_ge(S["q_ld"], 16)
            turn_q(0, ((0, 0), (1, 0)))
            pe.wait_ge(S2["kvd"][0], 64)
            turn_k(0, ((0, 1), (1, 1)))
            pe.wait_ge(S["att_w"], 32)
            pe.wait_ge(S["cell_ok"], 1)
            periods(pe, period)
            turn_p(NB - 1, 14)
            mix(NB - 1, 13, 1)
            turn_p(NB - 1, 15)
            mix(NB - 1, 14, 1)
            mix(NB - 1, 15, 1)
            at = uses(NB, "after")
            tail(at, "1", 2 * NB)
            project(at, "1")
            count(at, NB)
            pe.wait_ge(S["r_ok"], 1)
            pe.wait_ge(S["m_done"], NB)

            def turn_x(load, done, turned, i, s):
                pe.wait_ge(load[s], 16 * i + 16)
                wait(pe, done[s], i)
                turn4(ps[:, s, :], xs_in[s]).then_inc(turned[s], 1)

            def layer0(i, now, after):
                es = [pe.value_load(ex_i[0:1, bass.ds(2 * i + s, 1)], min_val=0, max_val=NE - 1) for s in now]
                for s in now:
                    pe.wait_ge(S2["l_xt"][s], i + 1)
                    wait(pe, S2["l_ye"][s], i)
                    chunks(ps[:, 2 + s, :], lambda k: xs_t[s][:, k, :], lambda k: m_w[:, k, es[s], :]
                           ).then_inc(S2["l_mm"][s], 1)
                    if s in after:
                        turn_x(S2["l_in"], S2["l_xt"], S2["l_tx"], i + 1, s)

            for s in range(2):
                turn_x(S2["l_in"], S2["l_xt"], S2["l_tx"], 0, s)
            with pe.Fori(0, PAIRS - 2) as i:
                layer0(i, BOTH, BOTH)
            layer0(PAIRS - 2, BOTH, LAST)
            layer0(PAIRS - 1, LAST, ())

            pe.wait_ge(S["w5"], 48)

            def turn_x1(i, s):
                pe.wait_ge(S2["c_x1"][s], i + 1)
                wait(pe, S2["c_xt"][s], i)
                turn4(ps[:, s, :], x1[s]).then_inc(S2["c_tx"][s], 1)

            def count1(n, more=True):
                wait(pe, S["r_sel"], NB + n)
                wait(pe, S2["c_xe"][1], n + 1 if more else n)
                sel = selb16[:].rearrange("p t e -> p (t e)")
                pe.matmul(ps[:, 3, P:P + 2 * NE], tri[:], sel, start=True, stop=True)
                pe.matmul(ps[:, 3, P + 2 * NE:P + 4 * NE], ones[:], sel, start=True, stop=True).then_inc(S["c_rt"], 1)

            def linear(i, first, more):
                for s in range(2):
                    pe.wait_ge(S2["c_xt"][s], i + 1)
                    wait(pe, S2["c_xe"][s], i)
                    if s == 1 and not first:
                        wait(pe, S["c_rtc"], i - 1)
                    chunks(ps[:, 2 + s, 0:P], lambda k: lora_a[:, k, :], lambda k: x1_t[s][:, k, :]).then_inc(S2["c_xa"][s], 1)
                for s in range(2):
                    wait(pe, S2["c_x2"][s], i)
                    chunks(ps[:, 4 + s, :], lambda k: x1_t[s][:, k, :], lambda k: w1_t[:, k, :], last=False)
                    if s == 1 and not first:
                        count1(i)
                    pe.wait_ge(S2["c_xe"][s], i + 1)
                    pe.matmul(ps[:, 4 + s, :], xa_t[s], lora_b[:], start=False, stop=True).then_inc(S2["c_h"][s], 1)
                    wait(pe, S2["c_lg"][s], i)
                    chunks(ps[:, 6 + s, 0:NE], lambda k: x1_t[s][:, k, :], lambda k: w1_g[:, k, :], last=False)
                    pe.matmul(ps[:, 6 + s, 0:NE], xa_t[s], b_g[:], start=False, stop=True).then_inc(S2["c_g"][s], 1)
                    if more:
                        turn_x1(i + 1, s)

            for s in range(2):
                turn_x1(0, s)
            linear(0, True, True)
            with pe.Fori(1, NT // 2 - 1) as i:
                linear(i, False, True)
            linear(NT // 2 - 1, False, False)
            count1(NT // 2, False)
            pe.wait_ge(S["r_ok"], 2)
            pe.wait_ge(S["fc1_d"], 32 * KC)
            pe.wait_ge(S["fc2_d"], 32 * KC)

            def layer1(i, now, after):
                es = [pe.value_load(ex_i[0:1, bass.ds(2 * i + s, 1)], min_val=0, max_val=NE - 1) for s in now]
                for s in now:
                    pe.wait_ge(S2["k_xt"][s], i + 1)
                    wait(pe, S2["k_hb"][s], i)
                    chunks(ps[:, 2 + s, :], lambda k: xs_t[s][:, k, :], lambda k: fc1[:, k, es[s], :]
                           ).then_inc(S2["k_m1"][s], 1)
                for s in now:
                    pe.wait_ge(S2["k_hg"][s], i + 1)
                    wait(pe, S2["k_ht"][s], i)
                    turn4(ps[:, 4 + s, :], h_sb[s]).then_inc(S2["k_th"][s], 1)
                    if s in after:
                        turn_x(S2["k_in"], S2["k_xt"], S2["k_tx"], i + 1, s)
                for s in now:
                    pe.wait_ge(S2["k_ht"][s], i + 1)
                    wait(pe, S2["k_yb"][s], i)
                    chunks(ps[:, 6 + s, :], lambda k: h_t[s][:, k, :], lambda k: fc2[:, k, es[s], :]
                           ).then_inc(S2["k_m2"][s], 1)

            for s in range(2):
                turn_x(S2["k_in"], S2["k_xt"], S2["k_tx"], 0, s)
            with pe.Fori(0, PAIRS - 2) as i:
                layer1(i, BOTH, BOTH)
            layer1(PAIRS - 2, BOTH, LAST)
            layer1(PAIRS - 1, LAST, ())

        @block.scalar
        def _(ac):
            chunked = "(k p) n -> p k n"
            ac.dma_start(gate0[:], d["gate0_t"].rearrange(chunked, p=P)).then_inc(S["raw_dma"], 16)
            ac.dma_start(gate1[:], d["gate1"].rearrange(chunked, p=P)).then_inc(S["raw_dma"], 16)
            ac.dma_start(raw_wo, d["wo"].rearrange(chunked, p=P)).then_inc(S["raw_dma"], 16)
            ac.dma_start(raw_w1, d["w1"].rearrange(chunked, p=P)).then_inc(S["raw_dma"], 16)
            ac.dma_start(raw_b, d["b_o"].rearrange(chunked, p=P)).then_inc(S["raw_dma"], 16)
            ac.dma_start(wqkv, d["wqkv_t"].rearrange(chunked, p=P)).then_inc(S["w_qkv"], 16)
            xt_v = d["x_t"].rearrange("(k p) (t m) -> p k t m", p=P, m=P)
            for s in range(4):
                ac.dma_start(xt[s], xt_v[:, :, s, :]).then_inc(S4["x_in"][s], 16)
            ac.wait_ge(S["rope_in"], 1)
            ac.activation(sin_t.rearrange("p a b -> p (a b)"), ang.rearrange("p a b -> p (a b)"), ACT.Sin)
            ac.activation(cos_t.rearrange("p a b -> p (a b)"), ang2.rearrange("p a b -> p (a b)"), ACT.Sin
                          ).then_inc(S["rope_r"], 1)
            ac.wait_ge(S["pre_w"], 1)
            ac.activation(wo_g[:].rearrange("p a b -> p (a b)"), ps[:, 7, 0:KC * NE], ACT.Copy)
            ac.activation(w1_g[:].rearrange("p a b -> p (a b)"), ps[:, 7, 64:64 + KC * NE], ACT.Copy)
            ac.activation(b_g[:], ps[:, 7, 128:128 + NE], ACT.Copy).then_inc(S["pre_c"], 1)
            ac.wait_ge(S["eaw_in"], 1)
            ac.wait_ge(S["sparse_d"], 16 * 3)
            ac.activation(eaw[:], eaw[:], ACT.Exp, bias=eaw_s[:, 0:1], accum_out=eaw_s[:, 1:2])
            ac.activation(imp.rearrange("p a b -> p (a b)"), imp.rearrange("p a b -> p (a b)"), ACT.Sigmoid
                          ).then_inc(S["imp_s"], 1)
            ac.wait_ge(S["rope_ok"], 1)
            flat = "p a b -> p (a b)"
            with ac.Fori(0, NT // 4) as i:
                for pair in range(2):
                    for x in range(2):
                        s = 2 * pair + x
                        ac.wait_ge(S4["qkv"][s], i + 1)
                        ac.wait_ge(S2["ssd"][x], 2 * i + pair)
                        heads = ps[:, 2 * s:2 * s + 2, :].rearrange(flat)
                        for h in range(NQK):
                            ac.activation(sq[x][:, h * HD:(h + 1) * HD], heads[:, h * HD:(h + 1) * HD], ACT.Square,
                                          accum_out=ss[:, x, h:h + 1])
                        ac.wait_ge(S2["p1w"][x], 64 * i + 32 * pair)
                        ac.activation(qkv_out[x][:, QK:2 * D], ps[:, 2 * s + 1, QK - D:D], ACT.Copy).then_inc(S4["a1"][s], 1)
                    ac.wait_ge(S2["rec"][0], 2 * i + pair + 1)
                    ac.activation(root[:].rearrange(flat), rstd[:].rearrange(flat), ACT.Sqrt).then_inc(S2["root"][0], 1)
            ac.wait_ge(S["eaw_p"], 1)
            ac.activation(eaw_t[:], ps[0:64, 2, 0:NE], ACT.Copy).then_inc(S["eaw_c"], 1)

            bk, bc = S2["bk"], S2["bc"]

            def out_of(use, dst):
                b, n = use
                wait(ac, bk[b], n + 1)
                ac.activation(dst, ps[:, b, :] if len(dst.shape) == 2 else ps[:, b, :].rearrange("p (a b) -> p a b", b=P),
                              ACT.Copy).then_inc(bc[b], 1)

            def expo(B, u):
                wait(ac, S["s_mx"], 16 * B + u + 1)
                wait(ac, S["s_pt"], 16 * B + u - 3)
                ac.activation(prob[u % 4], msk_s[u % 2], ACT.Exp, bias=nmx[:, u:u + 1], scale=SCALE,
                              accum_out=sums[:, u:u + 1]).then_inc(S["s_exp"], 1)

            def evac(B, u):
                wait(ac, S["s_pt"], 16 * B + u + 1)
                wait(ac, S["s_pv"], 16 * B + u - 3)
                ac.activation(prob_t[u % 4], ps[:, 4 + u % 2, 0:KW], ACT.Copy).then_inc(S["s_pe"], 1)

            def period(B, kind, s, i):
                at = uses(B, kind)
                for u in range(2 * NH):
                    if u >= 2 or kind != "first":
                        evac(B if u >= 2 else B - 1, (u - 2) % 16)
                    expo(B, u)
                    if u == 5 and "o1" in at:
                        out_of(at["o1"], o_t.rearrange(flat))
                    if u == 8 and "q0" in at:
                        for qt in range(2):
                            out_of(at[f"q{qt}"], q_t[1 - s][:, :, qt * P:(qt + 1) * P])
                    if u == 11 and "k0" in at:
                        for p in range(2):
                            out_of(at[f"k{p}"], k_t[1 - s][:, p, :])
                    if u == 13:
                        out_of(at["o0"], o_t.rearrange(flat))

            for s in range(2):
                ac.wait_ge(S2["p1w"][s], 32 * (NT // 2))
            for qt in range(2):
                out_of((qt, 0), q_t[0][:, :, qt * P:(qt + 1) * P])
            for p in range(2):
                out_of((p, 1), k_t[0][:, p, :])
            periods(ac, period)
            evac(NB - 1, 14)
            evac(NB - 1, 15)
            out_of(uses(NB, "after")["o1"], o_t.rearrange(flat))
            ac.wait_ge(S["xs_sc"], 32 * NT)
            ac.wait_ge(S["m_done"], 2 * KC)
            ac.wait_ge(S["r_ok"], 1)
            fc1_v = d["fc1"].rearrange("e (k p) n -> p k e n", p=P)

            def load_fc(dst, src, m, signal):
                k, e = m // 2, slice(NE // 2 * (m % 2), NE // 2 * (m % 2 + 1))
                ac.dma_start(dst[:, k, e], src[:, k, e]).then_inc(signal, 16)

            def layer0(i, slots=BOTH):
                for s in slots:
                    ac.wait_ge(S2["l_tx"][s], i + 1)
                    wait(ac, S2["l_mm"][s], i)
                    ac.activation(xs_t[s].rearrange(flat), ps[:, s, :], ACT.Copy).then_inc(S2["l_xt"][s], 1)
                ac.wait_ge(S["l_mi"], 32 * i + 16 * len(slots))
                wait(ac, S["l_mt"], i)
                ac.activation(ew[:], meta_in[:, :, 1:3], ACT.Exp).then_inc(S["l_ex"], 1)
            for i in range(2 * KC):
                layer0(i)
                load_fc(fc1, fc1_v, i, S["fc1_d"])
                if i == 0:
                    ac.dma_start(w1_t, d["w1_t"].rearrange(chunked, p=P)).then_inc(S["w5"], 16)
                    ac.dma_start(lora_a, d["a_t"].rearrange(chunked, p=P)).then_inc(S["w5"], 16)
                    ac.dma_start(lora_b[:], d["b_t"]).then_inc(S["w5"], 16)
            with ac.Fori(2 * KC, PAIRS - 1) as i:
                layer0(i)
            layer0(PAIRS - 1, LAST)
            for s in range(2):
                ac.wait_ge(S2["l_st"][s], 16 * ((NTILE + 1 - s) // 2))
            fc2_v = d["fc2"].rearrange("e (k p) n -> p k e n", p=P)

            def turned(i, s):
                ac.wait_ge(S2["c_tx"][s], i + 1)
                wait(ac, S2["c_h"][s], i)
                ac.activation(x1_t[s].rearrange(flat), ps[:, s, :], ACT.Copy).then_inc(S2["c_xt"][s], 1)

            def x2_out(i, s):
                ac.wait_ge(S2["c_h"][s], i + 1)
                ac.activation(junk_a[:, s:s + 1], ident[:, 0:1], ACT.Copy)
                ac.activation(x2_rows[:, 2 * i + s, :], ps[:, 4 + s, :], ACT.Copy).then_inc(S2["c_x2"][s], 1)

            def soft(i):
                ac.wait_ge(S["r_l"], i + 1)
                ac.activation(lg[:].rearrange(flat), lg[:].rearrange(flat), ACT.Exp).then_inc(S["r_lexp"], 1)

            def outs(i, more=True):
                for s in range(2):
                    x2_out(i, s)
                    if more:
                        turned(i + 1, s)
                ac.drain()
            for s in range(2):
                turned(0, s)
            for i in range(KC):
                outs(i)
                load_fc(fc2, fc2_v, 2 * i, S["fc2_d"])
                soft(i)
                load_fc(fc2, fc2_v, 2 * i + 1, S["fc2_d"])
            with ac.Fori(KC, NT // 2 - 1) as i:
                outs(i)
                soft(i)
            outs(NT // 2 - 1, False)
            soft(NT // 2 - 1)
            for s in range(2):
                ac.wait_ge(S2["c_st"][s], 16 * (NT // 2))
            def gelu(i, slots):
                for s in slots:
                    ac.wait_ge(S2["k_hb"][s], i + 1)
                    ac.activation(h_sb[s], h_sb[s], ACT.Gelu).then_inc(S2["k_hg"][s], 1)
            with ac.Fori(0, PAIRS - 1) as i:
                gelu(i, BOTH)
            gelu(PAIRS - 1, LAST)

        @block.vector
        def _(ve):
            TT, TS, CP = ve.tensor_tensor, ve.tensor_scalar, ve.tensor_copy

            def red(out, in_, op=ALU.max):
                return ve.tensor_reduce(out, in_, AX, op)

            ve.wait_ge(S["rope_d"], 16 * 4)
            ve.wait_ge(S["consts"], 1)
            CP(iof[:, 0:33], iot[:, 0:33])
            CP(lens[:], lens_i[:])
            ve.drain()
            CP(part[:, 0:1], iof[:, 32:33])
            ve.drain()
            TS(gains[:], gains[:], 1.0, None, ALU.add)
            for h in range(2):
                TS(pos[:, h:NT:2], lens[:], part[:, 0:1], float(P * h), ALU.add, ALU.add)
            ve.drain()
            TT(ang, pos[:].unsqueeze(2).broadcast_to([P, NT, HD // 2]), inv_f[:].unsqueeze(1).broadcast_to([P, NT, HD // 2]), ALU.mult)
            ve.drain()
            TS(ang2, ang, float(np.float32(1 / (2 * np.pi))), 12582912.0, ALU.mult, ALU.add)
            ve.drain()
            TS(ang2, ang2, 12582912.0, None, ALU.subtract)
            ve.drain()
            c1 = 6.28125
            c2 = float(np.float32(int((2 * np.pi - c1) * 2 ** 20) / 2 ** 20))
            c3 = float(np.float32(2 * np.pi - c1 - c2))
            for c in (c1, c2, c3):
                ve.scalar_tensor_tensor(ang, ang2, -c, ang, ALU.mult, ALU.add)
                ve.drain()
            TS(ang, ang, 3.1415925, -3.1415925, ALU.min, ALU.max)
            ve.drain()
            TS(ang2, ang, -1.0, None, ALU.mult)
            ve.drain()
            TT(ang2, ang2, ang, ALU.min)
            ve.drain()
            TS(ang2, ang2, float(np.float32(np.pi / 2)), None, ALU.add).then_inc(S["rope_in"], 1)
            ve.wait_ge(S["p0_dma"], 16 * 6)
            CP(tile_io[:], tile_ii)
            CP(jrow[:], jrow_i)
            TS(ints[:, 0:8], lens_i[:], 4, None, ALU.arith_shift_right)
            TS(ints[:, 8:16], lens_i[:], BLK - 1, None, ALU.bitwise_and)
            TS(ints[:, 16:17], iot[:, 32:33], 4, None, ALU.arith_shift_right)
            TS(ints[:, 17:18], iot[:, 32:33], BLK - 1, None, ALU.bitwise_and)
            CP(ms_f[:], ms_i[:])
            TS(cell_i[:], ms_i[:], D - 1, 9, ALU.bitwise_and, ALU.logical_shift_left)
            TS(cell_j[:], ms_i[:], 9, None, ALU.arith_shift_right)
            ve.drain()
            CP(first[:], ints[:, 0:8])
            TS(neg_len[:], lens[:], -1.0, None, ALU.mult)
            TS(room[:], lens[:], -1.0, float(SEQ), ALU.mult, ALU.add)
            CP(lo[:], ints[:, 8:16])
            CP(part[:, 1:3], ints[:, 16:18])
            TS(rev[:], iof[:, 0:NE], -1.0, float(NE), ALU.mult, ALU.add)
            TT(cell_i[:], cell_i[:], cell_j[:], ALU.bitwise_or)
            red(eaw_s[:, 2:3], eaw[:])
            ve.drain()
            TS(eaw_s[:, 0:1], eaw_s[:, 2:3], -1.0, None, ALU.mult).then_inc(S["eaw_in"], 1)
            for b in range(NB):
                s0 = ve.value_load(ints[0:1, b:b + 1], min_val=0, max_val=(SEQ - WIN + P) // BLK + 8)
                CP(win[:, b, :], table_bc[:, bass.ds(s0 + b * NBLK, SB)])
            TS(eqk[:, 0, 0:NE], iof[:, 0:NE], part[:, 1:2], None, ALU.is_equal)
            ve.drain()
            TT(eqk[:, 1, 0:NE], eqk[:, 0, 0:NE], scal_bc[:], ALU.mult)
            CP(sel_b[:], adapt_i[:])
            ve.drain()
            red(part[:, 3:4], eqk[:, 1, 0:NE], ALU.add)
            ve.drain()
            TS(sel_b[:], sel_b[:], part[:, 1:2], part[:, 3:4], ALU.is_equal, ALU.mult)
            TS(carry[:], lo[:], part[:, 2:3], float(BLK), ALU.add, ALU.is_ge)
            TS(off[:], lo[:], part[:, 2:3], None, ALU.add)
            ve.drain()
            ve.scalar_tensor_tensor(off[:], carry[:], -float(BLK), off[:], ALU.mult, ALU.add)
            TS(carry[:], carry[:], part[:, 1:2], None, ALU.add)
            ve.drain()
            TT(eqk, iof[:, 0:9].unsqueeze(1).broadcast_to([P, NB, 9]), carry[:].unsqueeze(2).broadcast_to([P, NB, 9]), ALU.is_equal)
            ve.drain()
            for c in range(NC):
                TT(tmp9, eqk, win[:, :, 8 * c:8 * c + 9], ALU.mult)
                ve.drain()
                red(blk[:, c, :], tmp9, ALU.add)
                ve.drain()
            TT(wr_tok, iof[:, 0:SW].unsqueeze(1).broadcast_to([P, NB, SW]), first[:].unsqueeze(2).broadcast_to([P, NB, SW]), ALU.add)
            ve.drain()
            TS(wr_tok, wr_tok, float(NBLK), None, ALU.is_lt)
            TS(wr_blk, win[:, :, SB - SW:SB], 1.0, None, ALU.add)
            ve.drain()
            TT(wr_blk, wr_blk, wr_tok, ALU.mult)
            ve.drain()
            TS(wr_blk, wr_blk, -1.0, None, ALU.add)
            TS(junk[:, 0:1], part[:, 0:1], 1.0, None, ALU.mult)
            TS(wr_tok, iof[:, 0:SW].unsqueeze(1).broadcast_to([P, NB, SW]), float(BLK), float(BLK), ALU.mult, ALU.add)
            ve.drain()
            TT(wr_tok, wr_tok, lo[:].unsqueeze(2).broadcast_to([P, NB, SW]), ALU.subtract)
            TS(ntf[0][:], iof[:, 0:NB], float(T), None, ALU.mult)
            ve.drain()
            TT(wr_tok, wr_tok, ntf[0][:].unsqueeze(2).broadcast_to([P, NB, SW]), ALU.add)
            TT(edge[:, 0], off[:].unsqueeze(2).broadcast_to([P, NB, NB]), lo[:].unsqueeze(1).broadcast_to([P, NB, NB]), ALU.is_ge)
            ve.drain()
            TS(edge[:, 1], edge[:, 0], -1.0, 1.0, ALU.mult, ALU.add)
            TT(hits, blk[:].rearrange("p c b -> p (c b)").unsqueeze(2).broadcast_to([P, NC * NB, NB * SW]),
               wr_blk.rearrange("p b s -> p (b s)").unsqueeze(1).broadcast_to([P, NC * NB, NB * SW]), ALU.is_equal)
            ve.drain()
            TT(hits, hits, wr_tok.rearrange("p b s -> p (b s)").unsqueeze(1).broadcast_to([P, NC * NB, NB * SW]), ALU.mult)
            ve.drain()
            hv = hits.rearrange("p (c b) (w s) -> p c b w s", c=NC, w=NB)
            for c in range(NC):
                for x, sl in ((0, 0), (1, SW - 1)):
                    TT(hv[:, c, :, :, sl], hv[:, c, :, :, sl], edge[:, x], ALU.mult)
            ve.drain()
            red(best[:].rearrange("p c b -> p (c b)"), hits)
            ve.drain()
            TS(found[:], best[:], 0.0, None, ALU.is_gt)
            ve.drain()
            TS(best[:], best[:], -float(BLK), None, ALU.add)
            ve.drain()
            TT(best[:], best[:], off[:].unsqueeze(1).broadcast_to([P, NC, NB]), ALU.add)
            ve.drain()
            TT(best[:], best[:], found[:], ALU.mult)
            ve.drain()
            TS(found[:, 0:2, :], found[:, 0:2, :], -float(4 * N), float(4 * N), ALU.mult, ALU.add)
            TS(fidx[:, 0:2], blk[:, 0:2], float(BLK), None, ALU.mult)
            ve.drain()
            TT(best[:, 0:2, :], best[:, 0:2, :], found[:, 0:2, :], ALU.add)
            TT(fidx[:, 0:2], fidx[:, 0:2], off[:].unsqueeze(1).broadcast_to([P, 2, NB]), ALU.add)
            ve.drain()
            CP(new_idx[:], best[:].rearrange("p c b -> p (c b)"))
            CP(old_idx[:], fidx[:, 0:2].rearrange("p c b -> p (c b)"))
            ve.drain().then_inc(S["idx_ok"], 1)

            ve.wait_ge(S["rope_r"], 1)
            hh = HD // 2
            for w in range(2):
                for h in range(2):
                    TT(tab_a[:, :, w, h * hh:(h + 1) * hh], cos_t, gains[:, w, h * hh:(h + 1) * hh].unsqueeze(1).broadcast_to([P, NT, hh]), ALU.mult)
                TT(tab_b[:, :, w, 0:hh], sin_t, gains[:, w, hh:HD].unsqueeze(1).broadcast_to([P, NT, hh]), ALU.mult)
                TT(tab_b[:, :, w, hh:HD], sin_t, gains[:, w, 0:hh].unsqueeze(1).broadcast_to([P, NT, hh]), ALU.mult)
            ve.drain()
            TS(tab_b[:, :, :, 0:hh], tab_b[:, :, :, 0:hh], -1.0, None, ALU.mult)
            ve.drain().then_inc(S["rope_ok"], 1)
            ve.wait_ge(S["imp_s"], 1)
            ve.reciprocal(eaw_s[:, 3:4], eaw_s[:, 1:2])
            ve.drain()
            TS(eaw[:], eaw[:], eaw_s[:, 3:4], None, ALU.mult).then_inc(S["eaw_ok"], 1)

            flat = "p a b -> p (a b)"
            def four_tiles(i):
                for pair in range(2):
                    for x in range(2):
                        ve.wait_ge(S4["a1"][2 * pair + x], i + 1)
                        ve.memset(junk[:, x:x + 1], 0.0)
                    TS(ss[:], ss[:], 1.0 / HD, RMS_EPS, ALU.mult, ALU.add)
                    ve.drain()
                    ve.reciprocal(rstd[:], ss[:]).then_inc(S2["rec"][0], 1)
                    ve.wait_ge(S2["root"][0], 2 * i + pair + 1)
                    TT(rstd[:], root[:], root[:], ALU.mult)
                    ve.drain()
                    TT(rstd[:], rstd[:], ss[:], ALU.mult)
                    ve.drain()
                    for x in range(2):
                        ve.memset(junk[:, 2 + x:3 + x], 0.0).then_inc(S2["ssd"][x], 1)
                    TS(rstd[:], rstd[:], -0.5, 1.5, ALU.mult, ALU.add)
                    ve.drain()
                    TT(rstd[:], rstd[:], root[:], ALU.mult)
                    ve.drain()
                    for x in range(2):
                        s = 2 * pair + x
                        t = 4 * i + s
                        TT(nrm.rearrange("p (h d) -> p h d", d=HD),
                           ps[:, 2 * s:2 * s + 2, :].rearrange(flat)[:, 0:QK].rearrange("p (h d) -> p h d", d=HD),
                           rstd[:, x, :].unsqueeze(2).broadcast_to([P, NQK, HD]), ALU.mult).then_inc(S4["p1p"][s], 1)
                        ve.drain()
                        nv = nrm.rearrange("p (h x d) -> p h x d", x=2, d=hh)
                        bv = rot_b.rearrange("p (h x d) -> p h x d", x=2, d=hh)
                        av = rot_a.rearrange("p (h d) -> p h d", d=HD)
                        for w, h0, h1 in ((0, 0, NH), (1, NH, NQK)):
                            TT(av[:, h0:h1], nrm.rearrange("p (h d) -> p h d", d=HD)[:, h0:h1],
                               tab_a[:, t, w, :].unsqueeze(1).broadcast_to([P, h1 - h0, HD]), ALU.mult)
                            for y in range(2):
                                TT(bv[:, h0:h1, y], nv[:, h0:h1, 1 - y],
                                   tab_b[:, t, w, y * hh:(y + 1) * hh].unsqueeze(1).broadcast_to([P, h1 - h0, hh]), ALU.mult)
                        ve.drain()
                        TT(qkv_out[x][:, 0:QK], rot_a, rot_b, ALU.add).then_inc(S2["p1o"][x], 1)
                        ve.drain()

            four_tiles(0)
            ve.wait_ge(S["sparse_d"], 16 * 3)
            TT(eq_all, mask_bc.rearrange("p (s t) -> p t s", t=ST), ms_f[:].unsqueeze(2).broadcast_to([P, ST, P]),
               ALU.is_equal).then_inc(S["eqa"], 1)
            with ve.Fori(1, NT // 4) as i:
                four_tiles(i)

            ve.wait_ge(S["delta"], 1)
            TT(wgt.rearrange(flat), ps[:, 2, 0:ST * NE], imp.rearrange(flat), ALU.mult).then_inc(S["wgt_ok"], 1)
            ve.wait_ge(S["eql"], 1)
            red(dup[:], eq_low)
            CP(cell_f[:], cell_i[:])
            ve.drain()
            TS(ms_f[:], cell_f[:], -1.0, float(CELLS), ALU.mult, ALU.add)
            ve.drain()
            TS(ms_f[:], ms_f[:], part[:, 0:1], None, ALU.add)
            ve.drain()
            TT(ms_f[:], ms_f[:], dup[:], ALU.mult)
            ve.drain()
            TT(cell_f[:], cell_f[:], ms_f[:], ALU.add)
            ve.drain()
            CP(cell_i[:], cell_f[:])
            ve.wait_ge(S["tot_p"], 1)
            CP(tot[:].rearrange(flat), ps[:, 3, 0:ST * NE])
            ve.drain().then_inc(S["cell_ok"], 1)
            bk, bc = S2["bk"], S2["bc"]

            def build_mask(B, qt):
                out1, out2 = key_bias[:, 0, :], key_bias[:, 1, :]
                jr = jrow[:, qt * P:qt * P + KW]
                ve.scalar_tensor_tensor(out1, jr, neg_len[:, bass.ds(B, 1)], band[:], ALU.is_lt, ALU.max)
                ve.drain()
                ve.scalar_tensor_tensor(out2, jr, room[:, bass.ds(B, 1)], out1, ALU.is_ge, ALU.max)
                ve.drain()
                TS(mask[:, qt, :], out2, -BIG, None, ALU.mult)
                ve.drain()

            def top(B, u):
                wait(ve, S["s_dot"], 16 * B + u + 1)
                ve.memset(junk[:, 0:1], 0.0)
                if not isinstance(B, int) or 16 * B + u - 1 > 0:
                    wait(ve, S["s_exp"], 16 * B + u - 1)
                    ve.memset(junk[:, 1:2], 0.0)
                ve.tensor_tensor_reduce(out=msk_s[u % 2], in0=ps[:, 2 + u % 2, 0:KW], in1=mask[:, u // NH, :], scale=1.0,
                                        scalar=-3e38, op0=ALU.add, op1=ALU.max, accum_out=mx[:, u:u + 1])
                ve.drain()
                TS(nmx[:, u:u + 1], mx[:, u:u + 1], -SCALE, None, ALU.mult).then_inc(S["s_mx"], 1)

            def norm(B, qt):
                wait(ve, S["s_pv"], 16 * B + 8 * qt + 8)
                ve.reciprocal(rsum[:], sums[:, 8 * qt:8 * qt + 8])
                ve.drain()
                for y in range(2):
                    TT(o_sb.rearrange("p (g y x d) -> p g y x d", g=2, y=2, x=2)[:, :, y],
                       ps[:, 6 + qt, :].rearrange("p (g y x d) -> p g y x d", g=2, y=2, x=2)[:, :, y],
                       rsum[:].rearrange("p (g x y) -> p g x y", g=2, x=2)[:, :, :, y].unsqueeze(3).broadcast_to([P, 2, 2, HD]),
                       ALU.mult)
                ve.drain().then_inc(S["s_norm"], 1)

            def row(at, x, t):
                b, n = at["a" + x]
                wait(ve, bk[b], n + 1)
                ve.memset(junk[:, 2:3], 0.0)
                CP(a_rows[:, t, :], ps[:, b, :]).then_inc(bc[b], 1)
                b, n = at["g" + x]
                wait(ve, bk[b], n + 1)
                TS(lg[:, int(x), :], ps[:, b, 0:NE], 50.0, -50.0, ALU.min, ALU.max).then_inc(bc[b], 1)

            def b3(a):
                return a.unsqueeze(2).broadcast_to([P, 2, NE])

            def rb(a):
                return a.unsqueeze(1).broadcast_to([P, 2, NE])

            def choose(layer):
                ve.drain()
                src = lg
                for c in range(2):
                    oh = chosen_e[:, c]
                    red(best2[:, c, :], src[:])
                    ve.drain()
                    TT(t1[:], src[:], b3(best2[:, c, :]), ALU.is_equal)
                    ve.drain()
                    TT(t1[:], t1[:], rb(rev[:]), ALU.mult)
                    ve.drain()
                    red(rr[:], t1[:])
                    ve.drain()
                    TT(oh, rb(rev[:]), b3(rr[:]), ALU.is_equal)
                    ve.drain()
                    if c == 0:
                        yield
                        ve.scalar_tensor_tensor(t2[:].rearrange(flat), oh.rearrange(flat), -BIG, lg[:].rearrange(flat),
                                                ALU.mult, ALU.add)
                        ve.drain()
                        src = t2
                TT(selb16[:], chosen_e[:, 0], chosen_e[:, 1], ALU.add).then_inc(S["r_sel"], 1)
                yield
                if layer == 1:
                    TT(t3.rearrange("p c t e -> p (c t) e"), chosen_e[:].rearrange("p c t e -> p (c t) e"),
                       alpha_bc[:].unsqueeze(1).broadcast_to([P, 4, NE]), ALU.mult)
                    ve.drain()
                    red(al[:].rearrange("p c t -> p (c t)"), t3.rearrange("p c t e -> p (c t) e"), ALU.add)
                    ve.drain()

            def place(t, layer, pre, tot_b, done):
                ve.drain()
                if layer == 0:
                    TT(diff[:], best2[:, 1, :], best2[:, 0, :], ALU.subtract)
                else:
                    TT(diff[:], best2[:, 0, :], best2[:, 1, :], ALU.add)
                    ve.drain()
                    ve.reciprocal(rs2[:], diff[:])
                    ve.drain()
                    TT(best2[:], best2[:], rs2[:].unsqueeze(1).broadcast_to([P, 2, 2]), ALU.mult)
                TT(t1[:], pre.rearrange("p (t e) -> p t e", e=NE), rb(run[:]), ALU.add)
                CP(t2[:], tot_b.rearrange("p (t e) -> p t e", e=NE)).then_inc(*done)
                ve.drain()
                TT(t1[:, 1, :], t1[:, 1, :], t2[:, 0, :], ALU.add)
                TT(run[:], run[:], t2[:, 0, :], ALU.add)
                ve.drain()
                TT(run[:], run[:], t2[:, 1, :], ALU.add)
                yield
                TT(t3, chosen_e[:], t1[:].unsqueeze(1).broadcast_to([P, 2, 2, NE]), ALU.mult)
                ve.drain()
                red(slot_f[:].rearrange("p c t -> p (c t)"), t3.rearrange("p c t e -> p (c t) e"), ALU.add)
                ve.drain()
                CP(slot_i[:, :, bass.ds(t, 2)], slot_f[:])
                if layer == 0:
                    CP(meta[:, :, bass.ds(t, 2), 1], diff[:].unsqueeze(1).broadcast_to([P, 2, 2]))
                    CP(meta[:, 1, bass.ds(t, 2), 2], diff[:])
                else:
                    TT(meta[:, :, bass.ds(t, 2), 1], best2[:], al[:], ALU.mult)
                ve.drain().then_inc(S["r_slot"], 1)
                yield

            def place0(at, t):
                b, n = at["rt"]
                wait(ve, bk[b], n + 1)
                ve.memset(junk[:, 3:4], 0.0)
                return place(t, 0, ps[:, b, 0:2 * NE], ps[:, b, 2 * NE:4 * NE], (bc[b], 1))

            def tiles():
                def step(ins):
                    ve.drain()
                    return ins
                ve.drain()
                CP(end_i[:], run[:])
                ve.drain().then_inc(S["r_end"], 1)
                step(TT(ntf[0][:], run[:], region0[:], ALU.subtract))
                step(TS(ntf[0][:], ntf[0][:], float(P - 1), None, ALU.add))
                step(CP(nti[:], ntf[0][:]))
                step(TS(nti[:], nti[:], 7, None, ALU.arith_shift_right))
                CP(ntf[2][:], nti[:])
                step(CP(ntf[0][:], nti[:]))
                u, v = ntf[0], ntf[1]
                for sh in (1, 2, 4):
                    TT(v[:, sh:], u[:, sh:], u[:, :NE - sh], ALU.add)
                    step(CP(v[:, :sh], u[:, :sh]))
                    u, v = v, u
                TS(ntf[3][:], ntf[2][:], -float(P), float(REGION), ALU.mult, ALU.add)
                ve.drain()
                step(TT(ex_c[:], u[:].unsqueeze(1).broadcast_to([P, NTILE, NE]),
                        tile_io[:].unsqueeze(2).broadcast_to([P, NTILE, NE]), ALU.is_le))
                step(red(ex_f[:], ex_c[:, :, 0:NE - 1], ALU.add))
                CP(ex_i[:], ex_f[:])
                step(TT(ex_c[:], ex_c[:], ntf[3][:].unsqueeze(1).broadcast_to([P, NTILE, NE]), ALU.mult))
                step(red(ex_f[:], ex_c[:], ALU.add))
                step(ve.scalar_tensor_tensor(ex_f[:], tile_io[:], float(P), ex_f[:], ALU.mult, ALU.add))
                CP(row_i[:], ex_f[:])
                ve.drain().then_inc(S["r_ok"], 1)
                CP(run[:], region0[:])

            def period(B, kind, s, i):
                at = uses(B, kind)
                for u in range(2 * NH):
                    top(B, u)
                    if u == 0:
                        build_mask(B, 1)
                    if u == 3 and "o1" in at:
                        norm(B - 1, 1)
                    if u == 7 and "a1" in at:
                        row(at, "1", 2 * B - 1)
                    if u == 8 and "rt" in at:
                        chosen = choose(0)
                        next(chosen)
                    if u == 9 and "rt" in at:
                        next(chosen)
                    if u == 10 and kind != "last":
                        build_mask(B + 1, 0)
                    if u == 13 and "rt" in at:
                        placed = place0(at, 2 * B - 2)
                        next(placed)
                    if u == 14 and "rt" in at:
                        next(placed)
                    if u == 11:
                        norm(B, 0)
                    if u == 15:
                        row(at, "0", 2 * B)

            ve.memset(meta[:], 0.0)
            ve.drain()
            TS(meta[:, :, :, 0], iof[:, 0:NT].unsqueeze(1).broadcast_to([P, 2, NT]), float(P), 1.0, ALU.mult, ALU.add)
            ve.drain()
            TS(meta[:, :, :, 0], meta[:, :, :, 0], part[:, 0:1], None, ALU.add)
            TS(region0[:], iof[:, 0:NE], float(REGION), None, ALU.mult)
            ve.drain()
            CP(run[:], region0[:])
            for s in range(2):
                ve.wait_ge(S2["p1w"][s], 32 * (NT // 2))
            build_mask(0, 0)
            periods(ve, period)
            norm(NB - 1, 1)
            at = uses(NB, "after")
            row(at, "1", NT - 1)
            for _ in choose(0):
                pass
            for _ in place0(at, NT - 2):
                pass
            tiles()
            ve.wait_ge(S["xs_sc"], 32 * NT)

            def tokens(i, load, slots):
                ve.wait_ge(load, 32 * i + 16 * len(slots))
                TS(tok_f[:], meta_in[:, :, 0], 0.0, float(4 * N), ALU.is_equal, ALU.mult)
                ve.drain()
                ve.scalar_tensor_tensor(tok_f[:], tok_f[:], -1.0, meta_in[:, :, 0], ALU.add, ALU.add)
                ve.drain()

            def layer0(i, slots):
                tokens(i, S["l_mi"], slots)
                ve.wait_ge(S["l_ex"], i + 1)
                TS(w_row[:], ew[:, :, 0], 1.0, None, ALU.add)
                ve.drain()
                ve.reciprocal(w_row[:], w_row[:])
                ve.drain()
                TT(w_row[:], w_row[:], ew[:, :, 1], ALU.mult).then_inc(S["l_mt"], 1)
                ve.drain()
                for s in slots:
                    wait(ve, S2["l_st"][s], 16 * i)
                    CP(tok_i[:, s:s + 1], tok_f[:, s:s + 1])
                    ve.wait_ge(S2["l_mm"][s], i + 1)
                    TS(y_sb[s], ps[:, 2 + s, :], w_row[:, s:s + 1], None, ALU.mult).then_inc(S2["l_ye"][s], 1)
                ve.drain()
            with ve.Fori(0, PAIRS - 1) as i:
                layer0(i, BOTH)
            layer0(PAIRS - 1, LAST)
            for s in range(2):
                ve.wait_ge(S2["l_st"][s], 16 * ((NTILE + 1 - s) // 2))

            def make_x1(i, s):
                ve.wait_ge(S2["c_in"][s], 32 * i + 32)
                ve.memset(junk[:, 8 + s:9 + s], 0.0)
                if not isinstance(i, int) or i > 0:
                    ve.wait_ge(S2["c_st"][s], 16 * i)
                    ve.memset(junk[:, 10 + s:11 + s], 0.0)
                    ve.wait_ge(S2["c_tx"][s], i)
                    ve.memset(junk[:, 12 + s:13 + s], 0.0)
                TT(x1[s], x_row[s], y1[s], ALU.add).then_inc(S2["c_x1"][s], 1)

            def place1(i):
                ve.wait_ge(S["c_rt"], i + 1)
                ve.memset(junk[:, 3:4], 0.0)
                return place(2 * i, 1, ps[:, 3, P:P + 2 * NE], ps[:, 3, P + 2 * NE:P + 4 * NE], (S["c_rtc"], 1))

            def linear(i, first, more):
                for s in range(2):
                    ve.wait_ge(S2["c_xa"][s], i + 1)
                    TS(xa_t[s], ps[:, 2 + s, 0:P], sel_b[:, bass.ds(i, 1)], None, ALU.mult).then_inc(S2["c_xe"][s], 1)
                if more:
                    make_x1(i + 1, 0)
                    make_x1(i + 1, 1)
                if not first:
                    for _ in choose(1):
                        pass
                for s in range(2):
                    if s == 1 and not first:
                        for _ in place1(i - 1):
                            pass
                    ve.wait_ge(S2["c_g"][s], i + 1)
                    CP(lg[:, s, :], ps[:, 6 + s, 0:NE]).then_inc(S2["c_lg"][s], 1)
                ve.drain()
                red(rr[:], lg[:])
                ve.drain()
                TT(lg[:], lg[:], b3(rr[:]), ALU.subtract).then_inc(S["r_l"], 1)
                ve.wait_ge(S["r_lexp"], i + 1)
                red(rr[:], lg[:], ALU.add)
                ve.drain()
                ve.reciprocal(rs2[:], rr[:])
                ve.drain()
                TT(lg[:], lg[:], b3(rs2[:]), ALU.mult)

            make_x1(0, 0)
            make_x1(0, 1)
            linear(0, True, True)
            with ve.Fori(1, NT // 2 - 1) as i:
                linear(i, False, True)
            linear(NT // 2 - 1, False, False)
            for _ in choose(1):
                pass
            for _ in place1(NT // 2 - 1):
                pass
            tiles()
            ve.wait_ge(S["b1_d"], 16)
            for s in range(2):
                ve.wait_ge(S2["c_st"][s], 16 * (NT // 2))

            def turned1(i, slots):
                for s in slots:
                    ve.wait_ge(S2["k_tx"][s], i + 1)
                    wait(ve, S2["k_m1"][s], i)
                    CP(xs_t[s].rearrange(flat), ps[:, s, :]).then_inc(S2["k_xt"][s], 1)

            def layer1(i, now, after):
                es = [ve.value_load(ex_i[0:1, bass.ds(2 * i + s, 1)], min_val=0, max_val=NE - 1) for s in now]
                tokens(i, S["k_mi"], now)
                CP(w_row[:], meta_in[:, :, 1]).then_inc(S["k_mt"], 1)
                ve.drain()
                for s in now:
                    ve.wait_ge(S2["k_m1"][s], i + 1)
                    TT(h_sb[s], ps[:, 2 + s, :], b1_bc[:, es[s], :], ALU.add).then_inc(S2["k_hb"][s], 1)
                if isinstance(i, int):
                    ve.wait_ge(S["b2_d"], 16)
                for s in now:
                    ve.wait_ge(S2["k_th"][s], i + 1)
                    wait(ve, S2["k_m2"][s], i)
                    CP(h_t[s].rearrange(flat), ps[:, 4 + s, :]).then_inc(S2["k_ht"][s], 1)
                if after:
                    turned1(i + 1, after)
                for s in now:
                    ve.wait_ge(S2["k_m2"][s], i + 1)
                    TT(yb[s], ps[:, 6 + s, :], b2_bc[:, es[s], :], ALU.add).then_inc(S2["k_yb"][s], 1)
                    ve.drain()
                    wait(ve, S2["k_st"][s], 16 * i)
                    CP(tok_i[:, s:s + 1], tok_f[:, s:s + 1])
                    TS(y_sb[s], yb[s], w_row[:, s:s + 1], None, ALU.mult)
                    ve.drain().then_inc(S2["k_ye"][s], 1)
            turned1(0, BOTH)
            layer1(0, BOTH, BOTH)
            with ve.Fori(1, PAIRS - 2) as i:
                layer1(i, BOTH, BOTH)
            layer1(PAIRS - 2, BOTH, LAST)
            layer1(PAIRS - 1, LAST, ())


def kernel(**inputs):
    import concourse.bacc as bacc
    from concourse.bass_utils import run_bass_kernel_spmd

    a = {k: np.asarray(v) for k, v in inputs.items()}
    t = np.ascontiguousarray
    x = a["x"].reshape(N, D)
    half = HD // 2
    wq = a["L0_cond_Wq"].reshape(2, 2, 2, HD, D).transpose(0, 2, 1, 3, 4).reshape(NH * HD, D)
    ins = {
        "x": x,
        "x_t": x.T,
        "wqkv_t": np.concatenate([wq, a["L0_cond_Wk"], a["L0_cond_Wv"]], 0).T,
        "wo_t": a["L0_cond_Wo"].T,
        "wo": a["L0_cond_Wo"],
        "w1": a["L1_cond_W"],
        "b_o": a["L1_cond_Bm"].transpose(1, 0, 2).reshape(D, NE * RANK),
        "w0_t": a["L0_ffn_W"].T,
        "kv_pool": np.stack([a["L0_cond_k_blocks"].transpose(0, 2, 1, 3), a["L0_cond_v_blocks"].transpose(0, 2, 1, 3)],
                            2).reshape(NPHYS * BLK, 2 * NG * HD),
        "table": a["itok_Bx257_0_4111"].reshape(-1),
        "lens": a["itok_B_37_3939"],
        "adapter": a["itok_B_0_6"],
        "q_gain": a["L0_cond_q_norm_scale"],
        "k_gain": a["L0_cond_k_norm_scale"],
        "inv_freq": (1.0 / THETA ** (np.arange(half) / half)).astype(np.float32),
        "gate0_t": a["L0_ffn_gate_w"].T,
        "atoms": a["L0_ffn_atoms"],
        "eaw": a["L0_ffn_expert_atom_weights"],
        "imp_t": a["L0_ffn_importance"].T,
        "mask_idx": a["L0_ffn_mask_idx"],
        "w1_t": a["L1_cond_W"].T,
        "a_t": a["L1_cond_A"].reshape(NE * RANK, D).T,
        "b_t": a["L1_cond_Bm"].transpose(0, 2, 1).reshape(NE * RANK, D),
        "scal": a["L1_cond_scalings"],
        "gate1": a["L1_ffn_gate_w"],
        "fc1": a["L1_ffn_fc1_w"],
        "b1": a["L1_ffn_fc1_b"].reshape(-1),
        "fc2": a["L1_ffn_fc2_w"],
        "b2": a["L1_ffn_fc2_b"].reshape(-1),
        "alpha": a["L1_ffn_alpha"],
    }
    nc = bacc.Bacc("TRN2", target_bir_lowering=False, num_devices=1)
    arrays, d = {}, {}
    for name, v in ins.items():
        v = t(v)
        arrays["in_" + name] = v
        d[name] = nc.dram_tensor("in_" + name, v.shape, mybir.dt.from_np(v.dtype), kind="ExternalInput").ap()
    for name, shape in (("new_kv", [N, D]), ("qn", [N, D]), ("m_buf", [CELLS + P, NE]), ("xs", [ROWS, D]),
                        ("meta0", [ROWS, MW]), ("meta1", [ROWS, MW]),
                        ("acc0", [N, D]), ("acc1", [N, D])):
        d[name] = nc.dram_tensor(name, shape, F32, kind="Internal").ap()
    d["out"] = nc.dram_tensor("out_x", [N, D], F32, kind="ExternalOutput").ap()
    program(nc, d)
    r = run_bass_kernel_spmd(nc, [arrays], core_ids=[0])
    return r.results[0]["out_x"].reshape(NB, T, D)
```
